# Optimizing a Trainium2 kernel written in Bass

```python
import numpy as np
import jax
import jax.numpy as jnp

def _softmax(x, axis=-1):
    return jax.nn.softmax(x, axis=axis)

def _gelu(x):
    return jax.nn.gelu(x, approximate=True)

def _silu(x):
    return jax.nn.silu(x)

def _sigmoid(x):
    return jax.nn.sigmoid(x)

def _layernorm(x, axis=-1, eps=1e-05):
    m = jnp.mean(x, axis=axis, keepdims=True)
    v = jnp.var(x, axis=axis, keepdims=True)
    return (x - m) / jnp.sqrt(v + eps)

def _scatter_add(tgt, idx, src, axis=0):
    return tgt.at[idx].add(src)

def _segment_sum(src, seg, n):
    return jax.ops.segment_sum(src, seg, n)
kernel_name = 'mk_flamingo_gated_d1_seqx_r4_e60751'

def setup_inputs(seed: int=0):
    np.random.seed(seed)
    _w = jnp.asarray

    def _rec_inputs():
        import jax
        import jax.numpy as jnp
        _rk = jax.random.key(seed)
        x = 7.22e-05 + 1 * jax.random.normal(jax.random.fold_in(_rk, 1), (8, 256, 512), jnp.float32)
        _lenS = 256 - jax.random.randint(jax.random.fold_in(_rk, 7), (8,), 0, max(1, 256 // 4) + 1, jnp.int32)
        _lenS2 = 256 - jax.random.randint(jax.random.fold_in(_rk, 8), (8,), 0, max(1, 256 // 4) + 1, jnp.int32)
        _ctx_2048P = jax.random.normal(jax.random.fold_in(_rk, 11), (8, 16, 512), jnp.float32)
        _ctx_2048c = jax.random.dirichlet(jax.random.fold_in(_rk, 511), 0.3 * jnp.ones((16,), jnp.float32), (8, 256))
        _ctx_2048t = jnp.einsum('bsk,bkd->bsd', _ctx_2048c, _ctx_2048P)
        _ctx_2048t = _ctx_2048t * jax.lax.rsqrt(jnp.mean(jnp.square(_ctx_2048t)) + 1e-12) * 0.953939
        ctx_2048 = 4.13588e-05 + 0.999923 * (_ctx_2048t + 0.3 * jax.random.normal(jax.random.fold_in(_rk, 611), (8, 256, 512), jnp.float32))
        _validS = jnp.arange(256)[None, :] < _lenS[:, None]
        _validS2 = jnp.arange(256)[None, :] < _lenS2[:, None]
        _causal = jnp.tril(jnp.ones((256, 256), dtype=bool))
        mask_SxS2_bc0 = jnp.logical_not(jnp.broadcast_to(_validS2[0:1, :], (256, 256)))
        mask_BxS2_bk0 = jnp.logical_not(jnp.broadcast_to(_validS2[:, :], (8, 256)))
        _g = jax.random.normal(jax.random.fold_in(_rk, 9001), (2, 1), jnp.float32)
        _g = jnp.sign(_g) * jnp.maximum(jnp.abs(_g), 1.0) + (_g == 0) * 1.0
        g_xattn = _g[0]
        g_ffn = _g[1]
        return (x, ctx_2048, mask_SxS2_bc0, mask_BxS2_bk0, g_xattn, g_ffn)
    x, ctx_2048, mask_SxS2_bc0, mask_BxS2_bk0, g_xattn, g_ffn = _rec_inputs()

    def _L0_xattn_setup():
        import jax, jax.numpy as jnp
        import numpy as np
        B, LQ, LKV = (4, 256, 256)
        HID, H, G = (512, 32, 8)
        HD = HID // H
        HPG = H // G
        key = jax.random.key(seed)
        ks = jax.random.split(key, 10)
        s = 0.02
        inp = {'X': jax.random.normal(ks[0], (B, LQ, HID), jnp.float32), 'encoder_output': jax.random.normal(ks[1], (B, LKV, HID), jnp.float32), 'causal_mask': jnp.triu(jnp.ones((LQ, LKV), bool), 1), 'padding_mask': jnp.zeros((B, LKV), bool).at[B // 2:, LKV - LKV // 4:].set(True), 'Wq': jax.random.normal(ks[2], (HID, HID), jnp.float32) * s, 'bq': jnp.zeros((HID,), jnp.float32), 'Wk': jax.random.normal(ks[3], (G * HD, HID), jnp.float32) * s, 'bk': jnp.zeros((G * HD,), jnp.float32), 'Wv': jax.random.normal(ks[4], (G * HD, HID), jnp.float32) * s, 'bv': jnp.zeros((G * HD,), jnp.float32), 'Wo': jax.random.normal(ks[5], (HID, HID), jnp.float32) * s, 'bo': jnp.zeros((HID,), jnp.float32)}
        return inp
    _L0_xattn_all = _L0_xattn_setup()
    _L0_xattn_in = {k: v for k, v in _L0_xattn_all.items() if k in ('Wq', 'bq', 'Wk', 'bk', 'Wv', 'bv', 'Wo', 'bo')}
    del _L0_xattn_all

    def _L0_ffn_setup():
        import jax, jax.numpy as jnp
        import numpy as np
        N_EXPERTS = 8
        TOP_K = 2
        N_GROUP = 4
        TOPK_GROUP = 2
        ROUTED_SCALE = 1.0

        def _group_limited_topk(scores):
            T, N = scores.shape
            E = N // N_GROUP
            group_scores = scores.reshape(T, N_GROUP, E).max(axis=-1)
            _, gidx = jax.lax.top_k(group_scores, TOPK_GROUP)
            gmask = jax.nn.one_hot(gidx, N_GROUP, dtype=scores.dtype).sum(1)
            smask = jnp.repeat(gmask, E, axis=1)
            masked = jnp.where(smask > 0, scores, jnp.zeros((), scores.dtype))
            topk_w, topk_i = jax.lax.top_k(masked, TOP_K)
            return (topk_w, topk_i)
        key = jax.random.key(seed)
        ks = jax.random.split(key, 8)
        B, S, H, F, FS, N = (2, 256, 512, 352, 704, N_EXPERTS)
        std = jnp.float32(0.02)
        return {'hidden_states': jax.random.normal(ks[0], (B, S, H), jnp.float32), 'gate_weight': jax.random.normal(ks[1], (N, H), jnp.float32) * std, 'gate_w': jax.random.normal(ks[2], (N, F, H), jnp.float32) * std, 'up_w': jax.random.normal(ks[3], (N, F, H), jnp.float32) * std, 'down_w': jax.random.normal(ks[4], (N, H, F), jnp.float32) * std, 'sh_gate_w': jax.random.normal(ks[5], (FS, H), jnp.float32) * std, 'sh_up_w': jax.random.normal(ks[6], (FS, H), jnp.float32) * std, 'sh_down_w': jax.random.normal(ks[7], (H, FS), jnp.float32) * std}
    _L0_ffn_all = _L0_ffn_setup()
    _L0_ffn_in = {k: v for k, v in _L0_ffn_all.items() if k in ('gate_weight', 'gate_w', 'up_w', 'down_w', 'sh_gate_w', 'sh_up_w', 'sh_down_w')}
    del _L0_ffn_all
    return {'x': x, 'ctx_2048': ctx_2048, 'mask_SxS2_bc0': mask_SxS2_bc0, 'mask_BxS2_bk0': mask_BxS2_bk0, 'g_xattn': g_xattn, 'g_ffn': g_ffn, 'L0_xattn_Wq': _L0_xattn_in['Wq'], 'L0_xattn_bq': _L0_xattn_in['bq'], 'L0_xattn_Wk': _L0_xattn_in['Wk'], 'L0_xattn_bk': _L0_xattn_in['bk'], 'L0_xattn_Wv': _L0_xattn_in['Wv'], 'L0_xattn_bv': _L0_xattn_in['bv'], 'L0_xattn_Wo': _L0_xattn_in['Wo'], 'L0_xattn_bo': _L0_xattn_in['bo'], 'L0_ffn_gate_weight': _L0_ffn_in['gate_weight'], 'L0_ffn_gate_w': _L0_ffn_in['gate_w'], 'L0_ffn_up_w': _L0_ffn_in['up_w'], 'L0_ffn_down_w': _L0_ffn_in['down_w'], 'L0_ffn_sh_gate_w': _L0_ffn_in['sh_gate_w'], 'L0_ffn_sh_up_w': _L0_ffn_in['sh_up_w'], 'L0_ffn_sh_down_w': _L0_ffn_in['sh_down_w']}

def reference(x, ctx_2048, mask_SxS2_bc0, mask_BxS2_bk0, g_xattn, g_ffn, L0_xattn_Wq, L0_xattn_bq, L0_xattn_Wk, L0_xattn_bk, L0_xattn_Wv, L0_xattn_bv, L0_xattn_Wo, L0_xattn_bo, L0_ffn_gate_weight, L0_ffn_gate_w, L0_ffn_up_w, L0_ffn_down_w, L0_ffn_sh_gate_w, L0_ffn_sh_up_w, L0_ffn_sh_down_w):
    import jax
    import jax.numpy as jnp

    def _L0_xattn_ref(X, encoder_output, causal_mask, padding_mask, Wq, bq, Wk, bk, Wv, bv, Wo, bo):
        import jax, jax.numpy as jnp
        import numpy as np
        B, LQ, LKV = (4, 256, 256)
        HID, H, G = (512, 32, 8)
        HD = HID // H
        HPG = H // G
        b = X.shape[0]
        q = X @ Wq.T + bq
        k = encoder_output @ Wk.T + bk
        v = encoder_output @ Wv.T + bv
        q = q.reshape(b, LQ, G, HPG, HD).transpose(0, 2, 3, 1, 4)
        k = k.reshape(b, LKV, G, HD).transpose(0, 2, 1, 3)
        v = v.reshape(b, LKV, G, HD).transpose(0, 2, 1, 3)
        scores = jnp.einsum('bgrqd,bgkd->bgrqk', q, k) / jnp.sqrt(jnp.float32(HD))
        scores = jnp.where(causal_mask[None, None, None, :, :], -jnp.inf, scores)
        scores = jnp.where(padding_mask[:, None, None, None, :], -jnp.inf, scores)
        w = jax.nn.softmax(scores, axis=-1)
        out = jnp.einsum('bgrqk,bgkd->bgrqd', w, v)
        out = out.reshape(b, H, LQ, HD).transpose(0, 2, 1, 3).reshape(b, LQ, HID)
        return out @ Wo.T + bo

    def _L0_ffn_ref(hidden_states, gate_weight, gate_w, up_w, down_w, sh_gate_w, sh_up_w, sh_down_w):
        import jax, jax.numpy as jnp
        import numpy as np
        N_EXPERTS = 8
        TOP_K = 2
        N_GROUP = 4
        TOPK_GROUP = 2
        ROUTED_SCALE = 1.0

        def _group_limited_topk(scores):
            T, N = scores.shape
            E = N // N_GROUP
            group_scores = scores.reshape(T, N_GROUP, E).max(axis=-1)
            _, gidx = jax.lax.top_k(group_scores, TOPK_GROUP)
            gmask = jax.nn.one_hot(gidx, N_GROUP, dtype=scores.dtype).sum(1)
            smask = jnp.repeat(gmask, E, axis=1)
            masked = jnp.where(smask > 0, scores, jnp.zeros((), scores.dtype))
            topk_w, topk_i = jax.lax.top_k(masked, TOP_K)
            return (topk_w, topk_i)
        B, S, H = hidden_states.shape
        h = hidden_states.reshape(-1, H)
        logits = h.astype(jnp.float32) @ gate_weight.astype(jnp.float32).T
        scores = jax.nn.softmax(logits, axis=-1)
        topk_w, topk_i = _group_limited_topk(scores)
        topk_w = (topk_w * ROUTED_SCALE).astype(h.dtype)
        wmat = (jax.nn.one_hot(topk_i, N_EXPERTS, dtype=topk_w.dtype) * topk_w[..., None]).sum(axis=1)
        g = jnp.einsum('th,nfh->ntf', h, gate_w)
        u = jnp.einsum('th,nfh->ntf', h, up_w)
        e = jnp.einsum('ntf,nhf->nth', jax.nn.silu(g) * u, down_w)
        routed = jnp.einsum('nth,tn->th', e, wmat)
        sg = h @ sh_gate_w.T
        su = h @ sh_up_w.T
        shared = jax.nn.silu(sg) * su @ sh_down_w.T
        return (routed + shared).reshape(B, S, H)
    x = x + jnp.tanh(g_xattn[0]) * _L0_xattn_ref(_layernorm(x, axis=-1), ctx_2048, mask_SxS2_bc0, mask_BxS2_bk0, L0_xattn_Wq, L0_xattn_bq, L0_xattn_Wk, L0_xattn_bk, L0_xattn_Wv, L0_xattn_bv, L0_xattn_Wo, L0_xattn_bo)
    x = x + jnp.tanh(g_ffn[0]) * _L0_ffn_ref(_layernorm(x, axis=-1), L0_ffn_gate_weight, L0_ffn_gate_w, L0_ffn_up_w, L0_ffn_down_w, L0_ffn_sh_gate_w, L0_ffn_sh_up_w, L0_ffn_sh_down_w)
    return x

_drawn_inputs = setup_inputs


def setup_inputs(seed=0):
    import zlib

    import numpy as np

    out = dict(_drawn_inputs(seed))
    spreads = {'L0_xattn_bq': (0.0, 0.8),
     'L0_xattn_bk': (0.0, 2.0),
     'L0_xattn_bv': (0.0, 0.1),
     'L0_xattn_bo': (0.0, 0.1)}
    factors = {'L0_xattn_Wq': 8.0,
     'L0_xattn_Wk': 8.0,
     'L0_ffn_gate_weight': 5.96,
     'L0_ffn_gate_w': 5.168,
     'L0_ffn_up_w': 5.077,
     'L0_ffn_down_w': 5.079,
     'L0_ffn_sh_gate_w': 5.135,
     'L0_ffn_sh_up_w': 5.025,
     'L0_ffn_sh_down_w': 5.013}
    for name, (base, spread) in spreads.items():
        noise = np.random.default_rng([zlib.crc32(name.encode()), seed]).standard_normal(out[name].shape)
        drawn = base * np.exp(spread * noise) if base else spread * noise
        out[name] = jnp.asarray(drawn.astype(out[name].dtype))
    for name, factor in factors.items():
        out[name] = (out[name] * factor).astype(out[name].dtype)
    return out
```

```python
from contextlib import ExitStack

import concourse.bass as bass
from concourse import mybir

F32 = mybir.dt.float32
F32R = mybir.dt.float32r
BF16 = mybir.dt.bfloat16
I32 = mybir.dt.int32
U8 = mybir.dt.uint8
ALU = mybir.AluOpType
ACT = mybir.ActivationFunctionType
AX = mybir.AxisListType

P = 128
B, S, D = 8, 256, 512
T = B * S
QC = S // P
KC = D // P
G, R, HD = 8, 4, 16
GP = G // 2
H = G * R
PAIR = 2 * HD
AUX = 3 * PAIR
NEG = -1e30
EPS = 1e-5
RSQRT_MAGIC = float(0x5F3759DF)
NORM_STEPS = 18

SCORE_UNITS = GP * R * QC
PROB_UNITS = G * QC * R // 2
PROB_LAG = 3
PV_LAG = PROB_LAG + 5
SLOTS = PV_LAG + 4 * 7 + 2
POOL_SETUP = 13
STACK_DMAS = 13


def at_least(eng, sem, value):
    if isinstance(value, int) and value <= 0:
        return
    eng.wait_ge(sem, value)


def wait_alone(eng, over, sem, value):
    if isinstance(value, int):
        at_least(eng, sem, value)
        return
    count = eng.to_reg(value)
    eng.wait_ge(over, 1)
    eng.wait_ge(sem, count)


class Batch:

    def __init__(self, pair, parity):
        self.pair, self.parity = pair, parity
        self.index = 2 * pair + parity

    def ahead(self, k):
        return Batch(self.pair + (self.parity + k) // 2, (self.parity + k) % 2)


def build_kernel(nc, A, out):
    x2_buf = nc.dram_tensor("x2_buf", (T, D), F32, kind="Internal").ap()
    xn_buf = nc.dram_tensor("xn_buf", (T + P, D), F32, kind="Internal").ap()
    with ExitStack() as semaphores:
        attention_phase(nc, A, x2_buf, xn_buf, semaphores)
        expert_phase(nc, A, x2_buf, xn_buf, out, semaphores)


def attention_phase(nc, A, x2_buf, xn_buf, semaphores):
    with ExitStack() as ctx:
        def sb(name, shape, dt=F32):
            return ctx.enter_context(nc.sbuf_tensor(name, shape, dt))

        def ps(name, shape):
            return ctx.enter_context(nc.psum_tensor(name, shape, F32))

        def sem(name):
            return semaphores.enter_context(nc.semaphore(name))

        identf = sb("identf", [P, P])
        identb = sb("identb", [P, P], BF16)
        tanh_gate = sb("tanh_gate", [P, 1])
        bo_gated = sb("bo_gated", [P, D])
        bq = sb("bq", [P, R])
        bk = sb("bk", [P, 1])
        parity = sb("parity", [P, 2])
        bv = sb("bv", [P, 1])
        wqkv_hi = sb("wqkv_hi", [P, KC, 768], F32R)
        wqkv_lo = sb("wqkv_lo", [P, KC, 768], F32R)
        wo_hi = sb("wo_hi", [P, KC, D], F32R)
        wo_lo = sb("wo_lo", [P, KC, D], F32R)
        causal_raw = sb("causal_raw", [P, 2, QC, S], U8)
        causal_neg = sb("causal_neg", [P, QC, S], BF16)
        causalT_neg = sb("causalT_neg", [P, QC, S], BF16)
        pad_raw = sb("pad_raw", [P, B, S], U8)
        pad_neg = sb("pad_neg", [P, B, S], BF16)
        padT_raw = sb("padT_raw", [P, QC, B], U8)
        padT_neg = sb("padT_neg", [P, QC, B], BF16)
        xt = sb("xt", [P, QC, D])
        ln_stats = sb("ln_stats", [P, 2, QC, 6])
        ln_mv = sb("ln_mv", [P, 2, QC, 2])
        ln_var = sb("ln_var", [P, 2, QC])
        ln_y = sb("ln_y", [P, 2, QC])
        ln_t = sb("ln_t", [P, 2, QC])
        xn = sb("xn", [P, QC, D])
        xT_hi = sb("xT_hi", [P, KC, S], F32R)
        xT_lo = sb("xT_lo", [P, KC, S], F32R)
        cT_raw = sb("cT_raw", [P, KC, S])
        cT_hi = sb("cT_hi", [P, KC, S], F32R)
        cT_lo = sb("cT_lo", [P, KC, S], F32R)
        q_hi = sb("q_hi", [P, R, S], F32R)
        q_lo = sb("q_lo", [P, R, S], F32R)
        k_raw = sb("k_raw", [P, S])
        k_hi = sb("k_hi", [P, 2, S], F32R)
        k_lo = sb("k_lo", [P, 2, S], F32R)
        vT = sb("vT", [P, S])
        v_stage = sb("v_stage", [P, QC, G, HD])
        q_stack = [sb(f"q_stack{i}", [P, GP, R, S], F32R) for i in range(2)]
        k_stack = [sb(f"k_stack{i}", [P, GP, 2, S], F32R) for i in range(2)]
        v_ones = [sb(f"v_ones{i}", [P, QC, G, 2 * HD]) for i in range(2)]
        mask = [sb(f"mask{i}", [P, QC, S], BF16) for i in range(2)]
        maskT = [sb(f"maskT{i}", [P, QC, S], BF16) for i in range(2)]
        row_max = sb("row_max", [P, QC, H])
        neg_max = sb("neg_max", [P, QC, 2, 2, H // 2], F32R)
        neg_maxT = sb("neg_maxT", [2 * H, S], F32R)
        probs = sb("probs", [P, 8, 512])
        mixed = [sb(f"mixed{i}", [P, 4, 512]) for i in range(2)]
        inv_sum = sb("inv_sum", [P, R, 4])
        attn = sb("attn", [P, QC, D])
        aT_hi = sb("aT_hi", [P, KC, P], F32R)
        aT_lo = sb("aT_lo", [P, KC, P], F32R)
        x_res = sb("x_res", [P, QC, D])
        x2 = sb("x2", [P, QC, D])
        xn2 = sb("xn2", [P, QC, D])

        ones = xT_hi[0:2]
        zeros = k_stack[0][AUX + 4:AUX + 8].rearrange("p g h s -> p (g h s)").rearrange(
            "p (g r s) -> p g r s", g=GP // 2, r=R)

        score_bank = [ps(f"score_bank{i}", [P, 2, S]) for i in range(2)]
        prob_bank = [ps(f"prob_bank{i}", [P, 2, S]) for i in range(2)]
        pv_bank = ps("pv_bank", [P, 512])
        front_bank = [ps(f"front_bank{i}", [P, 512]) for i in range(2)]
        tail_bank = ps("tail_bank", [P, 512])

        weights_in, consts_in = sem("weights_in"), sem("consts_in")
        ones_in = sem("ones_in")
        x_in, ctx_in, res_in = sem("x_in"), sem("ctx_in"), sem("res_in")
        stack_in = [sem("stack_in_a"), sem("stack_in_b")]
        max_in = sem("max_in")
        x2_out, xn2_out = sem("x2_out"), sem("xn2_out")
        pool_setup, mask_setup = sem("pool_setup"), sem("mask_setup")
        dve_setup, act_setup = sem("dve_setup"), sem("act_setup")
        front_done, scores_done, maxT_done = sem("front_done"), sem("scores_done"), sem("maxT_done")
        probs_scored, pv_done, tail_done = sem("probs_scored"), sem("pv_done"), sem("tail_done")
        ln1_step, xT_lo_done, q_lo_done, k_lo_done = sem("ln1_step"), sem("xT_lo_done"), sem("q_lo_done"), sem("k_lo_done")
        maxima_done, max_split = sem("maxima_done"), sem("max_split")
        tail_step, ln2_step = sem("tail_step"), sem("ln2_step")
        xT_hi_done, q_hi_done, kv_copied, v_staged = sem("xT_hi_done"), sem("q_hi_done"), sem("kv_copied"), sem("v_staged")
        exp_done, mixed_done, maxT_copied, aT_hi_done = sem("exp_done"), sem("mixed_done"), sem("maxT_copied"), sem("aT_hi_done")
        ctx_split, mask_done, maskT_done, res_done, v_ready = (
            sem("ctx_split"), sem("mask_done"), sem("maskT_done"), sem("res_done"), sem("v_ready"))

        block = ctx.enter_context(nc.Block())

        def rows(buf, batch):
            return buf[bass.ds(S * batch.index, S), :].rearrange("(c p) d -> p c d", p=P)

        def copy_rows(eng, dst, src):
            return eng.dma_start(dst.bitcast(F32), src.bitcast(F32))

        def pipeline(iteration, eng):
            def part(n):
                return dict(prep=0 <= n + 3 < B, front=0 <= n + 2 < B, score=0 <= n + 1 < B, soft=0 <= n < B,
                            tail=0 <= n - 1 < B)
            for n in (-3, -2, -1, 0):
                iteration(Batch(n // 2, n % 2), **part(n))
            with eng.Fori(0, B // 2 - 2) as pair:
                for k in (1, 2):
                    iteration(Batch(pair, 0).ahead(k), prep=True, front=True, score=True, soft=True, tail=True)
            for n in (B - 3, B - 2, B - 1, B):
                iteration(Batch(n // 2, n % 2), **part(n))

        @block.sync
        def _(sp):
            wqkv_raw = probs[:, 0:6, :].rearrange("p a b -> p (a b)")
            wo_raw = mixed[0][:].rearrange("p a b -> p (a b)")
            sp.dma_start(wqkv_raw, A["wqkv"]).then_inc(weights_in, 16)
            sp.dma_start(wo_raw, A["wo"]).then_inc(weights_in, 16)
            sp.wait_ge(pool_setup, POOL_SETUP)
            for i in range(2):
                for g2 in range(2):
                    copy_rows(sp, k_stack[i][AUX + 2 * g2:AUX + 2 * g2 + 2, :, g2, :], ones).then_inc(ones_in, 16)
            sp.wait_ge(ones_in, 64)

            def stack(m, half):
                if half == 0:
                    wait_alone(sp, pool_setup, q_lo_done, R * (m.index + 1))
                    wait_alone(sp, pool_setup, k_lo_done, 2 * (m.index + 1))
                wait_alone(sp, pool_setup, probs_scored, PROB_UNITS * (m.index - 2) + PROB_UNITS // 2 * (half + 1))
                qs, ks = q_stack[m.parity], k_stack[m.parity]
                for gp in range(GP // 2 * half, GP // 2 * (half + 1)):
                    src = slice(PAIR * gp, PAIR * (gp + 1))
                    for part, (q, k) in enumerate([(q_hi, k_hi), (q_hi, k_lo), (q_lo, k_hi)]):
                        dst = slice(PAIR * part, PAIR * (part + 1))
                        copy_rows(sp, qs[dst, gp, :, :], q[src, :, :]).then_inc(stack_in[half], 16)
                        copy_rows(sp, ks[dst, gp, :, :], k[src, :, :]).then_inc(stack_in[half], 16)
                copy_rows(sp, qs[AUX:AUX + 4, GP // 2 * half:GP // 2 * (half + 1), :, :], zeros).then_inc(stack_in[half], 16)

            def iteration(n, prep, front, score, soft, tail):
                m, after, t = n.ahead(2), n.ahead(3), n.ahead(-1)
                if prep:
                    wait_alone(sp, pool_setup, ln1_step, NORM_STEPS * after.index)
                    sp.dma_start(xt[:], rows(A["x"], after)).then_inc(x_in, 16)
                    wait_alone(sp, pool_setup, ctx_split, 2 * after.index)
                    sp.dma_start(cT_raw[:], A["ctxT"][:, bass.ds(S * after.index, S)].rearrange(
                        "(k p) s -> p k s", p=P)).then_inc(ctx_in, 16)
                if front:
                    stack(m, 0)
                if tail:
                    wait_alone(sp, pool_setup, tail_step, 12 * (t.index + 1))
                    sp.dma_start(rows(x2_buf, t), x2[:]).then_inc(x2_out, 16)
                if soft:
                    wait_alone(sp, pool_setup, tail_step, 12 * n.index)
                    sp.dma_start(x_res[:], rows(A["x"], n)).then_inc(res_in, 16)
                if tail:
                    wait_alone(sp, pool_setup, ln2_step, NORM_STEPS * (t.index + 1))
                    sp.dma_start(rows(xn_buf, t), xn2[:]).then_inc(xn2_out, 16)
                if front:
                    stack(m, 1)

            pipeline(iteration, sp)
            sp.wait_ge(x2_out, 16 * B)
            sp.wait_ge(xn2_out, 16 * B)

        @block.gpsimd
        def _(pool):
            pool.dma_start(bq[:], A["bq"]).then_inc(consts_in, 16)
            pool.dma_start(bk[:], A["bk"]).then_inc(consts_in, 16)
            pool.dma_start(bv[:], A["bv"]).then_inc(consts_in, 16)
            pool.dma_start(parity[:], A["parity"]).then_inc(consts_in, 16)
            pool.dma_start(tanh_gate[:], A["g_xattn"].partition_broadcast(P)).then_inc(consts_in, 16)
            pool.dma_start(bo_gated[:], A["bo"].partition_broadcast(P)).then_inc(consts_in, 16)
            pool.dma_start(causal_raw[:, 0], A["causal"].rearrange("(c p) k -> p c k", p=P)).then_inc(consts_in, 16)
            pool.dma_start(causal_raw[:, 1], A["causalT"].rearrange("(c p) q -> p c q", p=P)).then_inc(consts_in, 16)
            pool.dma_start(pad_raw[:], A["pad"].partition_broadcast(P)).then_inc(consts_in, 16)
            pool.dma_start(padT_raw[:], A["padT"].rearrange("(c p) b -> p c b", p=P)).then_inc(consts_in, 16)
            pool.memset(identf[:], 0.0).then_inc(pool_setup, 1)
            pool.memset(identb[:], 0.0).then_inc(pool_setup, 1)
            pool.wait_ge(pool_setup, 2)
            for ident in (identf, identb):
                pool.affine_select(out=ident[:], in_=ident[:], compare_op=ALU.not_equal, fill=1.0, base=0,
                                   pattern=[[-1, P]], channel_multiplier=1).then_inc(pool_setup, 1)
            pool.memset(ones.bitcast(F32), 1.0).then_inc(pool_setup, 1)
            for i in range(2):
                pool.memset(k_stack[i][:].bitcast(F32), 0.0).then_inc(pool_setup, 1)
                pool.memset(v_ones[i][:], 0.0).then_inc(pool_setup, 1)
            pool.wait_ge(pool_setup, 9)
            for i in range(2):
                pool.memset(v_ones[i][:, :, :, HD:HD + 1], 1.0).then_inc(pool_setup, 1)
            pool.wait_ge(consts_in, 16 * 10)
            pool.tensor_scalar(causal_neg[:], causal_raw[:, 0], NEG, None, ALU.mult).then_inc(pool_setup, 1)
            pool.tensor_scalar(causalT_neg[:], causal_raw[:, 1], NEG, None, ALU.mult).then_inc(pool_setup, 1)
            pool.tensor_scalar(padT_neg[:], padT_raw[:], NEG, None, ALU.mult).then_inc(mask_setup, 1)
            pool.tensor_scalar(pad_neg[:], pad_raw[:], NEG, None, ALU.mult).then_inc(mask_setup, 1)
            pool.wait_ge(mask_setup, 2)
            pool.wait_ge(pool_setup, POOL_SETUP)

            def iteration(n, prep, front, score, soft, tail):
                m, after = n.ahead(2), n.ahead(3)
                if prep:
                    at_least(pool, ctx_in, 16 * (after.index + 1))
                    wait_alone(pool, mask_setup, front_done, 6 * (after.index - 1) + 5)
                    pool.tensor_copy(cT_hi[:], cT_raw[:]).then_inc(ctx_split, 1)
                    at_least(pool, ctx_split, 2 * after.index + 1)
                    pool.tensor_tensor(cT_lo[:], cT_raw[:], cT_hi[:].bitcast(F32), ALU.subtract).then_inc(ctx_split, 1)
                if front:
                    at_least(pool, maxima_done, SCORE_UNITS * (m.index - 1))
                    pool.tensor_tensor(mask[m.parity][:], causal_neg[:],
                                       pad_neg[:, bass.ds(m.index, 1), :].to_broadcast([P, QC, S]),
                                       ALU.add).then_inc(mask_done, 1)
                if soft:
                    at_least(pool, res_in, 16 * (n.index + 1))
                    at_least(pool, act_setup, 2)
                    pool.tensor_tensor(x_res[:], x_res[:], bo_gated[:].unsqueeze(1).to_broadcast([P, QC, D]),
                                       ALU.add).then_inc(res_done, 1)
                if front:
                    at_least(pool, probs_scored, PROB_UNITS * (m.index - 1))
                    pool.tensor_tensor(maskT[m.parity][:], causalT_neg[:],
                                       padT_neg[:, :, bass.ds(m.index, 1)].to_broadcast([P, QC, S]),
                                       ALU.add).then_inc(maskT_done, 1)
                    at_least(pool, v_staged, m.index + 1)
                    wait_alone(pool, mask_setup, pv_done, 8 * (m.index - 1))
                    pool.tensor_copy(v_ones[m.parity][:, :, :, 0:HD], v_stage[:]).then_inc(v_ready, 1)

            pipeline(iteration, pool)

        @block.tensor
        def _(pe):
            pe.wait_ge(pool_setup, POOL_SETUP)
            pe.wait_ge(ones_in, 64)
            pe.wait_ge(dve_setup, 4)

            def products(out_, left, right):
                n = len(left)
                for c in range(n):
                    for j, (a, b) in enumerate([(0, 0), (1, 0), (0, 1)]):
                        last = pe.matmul(out_, left[c][a], right[c][b], start=c == 0 and j == 0,
                                         stop=c == n - 1 and j == 2)
                return last

            def front_transposes(m, f):
                at_least(pe, ln1_step, NORM_STEPS * (m.index + 1))
                at_least(pe, (kv_copied, v_staged)[f], (4, 1)[f] * m.index)
                for k in range(2):
                    for c in range(QC):
                        last = pe.transpose(front_bank[f][:, k * S + c * P:k * S + (c + 1) * P],
                                            xn[:, c, (2 * f + k) * P:(2 * f + k + 1) * P], identf[:])
                last.then_inc(front_done, 1)

            def front_queries(m, f):
                if f == 0:
                    at_least(pe, xT_lo_done, 2 * (m.index + 1))
                for r in (2 * f, 2 * f + 1):
                    last = products(front_bank[f][:, (r % 2) * S:(r % 2 + 1) * S],
                                    [(wqkv_hi[:, c, r * P:(r + 1) * P], wqkv_lo[:, c, r * P:(r + 1) * P]) for c in range(KC)],
                                    [(xT_hi[:, c, :], xT_lo[:, c, :]) for c in range(KC)])
                last.then_inc(front_done, 1)

            def front_keys_values(m):
                at_least(pe, ctx_split, 2 * (m.index + 1))
                at_least(pe, q_lo_done, R * m.index + 2)
                for j in range(2):
                    cols = slice(D + j * P, D + (j + 1) * P)
                    last = products(front_bank[0][:, j * S:(j + 1) * S],
                                    [(wqkv_hi[:, c, cols], wqkv_lo[:, c, cols]) for c in range(KC)],
                                    [(cT_hi[:, c, :], cT_lo[:, c, :]) for c in range(KC)])
                last.then_inc(front_done, 1)

            def front_values(m):
                at_least(pe, kv_copied, 4 * m.index + 1)
                at_least(pe, q_lo_done, R * (m.index + 1))
                for c in range(QC):
                    last = pe.transpose(front_bank[1][:, c * P:(c + 1) * P], vT[:, c * P:(c + 1) * P], identf[:])
                last.then_inc(front_done, 1)

            def score_unit(m, u):
                gp, r, c = u // (R * QC), u // QC % R, u % QC
                if u % (SCORE_UNITS // 2) == 0:
                    at_least(pe, stack_in[2 * u // SCORE_UNITS], 16 * STACK_DMAS * (m.index + 1))
                bank = score_bank[(m.parity + u) % 2]
                if u == 0:
                    at_least(pe, maxima_done, SCORE_UNITS * m.index)
                elif u == 1:
                    at_least(pe, maxT_copied, m.index)
                else:
                    at_least(pe, maxima_done, SCORE_UNITS * m.index + u - 1)
                pe.matmul(bank[:].rearrange("p a b -> p (a b)"), q_stack[m.parity][:, gp, r, c * P:(c + 1) * P],
                          k_stack[m.parity][:, gp].rearrange("p a b -> p (a b)"),
                          start=True, stop=True).then_inc(scores_done, 1)

            def transpose_maxima(m):
                wait_alone(pe, dve_setup, max_split, 2 * (m.index + 1))
                bank = score_bank[(m.parity + SCORE_UNITS) % 2][:].rearrange("p a b -> p (a b)")
                for c in range(QC):
                    last = pe.transpose(bank[0:2 * H, c * P:(c + 1) * P],
                                        neg_max[:, c].rearrange("p a b h -> p (a b h)").bitcast(F32), identf[:])
                last.then_inc(maxT_done, 1)

            def prob_unit(n, v):
                gg, rp, kc, j = v // 16, v // 8 % 2, v // 4 % 2, v % 4
                gp, g2 = 2 * gg + j // 2, j % 2
                if v == 0:
                    at_least(pe, max_in, 16 * (n.index + 1))
                    at_least(pe, maskT_done, n.index + 1)
                at_least(pe, exp_done, PROB_UNITS * n.index + v - 1)
                bank = prob_bank[v % 2][:].rearrange("p a b -> p (a b)")
                pe.matmul(bank, k_stack[n.parity][:, gp, g2, kc * P:(kc + 1) * P],
                          q_stack[n.parity][:, gp, 2 * rp:2 * rp + 2, :].rearrange("p a b -> p (a b)"),
                          start=True, stop=False)
                pe.matmul(prob_bank[v % 2][:], identb[:],
                          maskT[n.parity][:, kc, :].unsqueeze(1).to_broadcast([P, 2, S]),
                          start=False, stop=True).then_inc(probs_scored, 1)

            def value_group(n, k):
                gg, w, kc = k // 4, k // 2, k % 2
                if k == 0:
                    at_least(pe, v_ready, n.index + 1)
                at_least(pe, exp_done, PROB_UNITS * n.index + 4 * k + 4)
                if kc == 0:
                    at_least(pe, mixed_done, 4 * n.index + w)
                for j in range(4):
                    last = pe.matmul(pv_bank[32 * j:32 * (j + 1), :], v_ones[n.parity][:, kc, 4 * gg + j, :],
                                     probs[:, (4 * k + j) % 8, :], start=kc == 0, stop=kc == 1)
                last.then_inc(pv_done, 1)

            def tail_unmix(t, c, gg):
                at_least(pe, mixed_done, 4 * (t.index + 1))
                at_least(pe, tail_step, 12 * t.index + 6 * c + 2 * gg)
                for r in range(R):
                    last = pe.transpose(tail_bank[:, r * P:(r + 1) * P],
                                        mixed[t.parity][:, 2 * gg + r // 2, (r % 2) * S + c * P:(r % 2) * S + (c + 1) * P],
                                        identf[:])
                last.then_inc(tail_done, 1)

            def tail_transposes(t, c):
                at_least(pe, tail_step, 12 * t.index + 6 * c + 4)
                for k in range(KC):
                    last = pe.transpose(tail_bank[:, k * P:(k + 1) * P], attn[:, c, k * P:(k + 1) * P], identf[:])
                last.then_inc(tail_done, 1)

            def tail_project(t, c):
                at_least(pe, tail_step, 12 * t.index + 6 * c + 5)
                products(tail_bank[:], [(aT_hi[:, k, :], aT_lo[:, k, :]) for k in range(KC)],
                         [(wo_hi[:, k, :], wo_lo[:, k, :]) for k in range(KC)]).then_inc(tail_done, 1)

            def iteration(n, prep, front, score, soft, tail):
                m, s, t = n.ahead(2), n.ahead(1), n.ahead(-1)
                for slot in range(SLOTS):
                    if score and slot < SCORE_UNITS:
                        score_unit(s, slot)
                    if soft and 0 <= slot - PROB_LAG < PROB_UNITS:
                        prob_unit(n, slot - PROB_LAG)
                    if soft and 0 <= slot - PV_LAG <= 28 and (slot - PV_LAG) % 4 == 0:
                        value_group(n, (slot - PV_LAG) // 4)
                    if front:
                        if slot in (0, 1):
                            front_transposes(m, slot)
                        if slot in (9, 11):
                            front_queries(m, (slot - 9) // 2)
                        if slot == 13:
                            front_keys_values(m)
                        if slot == 15:
                            front_values(m)
                    if tail:
                        for c in range(QC):
                            if slot == 17 * c:
                                tail_unmix(t, c, 0)
                            if slot == 17 * c + 2:
                                tail_unmix(t, c, 1)
                            if slot == 17 * c + 4:
                                tail_transposes(t, c)
                            if slot == 17 * c + 7:
                                tail_project(t, c)
                    if score and slot == 34:
                        transpose_maxima(s)

            pipeline(iteration, pe)

        @block.scalar
        def _(act):
            act.wait_ge(consts_in, 16 * 10)
            act.activation(tanh_gate[:], tanh_gate[:], ACT.Tanh).then_inc(act_setup, 1)
            act.wait_ge(act_setup, 1)
            act.activation(bo_gated[:], bo_gated[:], ACT.Copy, scale=tanh_gate[:, 0:1]).then_inc(act_setup, 1)
            act.wait_ge(weights_in, 32)
            act.activation(wqkv_hi[:].rearrange("p a b -> p (a b)"), probs[:, 0:6, :].rearrange("p a b -> p (a b)"),
                           ACT.Copy).then_inc(act_setup, 1)
            act.activation(wo_hi[:].rearrange("p a b -> p (a b)"), mixed[0][:].rearrange("p a b -> p (a b)"),
                           ACT.Copy).then_inc(act_setup, 1)
            act.wait_ge(dve_setup, 4)

            def front_x_hi(m, f):
                at_least(act, front_done, 6 * m.index + f + 1)
                at_least(act, front_done, 6 * (m.index - 1) + 4)
                act.activation(xT_hi[:, 2 * f:2 * f + 2, :].rearrange("p a b -> p (a b)"), front_bank[f][:],
                               ACT.Copy).then_inc(xT_hi_done, 1)

            def front_q_hi(m, r):
                at_least(act, front_done, 6 * m.index + 3 + r // 2)
                if r == 0:
                    for half in range(2):
                        at_least(act, stack_in[half], 16 * STACK_DMAS * m.index)
                act.activation(q_hi[:, r, :], front_bank[r // 2][:, (r % 2) * S:(r % 2 + 1) * S], ACT.Identity,
                               bias=bq[:, r:r + 1]).then_inc(q_hi_done, 1)

            def front_kv(m):
                at_least(act, front_done, 6 * m.index + 5)
                act.activation(vT[:], front_bank[0][:, S:2 * S], ACT.Identity, bias=bv[:, 0:1]).then_inc(kv_copied, 1)
                for half in range(2):
                    at_least(act, stack_in[half], 16 * STACK_DMAS * m.index)
                act.activation(k_raw[:], front_bank[0][:, 0:S], ACT.Identity, bias=bk[:, 0:1]).then_inc(kv_copied, 1)
                at_least(act, kv_copied, 4 * m.index + 2)
                for g2 in range(2):
                    act.activation(k_hi[:, g2, :], k_raw[:], ACT.Copy, scale=parity[:, g2:g2 + 1]).then_inc(kv_copied, 1)

            def front_v(m):
                at_least(act, front_done, 6 * m.index + 6)
                at_least(act, v_ready, m.index)
                act.activation(v_stage[:].rearrange("p c g d -> p (c g d)"), front_bank[1][:, 0:QC * P],
                               ACT.Copy).then_inc(v_staged, 1)

            def exp_unit(n, v):
                at_least(act, probs_scored, PROB_UNITS * n.index + v + 1)
                if v % 4 == 0:
                    at_least(act, pv_done, 8 * n.index + v // 4 - 1)
                act.activation(probs[:, v % 8, :], prob_bank[v % 2][:].rearrange("p a b -> p (a b)"), ACT.Exp,
                               scale=HD ** -0.5).then_inc(exp_done, 1)

            def copy_mixed(n, w):
                at_least(act, pv_done, 8 * n.index + 2 * w + 2)
                if w == 0:
                    at_least(act, tail_done, 8 * (n.index - 1))
                act.activation(mixed[n.parity][:, w, :], pv_bank[:], ACT.Copy).then_inc(mixed_done, 1)

            def stack_maxima(m):
                at_least(act, maxT_done, m.index + 1)
                at_least(act, max_in, 16 * m.index)
                at_least(act, stack_in[0], 16 * STACK_DMAS * (m.index + 1))
                at_least(act, stack_in[1], 16 * STACK_DMAS * (m.index + 1))
                act.activation(neg_maxT[:], score_bank[(m.parity + SCORE_UNITS) % 2][0:2 * H].rearrange(
                    "p a b -> p (a b)")[:, 0:S], ACT.Copy).then_inc(maxT_copied, 1)
                at_least(act, maxT_copied, m.index + 1)
                copy_rows(act, q_stack[m.parity][AUX:AUX + 4].rearrange("o g r s -> o (g r s)"), neg_maxT[:]).then_inc(max_in, 16)

            def tail_hi(t, c):
                at_least(act, tail_done, 8 * t.index + 4 * c + 3)
                at_least(act, tail_done, 8 * t.index + 4 * c)
                act.activation(aT_hi[:].rearrange("p k q -> p (k q)"), tail_bank[:], ACT.Copy).then_inc(aT_hi_done, 1)

            def iteration(n, prep, front, score, soft, tail):
                m, s, t = n.ahead(2), n.ahead(1), n.ahead(-1)
                for slot in range(SLOTS):
                    if soft and 0 <= slot - PROB_LAG < PROB_UNITS:
                        exp_unit(n, slot - PROB_LAG)
                    if soft and slot in (13, 21, 29, 37):
                        copy_mixed(n, (slot - 13) // 8)
                    if tail and slot in (5, 22):
                        tail_hi(t, slot // 22)
                    if front:
                        if slot in (1, 2):
                            front_x_hi(m, slot - 1)
                        if slot in (10, 12):
                            front_q_hi(m, slot - 10)
                            front_q_hi(m, slot - 9)
                        if slot == 14:
                            front_kv(m)
                        if slot == 16:
                            front_v(m)
                    if score and slot == 35:
                        stack_maxima(s)

            pipeline(iteration, act)

        @block.vector
        def _(dve):
            dve.memset(q_stack[0][:].bitcast(F32), 0.0).then_inc(dve_setup, 1)
            dve.memset(q_stack[1][:].bitcast(F32), 0.0).then_inc(dve_setup, 1)
            dve.wait_ge(act_setup, 4)
            dve.tensor_tensor(wqkv_lo[:].rearrange("p a b -> p (a b)"), probs[:, 0:6, :].rearrange("p a b -> p (a b)"),
                              wqkv_hi[:].rearrange("p a b -> p (a b)").bitcast(F32), ALU.subtract).then_inc(dve_setup, 1)
            dve.tensor_tensor(wo_lo[:].rearrange("p a b -> p (a b)"), mixed[0][:].rearrange("p a b -> p (a b)"),
                              wo_hi[:].rearrange("p a b -> p (a b)").bitcast(F32), ALU.subtract).then_inc(dve_setup, 1)

            def norm_step(k, which, x, out_, step, index):
                stats, mv, var = ln_stats[:, which], ln_mv[:, which], ln_var[:, which]
                y, t = ln_y[:, which], ln_t[:, which]
                wait_alone(dve, dve_setup, step, NORM_STEPS * index + k)
                if k < 2:
                    ins = dve.bn_stats(stats[:, k, :], x[:, k, :])
                elif k < 4:
                    ins = dve.bn_aggr(mv[:, k - 2, :], stats[:, k - 2, :])
                elif k == 4:
                    ins = dve.tensor_scalar(var, mv[:, :, 1], EPS, None, ALU.add)
                elif k == 5:
                    ins = dve.tensor_scalar(t.bitcast(I32), var.bitcast(I32), 1, None, ALU.logical_shift_right)
                elif k == 6:
                    ins = dve.tensor_scalar(y.bitcast(I32), t.bitcast(I32), -1.0, RSQRT_MAGIC, ALU.mult, ALU.add)
                elif k < 16:
                    if k % 3 == 1:
                        ins = dve.scalar_tensor_tensor(t, y, -0.5, y, ALU.mult, ALU.mult)
                    elif k % 3 == 2:
                        ins = dve.tensor_tensor(t, t, var, ALU.mult)
                    else:
                        ins = dve.scalar_tensor_tensor(y, t, 1.5, y, ALU.add, ALU.mult)
                else:
                    c = k - 16
                    ins = dve.tensor_scalar(out_[:, c, :], x[:, c, :], mv[:, c, 0:1], y[:, c:c + 1], ALU.subtract, ALU.mult)
                ins.then_inc(step, 1)

            def prep_norm(m, k):
                if k == 0:
                    at_least(dve, x_in, 16 * (m.index + 1))
                if k == 16:
                    at_least(dve, front_done, 6 * (m.index - 1) + 2)
                norm_step(k, 0, xt, xn, ln1_step, m.index)

            def front_x_lo(m, f):
                at_least(dve, xT_hi_done, 2 * m.index + f + 1)
                dve.tensor_tensor(xT_lo[:, 2 * f:2 * f + 2, :].rearrange("p a b -> p (a b)"), front_bank[f][:],
                                  xT_hi[:, 2 * f:2 * f + 2, :].rearrange("p a b -> p (a b)").bitcast(F32),
                                  ALU.subtract).then_inc(xT_lo_done, 1)

            def front_q_lo(m, r):
                at_least(dve, q_hi_done, R * m.index + 2 * (r // 2) + 2)
                dve.scalar_tensor_tensor(q_lo[:, r, :], front_bank[r // 2][:, (r % 2) * S:(r % 2 + 1) * S],
                                         bq[:, r:r + 1], q_hi[:, r, :].bitcast(F32), ALU.add,
                                         ALU.subtract).then_inc(q_lo_done, 1)

            def front_k_lo(m):
                at_least(dve, kv_copied, 4 * (m.index + 1))
                for g2 in range(2):
                    dve.scalar_tensor_tensor(k_lo[:, g2, :], k_raw[:], parity[:, g2:g2 + 1], k_hi[:, g2, :].bitcast(F32),
                                             ALU.mult, ALU.subtract).then_inc(k_lo_done, 1)

            def maxima_unit(m, u):
                gp, r, c = u // (R * QC), u // QC % R, u % QC
                if u == 0:
                    at_least(dve, mask_done, m.index + 1)
                    at_least(dve, max_split, 2 * m.index)
                wait_alone(dve, dve_setup, scores_done, SCORE_UNITS * m.index + u + 1)
                bank = score_bank[(m.parity + u) % 2]
                for g2 in range(2):
                    head = g2 * H // 2 + gp * R + r
                    last = dve.tensor_tensor_reduce(out=bank[:, g2, :], in0=bank[:, g2, :], in1=mask[m.parity][:, c, :],
                                                    scale=1.0, scalar=-3e38, op0=ALU.add, op1=ALU.max,
                                                    accum_out=row_max[:, c, head:head + 1])
                last.then_inc(maxima_done, 1)

            def split_maxima(m):
                at_least(dve, maxima_done, SCORE_UNITS * (m.index + 1))
                at_least(dve, maxT_done, m.index)
                maxima = row_max[:].rearrange("p c (a h) -> p c a h", a=2)
                dve.tensor_scalar(neg_max[:, :, :, 0, :], maxima, -1.0, None, ALU.mult).then_inc(max_split, 1)
                at_least(dve, max_split, 2 * m.index + 1)
                dve.scalar_tensor_tensor(neg_max[:, :, :, 1, :], maxima, -1.0, neg_max[:, :, :, 0, :].bitcast(F32),
                                         ALU.mult, ALU.subtract).then_inc(max_split, 1)

            def tail_normalize(t, c, gg):
                done = 12 * t.index + 6 * c + 2 * gg
                at_least(dve, tail_done, 8 * t.index + 4 * c + gg + 1)
                at_least(dve, tail_step, done)
                heads = tail_bank[:].rearrange("p (h w) -> p h w", w=2 * HD)
                sums = inv_sum[:].rearrange("p r j -> p (r j)")
                dve.reciprocal(sums, heads[:, :, HD]).then_inc(tail_step, 1)
                at_least(dve, tail_step, done + 1)
                dve.tensor_tensor(attn[:, c, gg * S:(gg + 1) * S].rearrange("p (h w) -> p h w", w=HD),
                                  heads[:, :, 0:HD], sums.unsqueeze(2).to_broadcast([P, H // 2, HD]),
                                  ALU.mult).then_inc(tail_step, 1)

            def tail_lo(t, c):
                at_least(dve, aT_hi_done, 2 * t.index + c + 1)
                dve.tensor_tensor(aT_lo[:].rearrange("p k q -> p (k q)"), tail_bank[:],
                                  aT_hi[:].rearrange("p k q -> p (k q)").bitcast(F32),
                                  ALU.subtract).then_inc(tail_step, 1)

            def tail_residual(t, c):
                at_least(dve, tail_done, 8 * t.index + 4 * c + 4)
                if c == 0:
                    at_least(dve, res_done, t.index + 1)
                    at_least(dve, x2_out, 16 * t.index)
                    at_least(dve, ln2_step, NORM_STEPS * t.index)
                dve.scalar_tensor_tensor(x2[:, c, :], tail_bank[:], tanh_gate[:, 0:1], x_res[:, c, :], ALU.mult,
                                         ALU.add).then_inc(tail_step, 1)

            def tail_norm(t, k):
                if k == 0:
                    at_least(dve, tail_step, 12 * (t.index + 1))
                if k == 16:
                    at_least(dve, xn2_out, 16 * t.index)
                norm_step(k, 1, x2, xn2, ln2_step, t.index)

            NORM_SLOTS = [(0, 1), (2, 3, 4), (5, 6, 7), (8, 9, 10), (11, 12, 13), (14, 15), (16,), (17,)]

            def iteration(n, prep, front, score, soft, tail):
                after, m, s, t = n.ahead(3), n.ahead(2), n.ahead(1), n.ahead(-1)
                for slot in range(SLOTS):
                    if score and slot < SCORE_UNITS:
                        maxima_unit(s, slot)
                    if front:
                        if slot in (2, 3):
                            front_x_lo(m, slot - 2)
                        if slot in (10, 12):
                            front_q_lo(m, slot - 10)
                            front_q_lo(m, slot - 9)
                        if slot == 15:
                            front_k_lo(m)
                    if tail:
                        for c in range(QC):
                            if slot == 17 * c + 1:
                                tail_normalize(t, c, 0)
                            if slot == 17 * c + 3:
                                tail_normalize(t, c, 1)
                            if slot == 17 * c + 5:
                                tail_lo(t, c)
                            if slot == 17 * c + 8:
                                tail_residual(t, c)
                        if 26 <= slot < 34:
                            for k in NORM_SLOTS[slot - 26]:
                                tail_norm(t, k)
                    if prep and 16 <= slot < 24:
                        for k in NORM_SLOTS[slot - 16]:
                            prep_norm(after, k)
                    if score and slot == 32:
                        split_maxima(s)

            pipeline(iteration, dve)


NE, TOP, FE = 8, 2, 352
PAIRS = NE // 2
NT = T // P
GATE_W = FE + NE
UP_AT = KC * GATE_W
DOWN_AT = UP_AT + KC * FE
FC = -(-FE // P)
WW = DOWN_AT + FC * D
LO_CUT = WW * 5 // 8
SHARED = 2
ROUTED_TILES = T * TOP // P + NE - 1
FIRST_ROUTED = SHARED * NT
STEPS = FIRST_ROUTED + ROUTED_TILES
SLOT_ROWS = ROUTED_TILES * P
C_TRI = P
C_TRI4 = C_TRI + NE * NE
C_FULL = C_TRI4 + PAIRS * PAIRS
C_TILE = C_FULL + NT - 1
C_TOK = C_TILE + ROUTED_TILES + 2
CONSTS = C_TOK + NT


CHOSEN_STEP = 19
ROUTE_STEPS = 65


class Step:

    def __init__(self, pair, parity):
        self.pair, self.parity = pair, parity
        self.index = 2 * pair + parity

    def ahead(self, k):
        return Step(self.pair + (self.parity + k) // 2, (self.parity + k) % 2)


def at_step(number):
    return Step(number // 2, number % 2)


def expert_phase(nc, A, x2_buf, xn_buf, out, semaphores):
    with ExitStack() as ctx:
        def sb(name, shape, dt=F32):
            return ctx.enter_context(nc.sbuf_tensor(name, shape, dt))

        def ps(name, shape):
            return ctx.enter_context(nc.psum_tensor(name, shape, F32))

        def sem(name):
            return semaphores.enter_context(nc.semaphore(name))

        row_table = nc.dram_tensor("row_table", (SLOT_ROWS, 2), I32, kind="Internal").ap()

        ident = sb("ident", [P, P])
        ones_mat = sb("ones_mat", [P, P])
        consts = sb("consts", [P, CONSTS])
        tanh_ffn = sb("tanh_ffn", [P, 1])
        zero_rows = sb("zero_rows", [P, D])
        w_raw = sb("w_raw", [P, 2, WW])
        w_hi = sb("w_hi", [P, 2 * WW], F32R)
        w_lo = sb("w_lo", [P, 2 * WW], F32R)
        base = sb("base", [P, NT, D])
        x_tile = [sb(f"x_tile{i}", [P, D]) for i in range(2)]
        xt_hi = [sb(f"xt_hi{i}", [P, KC, P], F32R) for i in range(2)]
        xt_lo = [sb(f"xt_lo{i}", [P, KC, P], F32R) for i in range(2)]
        silu = [sb(f"silu{i}", [P, FE]) for i in range(2)]
        h = sb("h", [P, FC * P])
        h_hi = sb("h_hi", [P, FC, P], F32R)
        h_lo = sb("h_lo", [P, FC, P], F32R)
        y = [sb(f"y{i}", [P, D]) for i in range(2)]
        logits = sb("logits", [P, NT, NE])
        score = sb("score", [P, NT, NE])
        stat = sb("stat", [P, NT])
        inv = sb("inv", [P, NT])
        best = sb("best", [P, NT, PAIRS])
        group_gt = sb("group_gt", [P, NT, PAIRS, PAIRS])
        group_eq = sb("group_eq", [P, NT, PAIRS, PAIRS])
        rank = sb("rank", [P, NT, NE])
        gt = sb("gt", [P, NT, NE, NE])
        eq = sb("eq", [P, NT, NE, NE])
        chosen = sb("chosen", [P, NT, NE])
        weight = sb("weight", [P, NT, NE])
        place = sb("place", [P, NT, NE])
        count = sb("count", [P, NE])
        full = sb("full", [P, NE, NT - 1])
        tiles = sb("tiles", [P, NE])
        before = sb("before", [P, NE, NE])
        start = sb("start", [P, NE])
        end = sb("end", [P, NE])
        slot = sb("slot", [P, TOP, NT])
        row = sb("row", [P, NT, 3, TOP], I32)
        expert_gt = sb("expert_gt", [P, ROUTED_TILES + 2, NE])
        expert = sb("expert", [P, ROUTED_TILES + 2])
        free_f = sb("free_f", [P, ROUTED_TILES + 2])
        parity_f = sb("parity_f", [P, ROUTED_TILES + 2])
        t_load = sb("t_load", [P, ROUTED_TILES + 2], I32)
        t_place = sb("t_place", [P, ROUTED_TILES + 2], I32)
        t_new = sb("t_new", [P, ROUTED_TILES + 2], I32)
        t_free = sb("t_free", [P, ROUTED_TILES + 2], I32)
        row_now = sb("row_now", [P, 4, 3, TOP], I32)
        table = sb("table", [P, ROUTED_TILES, 2], I32)
        gather_idx = [sb(f"gather_idx{i}", [P, 1], I32) for i in range(2)]
        add_idx = [sb(f"add_idx{i}", [P, 1], I32) for i in range(2)]

        gate_bank = [ps(f"gate_bank{i}", [P, 512]) for i in range(2)]
        up_bank = [ps(f"up_bank{i}", [P, 512]) for i in range(2)]
        xt_bank = ps("xt_bank", [P, 512])
        ht_bank = ps("ht_bank", [P, 512])
        y_bank = [ps(f"y_bank{i}", [P, 512]) for i in range(2)]

        const_in, base_in, raw_in = sem("const_in"), sem("base_in"), sem("raw_in")
        tile_in = [sem("tile_in_a"), sem("tile_in_b")]
        gathered = [sem("gathered_a"), sem("gathered_b")]
        pads_out, shared_out = sem("pads_out"), sem("shared_out")
        table_set, scattered, table_in, added = sem("table_set"), sem("scattered"), sem("table_in"), sem("added")
        b_setup, h_padded, tanh_done = sem("b_setup"), sem("h_padded"), sem("tanh_done")
        route_step, exp_scores, counted = sem("route_step"), sem("exp_scores"), sem("counted")
        row_copied, idx_copied = sem("row_copied"), sem("idx_copied")
        w_hi_done, w_lo_dve, w_lo_pool = sem("w_hi_done"), sem("w_lo_dve"), sem("w_lo_pool")
        gate_done, up_done, xt_done, ht_done, down_done = (
            sem("gate_done"), sem("up_done"), sem("xt_done"), sem("ht_done"), sem("down_done"))
        silu_done, xt_hi_done, h_hi_done, logits_copied = (
            sem("silu_done"), sem("xt_hi_done"), sem("h_hi_done"), sem("logits_copied"))
        xt_lo_done, h_done, h_lo_done, y_done = sem("xt_lo_done"), sem("h_done"), sem("h_lo_done"), sem("y_done")

        block = ctx.enter_context(nc.Block())

        def tile_rows(buf, t):
            return buf[bass.ds(P * t, P), :]

        def step_loop(eng, first, last, body):
            with eng.Fori(0, (last - first + 1) // 2) as pair:
                for k in range(2):
                    body(Step(pair + (first + k) // 2, (first + k) % 2))

        def table_value(eng, tab, s, ahead, hi):
            t = s.index + ahead - FIRST_ROUTED
            return eng.value_load(tab[0:1, bass.ds(t, 1)], min_val=0, max_val=hi)

        @block.sync
        def _(sp):
            def load_weights(j):
                wait_alone(sp, b_setup, raw_in, 16 * j)
                wait_alone(sp, b_setup, w_lo_dve, j - 1)
                wait_alone(sp, b_setup, w_lo_pool, j - 1)

            def weights_dma(j, place):
                sp.dma_start(w_raw[:, place, :], A["experts"][j]).then_inc(raw_in, 16)

            def load_tile(s, t):
                sp.dma_start(x_tile[s.parity][:], tile_rows(xn_buf, t)).then_inc(tile_in[s.parity], 16)

            weights_dma(0, 0)
            for k in range(2):
                load_tile(at_step(k), k)
            sp.dma_start(base[:], x2_buf.rearrange("(t p) d -> p t d", p=P)).then_inc(base_in, 16)
            load_weights(1)
            weights_dma(1, 1)

            def first_half(s):
                wait_alone(sp, b_setup, xt_done, s.index + 1)
                load_tile(s, (s.index + 2) % NT if isinstance(s.index, int) else s.index + 2)

            def store_shared(t):
                sp.dma_start(tile_rows(out, t), base[:, bass.ds(t, 1), :].rearrange("p o d -> p (o d)")).then_inc(shared_out, 16)

            def second_half(s):
                wait_alone(sp, b_setup, xt_done, s.index + 1)
                load_tile(s, s.index + 2 - NT)

            for s in range(2):
                first_half(at_step(s))
            load_weights(2)
            weights_dma(2, 0)
            step_loop(sp, 2, NT - 3, first_half)
            first_half(at_step(NT - 2))
            first_half(at_step(NT - 1))
            load_weights(3)
            weights_dma(3, 1)

            def second_and_store(s):
                second_half(s)
                wait_alone(sp, b_setup, y_done, s.index)
                store_shared(s.index - 1 - NT)

            second_half(at_step(NT))
            second_and_store(at_step(NT + 1))
            step_loop(sp, NT + 2, 2 * NT - 3, second_and_store)
            for t in range(NT - 3, NT):
                sp.wait_ge(y_done, NT + t + 1)
                store_shared(t)
            with sp.Fori(2, SHARED // 2 + NE // 2) as pair:
                for k in range(2):
                    load_weights(2 * pair + k)
                    sp.dma_start(w_raw[:, k, :], A["experts"][bass.ds(2 * pair + k, 1)].rearrange(
                        "o p w -> (o p) w")).then_inc(raw_in, 16)
            sp.wait_ge(shared_out, 16 * NT)

        @block.gpsimd
        def _(pool):
            pool.dma_start(consts[:], A["consts"]).then_inc(const_in, 16)
            pool.dma_start(tanh_ffn[:], A["g_ffn"].partition_broadcast(P)).then_inc(const_in, 16)
            pool.dma_start(row_table, A["no_rows"]).then_inc(table_set, 16)
            pool.memset(ident[:], 0.0).then_inc(b_setup, 1)
            pool.memset(ones_mat[:], 1.0).then_inc(b_setup, 1)
            pool.memset(zero_rows[:], 0.0).then_inc(b_setup, 1)
            pool.wait_ge(b_setup, 3)
            pool.affine_select(out=ident[:], in_=ident[:], compare_op=ALU.not_equal, fill=1.0, base=0,
                               pattern=[[-1, P]], channel_multiplier=1).then_inc(b_setup, 1)
            pool.dma_start(xn_buf[T:T + P, :], zero_rows[:]).then_inc(pads_out, 16)
            pool.dma_start(out[T:T + P, :], zero_rows[:]).then_inc(added, 16)

            def split_words(place, raw):
                pool.tensor_tensor(w_lo[:, bass.ds(place + LO_CUT, WW - LO_CUT)], raw[:, LO_CUT:WW],
                                   w_hi[:, bass.ds(place + LO_CUT, WW - LO_CUT)].bitcast(F32),
                                   ALU.subtract).then_inc(w_lo_pool, 1)

            for j in range(3):
                pool.wait_ge(w_hi_done, j + 1)
                split_words(j % 2 * WW, w_raw[:, j % 2, :])

            pool.wait_ge(table_set, 16)
            pool.wait_ge(route_step, ROUTE_STEPS)
            with pool.Fori(0, NT // 4) as four:
                wait_alone(pool, b_setup, scattered, 16 * 8 * four)
                pool.tensor_copy(row_now[:], row[:, bass.ds(4 * four, 4)]).then_inc(row_copied, 1)
                wait_alone(pool, b_setup, row_copied, four + 1)
                for t in range(4):
                    for k in range(TOP):
                        pool.indirect_dma_start(
                            out=row_table, out_offset=bass.IndirectOffsetOnAxis(ap=row_now[:, t, 0, k:k + 1], axis=0),
                            in_=row_now[:, t, k + 1, :], in_offset=None).then_inc(scattered, 16)
            pool.wait_ge(scattered, 16 * TOP * NT)
            pool.dma_start(table[:], row_table.rearrange("(t p) w -> p t w", p=P)).then_inc(table_in, 16)
            pool.wait_ge(table_in, 16)
            pool.wait_ge(pads_out, 16)

            def copy_index(dst, tile_number, turn):
                pool.tensor_copy(dst[:], table[:, bass.ds(tile_number, 1), 0]).then_inc(idx_copied, 1)
                wait_alone(pool, b_setup, idx_copied, turn)

            def gather(s, ahead, turn):
                at_least(pool, xt_done, s.index + ahead - 1)
                t = s.index + ahead - FIRST_ROUTED
                p = (s.parity + ahead) % 2
                copy_index(gather_idx[p], t, turn)
                pool.indirect_dma_start(out=x_tile[p][:], out_offset=None, in_=xn_buf,
                                        in_offset=bass.IndirectOffsetOnAxis(ap=gather_idx[p][:, :1], axis=0)
                                        ).then_inc(gathered[p], 16)

            def add_rows(s, turn):
                p = (s.parity + 1) % 2
                t = s.index - 1 - FIRST_ROUTED
                at_least(pool, added, 16 * t + 16)
                copy_index(add_idx[p], t, turn)
                wait_alone(pool, b_setup, y_done, s.index)
                pool.indirect_dma_start(out=out, out_offset=bass.IndirectOffsetOnAxis(ap=add_idx[p][:, :1], axis=0),
                                        in_=y[p][:], in_offset=None, compute_op=ALU.add).then_inc(added, 16)

            def split_new(s):
                new = table_value(pool, t_new, s, 2, 1)
                with pool.If(new > 0):
                    count_ = table_value(pool, t_load, s, 2, SHARED + NE)
                    place = table_value(pool, t_place, s, 2, WW)
                    pool.wait_ge(w_hi_done, count_)
                    pool.tensor_tensor(w_lo[:, bass.ds(place + LO_CUT, WW - LO_CUT)],
                                       w_raw[:].rearrange("p a w -> p (a w)")[:, bass.ds(place + LO_CUT, WW - LO_CUT)],
                                       w_hi[:, bass.ds(place + LO_CUT, WW - LO_CUT)].bitcast(F32),
                                       ALU.subtract).then_inc(w_lo_pool, 1)

            R0 = FIRST_ROUTED
            gather(at_step(R0 - 2), 2, 1)
            gather(at_step(R0 - 1), 2, 2)
            split_new(at_step(R0 - 1))
            gather(at_step(R0), 2, 3)
            split_new(at_step(R0))
            pool.wait_ge(shared_out, 16 * NT)

            def step(s):
                turn = 2 * (s.index - R0 - 1) + 4
                gather(s, 2, turn)
                add_rows(s, turn + 1)
                split_new(s)

            step_loop(pool, R0 + 1, STEPS - 3, step)
            turn = 2 * (STEPS - 2 - R0 - 1) + 4
            for k in range(3):
                add_rows(at_step(STEPS - 2 + k), turn + k)
            pool.wait_ge(added, 16 * (ROUTED_TILES + 1))

        @block.tensor
        def _(pe):
            pe.wait_ge(b_setup, 4)

            def products(out_, left, right):
                n = len(left)
                for c in range(n):
                    for k, (a, b) in enumerate([(0, 0), (1, 0), (0, 1)]):
                        last = pe.matmul(out_, left[c][a], right[c][b], start=c == 0 and k == 0,
                                         stop=c == n - 1 and k == 2)
                return last

            def weight_parts(place, at, n):
                return w_hi[:, bass.ds(place + at, n)], w_lo[:, bass.ds(place + at, n)]

            def gate_up(s, place, gate_w, loads):
                if loads is not None:
                    pe.wait_ge(w_lo_dve, loads)
                    pe.wait_ge(w_lo_pool, loads)
                pe.wait_ge(xt_lo_done, s.index + 1)
                at_least(pe, h_done, s.index - 1)
                left = [(xt_hi[s.parity][:, c, :], xt_lo[s.parity][:, c, :]) for c in range(KC)]
                products(gate_bank[s.parity][:, 0:gate_w], left,
                         [weight_parts(place, c * GATE_W, gate_w) for c in range(KC)]).then_inc(gate_done, 1)
                products(up_bank[s.parity][:, 0:FE], left,
                         [weight_parts(place, UP_AT + c * FE, FE) for c in range(KC)]).then_inc(up_done, 1)

            def transpose_x(s, gather):
                if gather:
                    at_least(pe, gathered[s.parity], 16 * (s.pair - NT + 1))
                else:
                    at_least(pe, tile_in[s.parity], 16 * (s.pair + 1))
                at_least(pe, xt_lo_done, s.index)
                for c in range(KC):
                    last = pe.transpose(xt_bank[:, c * P:(c + 1) * P], x_tile[s.parity][:, c * P:(c + 1) * P], ident[:])
                last.then_inc(xt_done, 1)

            def transpose_h(s):
                pe.wait_ge(h_done, s.index + 1)
                at_least(pe, h_lo_done, s.index)
                for c in range(FC):
                    last = pe.transpose(ht_bank[:, c * P:(c + 1) * P], h[:, c * P:(c + 1) * P], ident[:])
                last.then_inc(ht_done, 1)

            def down(s, place):
                pe.wait_ge(h_lo_done, s.index + 1)
                at_least(pe, y_done, s.index - 1)
                products(y_bank[s.parity][:], [(h_hi[:, c, :], h_lo[:, c, :]) for c in range(FC)],
                         [weight_parts(place, DOWN_AT + c * D, D) for c in range(FC)]).then_inc(down_done, 1)

            def step(s, place, place_before, gate_w=FE, loads=None, gather=False, first=False, last=False):
                gate_up(s, place, gate_w, loads)
                if not last:
                    transpose_x(s.ahead(1), gather)
                if not first:
                    down(s.ahead(-1), place_before)
                transpose_h(s)

            def routed(s, last=False):
                loads = table_value(pe, t_load, s, 0, SHARED + NE)
                place = table_value(pe, t_place, s, 0, WW)
                place_before = table_value(pe, t_place, s, -1, WW)
                step(s, place, place_before, loads=loads, gather=True, last=last)

            transpose_x(at_step(0), False)
            step(at_step(0), 0, 0, GATE_W, 1, first=True)
            for s in (1, 2):
                step(at_step(s), 0, 0, GATE_W)
            step_loop(pe, 3, NT - 2, lambda s: step(s, 0, 0, GATE_W))
            step(at_step(NT - 1), 0, 0, GATE_W)
            step(at_step(NT), WW, 0, loads=2)

            pe.wait_ge(route_step, CHOSEN_STEP)
            ranks = ht_bank[:, 0:NT * NE]
            flat = chosen[:].rearrange("p t e -> p (t e)")
            pe.matmul(ranks, consts[:, 0:P], flat, start=True, stop=False, skip_group_check=True)
            for t in range(NT - 1):
                n = NT - 1 - t
                pe.matmul(ht_bank[:, (t + 1) * NE:NT * NE].rearrange("p (t e) -> p t e", e=NE), ones_mat[:],
                          chosen[:, t:t + 1, :].to_broadcast([P, n, NE]), start=False, stop=t == NT - 2,
                          skip_group_check=True)
            for t in range(NT):
                last = pe.matmul(ht_bank[:, NT * NE:NT * NE + NE], ones_mat[:], chosen[:, t, :], start=t == 0,
                                 stop=t == NT - 1, skip_group_check=True)
            last.then_inc(counted, 1)

            step_loop(pe, NT + 1, 2 * NT - 2, lambda s: step(s, WW, WW))
            pe.wait_ge(route_step, ROUTE_STEPS)
            step(at_step(2 * NT - 1), WW, WW, gather=True)
            s = at_step(FIRST_ROUTED)
            step(s, 0, WW, loads=SHARED + 1, gather=True)
            step_loop(pe, FIRST_ROUTED + 1, STEPS - 3, routed)
            routed(at_step(STEPS - 2))
            routed(at_step(STEPS - 1), last=True)
            place = pe.value_load(t_place[0:1, ROUTED_TILES - 1:ROUTED_TILES], min_val=0, max_val=WW)
            down(at_step(STEPS - 1), place)

        @block.scalar
        def _(act):
            act.wait_ge(const_in, 32)
            act.activation(tanh_ffn[:], tanh_ffn[:], ACT.Tanh).then_inc(tanh_done, 1)

            def split(j):
                act.wait_ge(raw_in, 16 * (j + 1))
                act.activation(w_hi[:, j % 2 * WW:(j % 2 + 1) * WW], w_raw[:, j % 2, :], ACT.Copy).then_inc(w_hi_done, 1)

            def x_hi(s):
                act.wait_ge(xt_done, s.index + 1)
                at_least(act, up_done, s.index - 1)
                act.activation(xt_hi[s.parity][:].rearrange("p c q -> p (c q)"), xt_bank[:], ACT.Copy).then_inc(xt_hi_done, 1)

            def gate(s, with_logits):
                act.wait_ge(gate_done, s.index + 1)
                if with_logits:
                    act.activation(logits[:, bass.ds(s.index, 1), :].rearrange("p o e -> p (o e)"),
                                   gate_bank[s.parity][:, FE:GATE_W], ACT.Copy).then_inc(logits_copied, 1)
                at_least(act, h_done, s.index - 1)
                act.activation(silu[s.parity][:], gate_bank[s.parity][:, 0:FE], ACT.Silu).then_inc(silu_done, 1)

            def hidden_hi(s):
                act.wait_ge(ht_done, s.index + 1)
                at_least(act, down_done, s.index)
                act.activation(h_hi[:].rearrange("p c q -> p (c q)"), ht_bank[:, 0:FC * P], ACT.Copy).then_inc(h_hi_done, 1)

            def split_new(s):
                new = table_value(act, t_new, s, 2, 1)
                with act.If(new > 0):
                    count_ = table_value(act, t_load, s, 2, SHARED + NE)
                    place = table_value(act, t_place, s, 2, WW)
                    free = table_value(act, t_free, s, 2, STEPS)
                    act.wait_ge(down_done, free)
                    act.wait_ge(raw_in, 16 * count_)
                    act.activation(w_hi[:, bass.ds(place, WW)], w_raw[:].rearrange("p a w -> p (a w)")[:, bass.ds(place, WW)],
                                   ACT.Copy).then_inc(w_hi_done, 1)

            def step(s, with_logits=False, new=False, last=False):
                gate(s, with_logits)
                if not last:
                    x_hi(s.ahead(1))
                hidden_hi(s)
                if new:
                    split_new(s)

            x_hi(at_step(0))
            split(0)
            split(1)
            step(at_step(0), with_logits=True)
            step_loop(act, 1, NT - 2, lambda s: step(s, with_logits=True))
            step(at_step(NT - 1), with_logits=True)
            step(at_step(NT))
            act.wait_ge(route_step, 2)
            act.activation(score[:], score[:], ACT.Exp).then_inc(exp_scores, 1)
            act.wait_ge(down_done, NT)
            split(2)
            step_loop(act, NT + 1, 2 * NT - 2, step)
            act.wait_ge(route_step, ROUTE_STEPS)
            step(at_step(2 * NT - 1), new=True)
            step(at_step(2 * NT), new=True)
            step_loop(act, FIRST_ROUTED + 1, STEPS - 3, lambda s: step(s, new=True))
            step(at_step(STEPS - 2))
            step(at_step(STEPS - 1), last=True)

        @block.vector
        def _(dve):
            dve.memset(h[:, FE:FC * P], 0.0).then_inc(h_padded, 1)

            def split(j):
                dve.wait_ge(w_hi_done, j + 1)
                at = j % 2 * WW
                dve.tensor_tensor(w_lo[:, at:at + LO_CUT], w_raw[:, j % 2, 0:LO_CUT],
                                  w_hi[:, at:at + LO_CUT].bitcast(F32), ALU.subtract).then_inc(w_lo_dve, 1)

            def split_new(s):
                new = table_value(dve, t_new, s, 2, 1)
                with dve.If(new > 0):
                    count_ = table_value(dve, t_load, s, 2, SHARED + NE)
                    place = table_value(dve, t_place, s, 2, WW)
                    dve.wait_ge(w_hi_done, count_)
                    dve.tensor_tensor(w_lo[:, bass.ds(place, LO_CUT)],
                                      w_raw[:].rearrange("p a w -> p (a w)")[:, bass.ds(place, LO_CUT)],
                                      w_hi[:, bass.ds(place, LO_CUT)].bitcast(F32), ALU.subtract).then_inc(w_lo_dve, 1)

            def x_lo(s):
                dve.wait_ge(xt_hi_done, s.index + 1)
                dve.tensor_tensor(xt_lo[s.parity][:].rearrange("p c q -> p (c q)"), xt_bank[:],
                                  xt_hi[s.parity][:].rearrange("p c q -> p (c q)").bitcast(F32),
                                  ALU.subtract).then_inc(xt_lo_done, 1)

            def hidden(s):
                dve.wait_ge(silu_done, s.index + 1)
                dve.wait_ge(up_done, s.index + 1)
                at_least(dve, ht_done, s.index)
                dve.tensor_tensor(h[:, 0:FE], up_bank[s.parity][:, 0:FE], silu[s.parity][:], ALU.mult).then_inc(h_done, 1)

            def hidden_lo(s):
                dve.wait_ge(h_hi_done, s.index + 1)
                dve.tensor_tensor(h_lo[:].rearrange("p c q -> p (c q)"), ht_bank[:, 0:FC * P],
                                  h_hi[:].rearrange("p c q -> p (c q)").bitcast(F32), ALU.subtract).then_inc(h_lo_done, 1)

            def shared_y(s, t, second):
                dve.wait_ge(down_done, s.index + 1)
                if second:
                    at_least(dve, y_done, s.index + 1 - NT)
                rows = base[:, bass.ds(t, 1), :].rearrange("p o d -> p (o d)")
                dve.scalar_tensor_tensor(rows, y_bank[s.parity][:], tanh_ffn[:, 0:1], rows, ALU.mult, ALU.add).then_inc(y_done, 1)

            def routed_y(s):
                dve.wait_ge(down_done, s.index + 1)
                at_least(dve, added, 16 * (s.index - FIRST_ROUTED))
                t = s.index - FIRST_ROUTED
                dve.tensor_scalar(y[s.parity][:], y_bank[s.parity][:], table[:, bass.ds(t, 1), 1].bitcast(F32), None,
                                  ALU.mult).then_inc(y_done, 1)

            def step(s, finish_before, new=False, last=False):
                hidden(s)
                if not last:
                    x_lo(s.ahead(1))
                if finish_before is not None:
                    finish_before(s.ahead(-1))
                hidden_lo(s)
                if new:
                    split_new(s)

            def route():
                done = 0

                def then(ins):
                    nonlocal done
                    ins.then_inc(route_step, 1)
                    done += 1
                    dve.wait_ge(route_step, done)

                def tri(at, n):
                    return consts[:, at:at + n * n].rearrange("p (i j) -> p i j", i=n).unsqueeze(1).to_broadcast([P, NT, n, n])

                dve.wait_ge(logits_copied, NT)
                then(dve.tensor_reduce(stat[:], logits[:], AX.X, ALU.max))
                then(dve.tensor_tensor(score[:], logits[:], stat[:].unsqueeze(2).to_broadcast([P, NT, NE]), ALU.subtract))
                dve.wait_ge(exp_scores, 1)
                then(dve.tensor_reduce(stat[:], score[:], AX.X, ALU.add))
                then(dve.reciprocal(inv[:], stat[:]))
                then(dve.tensor_tensor(score[:], score[:], inv[:].unsqueeze(2).to_broadcast([P, NT, NE]), ALU.mult))
                pairs = score[:].rearrange("p t (g e) -> p t g e", e=2)
                then(dve.tensor_tensor(best[:], pairs[:, :, :, 0], pairs[:, :, :, 1], ALU.max))
                shape = [P, NT, PAIRS, PAIRS]
                mine, other = best[:].unsqueeze(3).to_broadcast(shape), best[:].unsqueeze(2).to_broadcast(shape)
                then(dve.tensor_tensor(group_gt[:], other, mine, ALU.is_gt))
                then(dve.tensor_tensor(group_eq[:], other, mine, ALU.is_equal))
                then(dve.tensor_tensor(group_eq[:], group_eq[:], tri(C_TRI4, PAIRS), ALU.mult))
                then(dve.tensor_tensor(group_gt[:], group_gt[:], group_eq[:], ALU.add))
                then(dve.tensor_reduce(best[:], group_gt[:], AX.X, ALU.add))
                then(dve.tensor_scalar(best[:], best[:], float(TOP), None, ALU.is_lt))
                then(dve.tensor_tensor(pairs, pairs, best[:].unsqueeze(3).to_broadcast([P, NT, PAIRS, 2]), ALU.mult))
                shape = [P, NT, NE, NE]
                mine, other = score[:].unsqueeze(3).to_broadcast(shape), score[:].unsqueeze(2).to_broadcast(shape)
                then(dve.tensor_tensor(gt[:], other, mine, ALU.is_gt))
                then(dve.tensor_tensor(eq[:], other, mine, ALU.is_equal))
                then(dve.tensor_tensor(eq[:], eq[:], tri(C_TRI, NE), ALU.mult))
                then(dve.tensor_tensor(gt[:], gt[:], eq[:], ALU.add))
                then(dve.tensor_reduce(rank[:], gt[:], AX.X, ALU.add))
                then(dve.tensor_scalar(chosen[:], rank[:], float(TOP), None, ALU.is_lt))
                assert done == CHOSEN_STEP
                then(dve.scalar_tensor_tensor(weight[:], score[:], tanh_ffn[:, 0:1], chosen[:], ALU.mult, ALU.mult))
                dve.wait_ge(counted, 1)
                then(dve.tensor_copy(count[:], ht_bank[:, NT * NE:NT * NE + NE]))
                shape = [P, NE, NT - 1]
                then(dve.tensor_tensor(full[:], count[:].unsqueeze(2).to_broadcast(shape),
                                       consts[:, C_FULL:C_FULL + NT - 1].unsqueeze(1).to_broadcast(shape), ALU.is_gt))
                then(dve.tensor_reduce(tiles[:], full[:], AX.X, ALU.add))
                then(dve.tensor_scalar(tiles[:], tiles[:], 1.0, None, ALU.add))
                then(dve.tensor_tensor(before[:], tiles[:].unsqueeze(1).to_broadcast([P, NE, NE]),
                                       consts[:, C_TRI:C_TRI + NE * NE].rearrange("p (i j) -> p i j", i=NE), ALU.mult))
                then(dve.tensor_reduce(start[:], before[:], AX.X, ALU.add))
                then(dve.tensor_tensor(end[:], start[:], tiles[:], ALU.add))
                then(dve.tensor_scalar(start[:], start[:], float(P), None, ALU.mult))
                then(dve.tensor_tensor(place[:], ht_bank[:, 0:NT * NE].rearrange("p (t e) -> p t e", e=NE),
                                       start[:].unsqueeze(1).to_broadcast([P, NT, NE]), ALU.add))
                then(dve.tensor_tensor(rank[:], place[:], chosen[:], ALU.mult))
                then(dve.tensor_reduce(slot[:, 1], rank[:], AX.X, ALU.max))
                then(dve.scalar_tensor_tensor(rank[:], place[:], -float(SLOT_ROWS), chosen[:], ALU.add, ALU.mult))
                then(dve.tensor_reduce(slot[:, 0], rank[:], AX.X, ALU.min))
                then(dve.tensor_scalar(slot[:, 0], slot[:, 0], float(SLOT_ROWS), None, ALU.add))
                for k in range(TOP):
                    then(dve.tensor_copy(row[:, :, 0, k], slot[:, k]))
                    then(dve.tensor_copy(row[:, :, 1 + k, 0], consts[:, C_TOK:C_TOK + NT]))
                    then(dve.tensor_tensor(rank[:], place[:], slot[:, k].unsqueeze(2).to_broadcast([P, NT, NE]), ALU.is_equal))
                    then(dve.tensor_tensor(rank[:], rank[:], weight[:], ALU.mult))
                    then(dve.tensor_reduce(row[:, :, 1 + k, 1].bitcast(F32), rank[:], AX.X, ALU.add))
                n = ROUTED_TILES + 2
                shape = [P, n, NE]
                tile_number = consts[:, C_TILE:C_TILE + n]
                then(dve.tensor_tensor(expert_gt[:, :, 0:NE - 1], tile_number.unsqueeze(2).to_broadcast([P, n, NE - 1]),
                                       end[:, 0:NE - 1].unsqueeze(1).to_broadcast([P, n, NE - 1]), ALU.is_ge))
                then(dve.tensor_reduce(expert[:], expert_gt[:, :, 0:NE - 1], AX.X, ALU.add))
                then(dve.tensor_scalar(t_load[:], expert[:], float(SHARED + 1), None, ALU.add))
                then(dve.tensor_scalar(parity_f[:], expert_gt[:, :, 0], float(WW), None, ALU.mult))
                for e in range(1, NE - 1):
                    then(dve.scalar_tensor_tensor(parity_f[:], expert_gt[:, :, e], float(WW if e % 2 == 0 else -WW),
                                                  parity_f[:], ALU.mult, ALU.add))
                then(dve.tensor_copy(t_place[:], parity_f[:]))
                then(dve.memset(t_new[:, 0:1], 0))
                then(dve.tensor_tensor(t_new[:, 1:n], expert[:, 1:n], expert[:, 0:n - 1], ALU.is_gt))
                then(dve.tensor_scalar(free_f[:], expert_gt[:, :, 0], float(NT), float(NT), ALU.mult, ALU.add))
                for e in range(1, NE - 1):
                    then(dve.scalar_tensor_tensor(free_f[:], expert_gt[:, :, e], tiles[:, e - 1:e], free_f[:],
                                                  ALU.mult, ALU.add))
                then(dve.tensor_copy(t_free[:], free_f[:]))
                assert done == ROUTE_STEPS, done

            def first_half(s):
                shared_y(s, s.index, False)

            def second_half(s):
                shared_y(s, s.index - NT, True)

            x_lo(at_step(0))
            split(0)
            split(1)
            dve.wait_ge(h_padded, 1)
            dve.wait_ge(base_in, 16)
            dve.wait_ge(tanh_done, 1)
            dve.wait_ge(const_in, 32)
            step(at_step(0), None)
            step_loop(dve, 1, NT - 2, lambda s: step(s, first_half))
            step(at_step(NT - 1), first_half)
            step(at_step(NT), first_half)
            route()
            split(2)
            step_loop(dve, NT + 1, 2 * NT - 2, lambda s: step(s, second_half))
            step(at_step(2 * NT - 1), second_half, new=True)
            step(at_step(2 * NT), second_half, new=True)
            dve.wait_ge(table_in, 16)
            step_loop(dve, FIRST_ROUTED + 1, STEPS - 3, lambda s: step(s, routed_y, new=True))
            step(at_step(STEPS - 2), routed_y)
            step(at_step(STEPS - 1), routed_y, last=True)
            routed_y(at_step(STEPS - 1))


def layout(i):
    import numpy as np

    def c(a):
        return np.ascontiguousarray(a)

    def wide(w):
        n = -(-w.shape[0] // P) * P
        full = np.zeros((n, w.shape[1]), np.float32)
        full[:w.shape[0]] = w
        return full.reshape(n // P, P, -1).transpose(1, 0, 2)

    def expert(gate, up, down_w, router=None):
        router = np.zeros((NE, D), np.float32) if router is None else router
        return np.concatenate([wide(np.concatenate([gate, router]).T).reshape(P, -1), wide(up.T).reshape(P, -1),
                               wide(down_w.T).reshape(P, -1)], axis=1)

    f = {}
    f["x"] = c(i["x"].reshape(T, D))
    f["ctxT"] = c(i["ctx_2048"].reshape(T, D).T)
    causal, pad = i["mask_SxS2_bc0"], i["mask_BxS2_bk0"]
    f["causal"], f["causalT"], f["pad"], f["padT"] = c(causal), c(causal.T), c(pad), c(pad.T)
    wq = i["L0_xattn_Wq"].reshape(G, R, HD, D).transpose(1, 0, 2, 3).reshape(D, D)
    f["wqkv"] = c(wide(np.concatenate([wq, i["L0_xattn_Wk"], i["L0_xattn_Wv"]]).T).reshape(P, -1))
    wo = i["L0_xattn_Wo"].T.reshape(2, G // 2, R, HD, D).transpose(0, 2, 1, 3, 4).reshape(D, D)
    f["wo"] = c(wide(wo).reshape(P, -1))
    f["bq"] = c(i["L0_xattn_bq"].reshape(G, R, HD).transpose(0, 2, 1).reshape(P, R))
    f["bk"], f["bv"] = c(i["L0_xattn_bk"].reshape(P, 1)), c(i["L0_xattn_bv"].reshape(P, 1))
    f["bo"], f["g_xattn"], f["g_ffn"] = c(i["L0_xattn_bo"]), c(i["g_xattn"]), c(i["g_ffn"])
    odd = np.arange(P) // HD % 2
    f["parity"] = c(np.stack([1 - odd, odd], 1).astype(np.float32))
    sg, su, sd = i["L0_ffn_sh_gate_w"], i["L0_ffn_sh_up_w"], i["L0_ffn_sh_down_w"]
    packed = [expert(sg[k * FE:(k + 1) * FE], su[k * FE:(k + 1) * FE], sd[:, k * FE:(k + 1) * FE],
                     i["L0_ffn_gate_weight"] if k == 0 else None) for k in range(SHARED)]
    packed += [expert(i["L0_ffn_gate_w"][e], i["L0_ffn_up_w"][e], i["L0_ffn_down_w"][e]) for e in range(NE)]
    f["experts"] = c(np.stack(packed))
    row = np.concatenate([np.tri(NE, k=-1).ravel(), np.tri(PAIRS, k=-1).ravel(), P * np.arange(1, NT),
                          np.arange(ROUTED_TILES + 2)])
    f["consts"] = c(np.concatenate([np.tri(P, k=-1).T, np.tile(row, (P, 1)),
                                    np.arange(P)[:, None] + P * np.arange(NT)[None]], axis=1).astype(np.float32))
    spare = T + np.arange(SLOT_ROWS) % P
    f["no_rows"] = c(np.stack([spare, np.zeros(SLOT_ROWS)], 1).astype(np.int32))
    return f


def kernel(**inputs):
    import numpy as np
    import concourse.bacc as bacc
    from concourse.bass_utils import run_bass_kernel_spmd

    nc = bacc.Bacc("TRN2", target_bir_lowering=False, num_devices=1)
    laid = layout({name: np.asarray(a) for name, a in inputs.items()})
    arrays, A = {}, {}
    for name, a in laid.items():
        arrays[f"in_{name}_dram"] = a
        A[name] = nc.dram_tensor(f"in_{name}_dram", a.shape, mybir.dt.from_np(a.dtype), kind="ExternalInput").ap()
    out = nc.dram_tensor("out_0_dram", (T + P, D), F32, kind="ExternalOutput").ap()
    build_kernel(nc, A, out)
    r = run_bass_kernel_spmd(nc, [arrays], core_ids=[0])
    return r.results[0]["out_0_dram"][:T].reshape(B, S, D)
```

```python
from contextlib import ExitStack

import concourse.bass as bass
from concourse import mybir

F32 = mybir.dt.float32
F32R = mybir.dt.float32r
BF16 = mybir.dt.bfloat16
I32 = mybir.dt.int32
U8 = mybir.dt.uint8
ALU = mybir.AluOpType
ACT = mybir.ActivationFunctionType
AX = mybir.AxisListType

P = 128
B, S, D = 8, 256, 512
T = B * S
QC = S // P
KC = D // P
G, R, HD = 8, 4, 16
GP = G // 2
H = G * R
PAIR = 2 * HD
AUX = 3 * PAIR
NEG = -1e30
EPS = 1e-5
RSQRT_MAGIC = float(0x5F3759DF)
NORM_STEPS = 18

SCORE_UNITS = GP * R * QC
PROB_UNITS = G * QC * R // 2
PROB_LAG = 3
PV_LAG = PROB_LAG + 5
SLOTS = PV_LAG + 4 * 7 + 2
POOL_SETUP = 13
STACK_DMAS = 13

NE, TOP, FE = 8, 2, 352
PAIRS = NE // 2
NT = T // P
GATE_W = FE + NE
UP_AT = KC * GATE_W
DOWN_AT = UP_AT + KC * FE
FC = -(-FE // P)
WW = DOWN_AT + FC * D
PARTS = ((0, UP_AT), (UP_AT, DOWN_AT), (DOWN_AT, WW))
SHARED = 2
ROUTED_TILES = T * TOP // P + NE - 1
FIRST_ROUTED = SHARED * NT
STEPS = FIRST_ROUTED + ROUTED_TILES
SLOT_ROWS = ROUTED_TILES * P
C_TRI = P
C_TRI4 = C_TRI + NE * NE
C_FULL = C_TRI4 + PAIRS * PAIRS
C_TILE = C_FULL + NT - 1
C_TOK = C_TILE + ROUTED_TILES + 2
CONSTS = C_TOK + NT


def at_least(eng, sem, value):
    if isinstance(value, int) and value <= 0:
        return
    eng.wait_ge(sem, value)


def wait_alone(eng, over, sem, value):
    if isinstance(value, int):
        at_least(eng, sem, value)
        return
    count = eng.to_reg(value)
    eng.wait_ge(over, 1)
    eng.wait_ge(sem, count)


class Batch:

    def __init__(self, pair, parity):
        self.pair, self.parity = pair, parity
        self.index = 2 * pair + parity

    def ahead(self, k):
        return Batch(self.pair + (self.parity + k) // 2, (self.parity + k) % 2)


class Common:

    def __init__(self, nc, stack):
        def sb(name, shape, dt=F32):
            return stack.enter_context(nc.sbuf_tensor(name, shape, dt))

        self.sem = lambda name: stack.enter_context(nc.semaphore(name))
        self.ident = sb("ident", [P, P])
        self.w_raw = sb("w_raw", [P, 2 * WW])
        self.w_hi = sb("w_hi", [P, 2 * WW], F32R)
        self.w_lo = sb("w_lo", [P, 2 * WW], F32R)
        self.tanh_ffn = sb("tanh_ffn", [P, 1])
        self.x2_out, self.xn2_out = self.sem("x2_out"), self.sem("xn2_out")
        self.raw_in = self.sem("raw_in")
        self.tile_in = [self.sem("tile_in_a"), self.sem("tile_in_b")]
        self.w_hi_done, self.w_lo_dve, self.w_lo_pool = self.sem("w_hi_done"), self.sem("w_lo_dve"), self.sem("w_lo_pool")

    def split_hi(self, act, place, k):
        lo, hi = PARTS[k]
        words = bass.ds(place + lo, hi - lo)
        act.activation(self.w_hi[:, words], self.w_raw[:, words], ACT.Copy).then_inc(self.w_hi_done, 1)

    def split_lo(self, eng, place, k, done):
        lo, hi = PARTS[k]
        words = bass.ds(place + lo, hi - lo)
        eng.tensor_tensor(self.w_lo[:, words], self.w_raw[:, words], self.w_hi[:, words].bitcast(F32),
                          ALU.subtract).then_inc(done, 1)

    def split_lo_gate(self, dve, place, number):
        dve.wait_ge(self.w_hi_done, 3 * number - 2)
        self.split_lo(dve, place, 0, self.w_lo_dve)

    def split_lo_up_down(self, pool, place, number):
        for k in (1, 2):
            pool.wait_ge(self.w_hi_done, 3 * number - 2 + k)
            self.split_lo(pool, place, k, self.w_lo_pool)


def build_kernel(nc, A, out):
    x2_buf = nc.dram_tensor("x2_buf", (T, D), F32, kind="Internal").ap()
    xn_buf = nc.dram_tensor("xn_buf", (T + P, D), F32, kind="Internal").ap()
    with ExitStack() as stack:
        common = Common(nc, stack)
        attention_phase(nc, A, x2_buf, xn_buf, common)
        expert_phase(nc, A, x2_buf, xn_buf, out, common)


def attention_phase(nc, A, x2_buf, xn_buf, common):
    with ExitStack() as ctx:
        def sb(name, shape, dt=F32):
            return ctx.enter_context(nc.sbuf_tensor(name, shape, dt))

        def ps(name, shape):
            return ctx.enter_context(nc.psum_tensor(name, shape, F32))

        sem = common.sem

        def part(buf, at, *shape):
            dims = dict(zip("abcd", shape))
            names = " ".join(dims)
            n = 1
            for size in shape:
                n *= size
            return buf[:, at:at + n].rearrange(f"p ({names}) -> p {names}", **dims)

        identf = common.ident
        identb = part(common.w_raw, WW + 4 * QC * D + QC * H, P // 2).bitcast(BF16)
        tanh_gate = sb("tanh_gate", [P, 1])
        bo_gated = sb("bo_gated", [P, D])
        bq = sb("bq", [P, R])
        bk = sb("bk", [P, 1])
        parity = sb("parity", [P, 2])
        bv = sb("bv", [P, 1])
        wqkv_hi = part(common.w_hi, 0, KC, 768)
        wqkv_lo = part(common.w_lo, 0, KC, 768)
        wo_hi = part(common.w_lo, WW, KC, D)
        wo_lo = part(common.w_lo, WW + KC * D, KC, D)
        causal_raw = part(common.w_raw, WW + 3 * QC * D, 2 * QC * S // 4).bitcast(U8).rearrange(
            "p (a c s) -> p a c s", a=2, c=QC)
        causal_neg = sb("causal_neg", [P, QC, S], BF16)
        causalT_neg = sb("causalT_neg", [P, QC, S], BF16)
        pad_raw = part(common.w_raw, 2 * QC * D + KC * S + 3 * S, B * S // 4).bitcast(U8).rearrange(
            "p (b s) -> p b s", b=B)
        pad_neg = sb("pad_neg", [P, B, S], BF16)
        padT_raw = sb("padT_raw", [P, QC, B], U8)
        padT_neg = sb("padT_neg", [P, QC, B], BF16)
        xt = part(common.w_raw, 0, QC, D)
        ln_stats = sb("ln_stats", [P, 2, QC, 6])
        ln_mv = sb("ln_mv", [P, 2, QC, 2])
        ln_var = sb("ln_var", [P, 2, QC])
        ln_y = sb("ln_y", [P, 2, QC])
        ln_t = sb("ln_t", [P, 2, QC])
        xn = part(common.w_raw, QC * D, QC, D)
        xT_hi = part(common.w_hi, KC * 768, KC, S)
        xT_lo = part(common.w_lo, KC * 768, KC, S)
        cT_raw = part(common.w_raw, 2 * QC * D, KC, S)
        cT_hi = part(common.w_hi, WW, KC, S)
        cT_lo = part(common.w_hi, WW + KC * S, KC, S)
        q_hi = part(common.w_hi, WW + 2 * KC * S, R, S)
        q_lo = part(common.w_hi, WW + 2 * KC * S + R * S, R, S)
        k_raw = part(common.w_raw, 2 * QC * D + KC * S, S)
        k_hi = sb("k_hi", [P, 2, S], F32R)
        k_lo = sb("k_lo", [P, 2, S], F32R)
        vT = part(common.w_raw, 2 * QC * D + KC * S + S, S)
        v_stage = part(common.w_raw, 2 * QC * D + KC * S + 2 * S, QC, G, HD)
        q_stack = [sb(f"q_stack{i}", [P, GP, R, S], F32R) for i in range(2)]
        k_stack = [sb(f"k_stack{i}", [P, GP, 2, S], F32R) for i in range(2)]
        v_ones = [sb(f"v_ones{i}", [P, QC, G, 2 * HD]) for i in range(2)]
        mask = [sb(f"mask{i}", [P, QC, S], BF16) for i in range(2)]
        maskT = [sb(f"maskT{i}", [P, QC, S], BF16) for i in range(2)]
        row_max = part(common.w_raw, WW + 4 * QC * D, QC, H)
        neg_max = part(common.w_hi, WW + 2 * (KC + R) * S, QC, 2, 2, H // 2)
        neg_maxT = part(common.w_lo[0:2 * H], WW + 2 * KC * D, S)
        probs = sb("probs", [P, 8, 512])
        mixed = [sb(f"mixed{i}", [P, 4, 512]) for i in range(2)]
        inv_sum = sb("inv_sum", [P, R, 4])
        attn = part(common.w_raw, WW, QC, D)
        aT_hi = sb("aT_hi", [P, KC, P], F32R)
        aT_lo = sb("aT_lo", [P, KC, P], F32R)
        x_res = part(common.w_raw, WW + QC * D, QC, D)
        x2 = part(common.w_raw, WW + 2 * QC * D, QC, D)
        xn2 = part(common.w_raw, WW + 3 * QC * D, QC, D)

        ones = xT_hi[0:2]
        zeros = k_stack[0][AUX + 4:AUX + 8].rearrange("p g h s -> p (g h s)").rearrange(
            "p (g r s) -> p g r s", g=GP // 2, r=R)

        score_bank = [ps(f"score_bank{i}", [P, 2, S]) for i in range(2)]
        prob_bank = [ps(f"prob_bank{i}", [P, 2, S]) for i in range(2)]
        pv_bank = ps("pv_bank", [P, 512])
        front_bank = [ps(f"front_bank{i}", [P, 512]) for i in range(2)]
        tail_bank = ps("tail_bank", [P, 512])

        weights_in, consts_in = sem("weights_in"), sem("consts_in")
        ones_in = sem("ones_in")
        x_in, ctx_in, res_in = sem("x_in"), sem("ctx_in"), sem("res_in")
        stack_in = [sem("stack_in_a"), sem("stack_in_b")]
        max_in = sem("max_in")
        x2_out, xn2_out = common.x2_out, common.xn2_out
        pool_setup, mask_setup = sem("pool_setup"), sem("mask_setup")
        dve_setup, act_setup = sem("dve_setup"), sem("act_setup")
        front_done, scores_done, maxT_done = sem("front_done"), sem("scores_done"), sem("maxT_done")
        probs_scored, pv_done, tail_done = sem("probs_scored"), sem("pv_done"), sem("tail_done")
        ln1_step, xT_lo_done, q_lo_done, k_lo_done = sem("ln1_step"), sem("xT_lo_done"), sem("q_lo_done"), sem("k_lo_done")
        maxima_done, max_split = sem("maxima_done"), sem("max_split")
        tail_step, ln2_step = sem("tail_step"), sem("ln2_step")
        xT_hi_done, q_hi_done, kv_copied, v_staged = sem("xT_hi_done"), sem("q_hi_done"), sem("kv_copied"), sem("v_staged")
        exp_done, mixed_done, maxT_copied, aT_hi_done = sem("exp_done"), sem("mixed_done"), sem("maxT_copied"), sem("aT_hi_done")
        ctx_split, mask_done, maskT_done, res_done, v_ready = (
            sem("ctx_split"), sem("mask_done"), sem("maskT_done"), sem("res_done"), sem("v_ready"))

        block = ctx.enter_context(nc.Block())

        def rows(buf, batch):
            return buf[bass.ds(S * batch.index, S), :].rearrange("(c p) d -> p c d", p=P)

        def copy_rows(eng, dst, src):
            return eng.dma_start(dst.bitcast(F32), src.bitcast(F32))

        def pipeline(iteration, eng):
            def part(n):
                return dict(prep=0 <= n + 3 < B, front=0 <= n + 2 < B, score=0 <= n + 1 < B, soft=0 <= n < B,
                            tail=0 <= n - 1 < B)
            for n in (-3, -2, -1, 0):
                iteration(Batch(n // 2, n % 2), **part(n))
            with eng.Fori(0, B // 2 - 2) as pair:
                for k in (1, 2):
                    iteration(Batch(pair, 0).ahead(k), prep=True, front=True, score=True, soft=True, tail=True)
            for n in (B - 3, B - 2, B - 1, B):
                iteration(Batch(n // 2, n % 2), **part(n))

        @block.sync
        def _(sp):
            wqkv_raw = probs[:, 0:6, :].rearrange("p a b -> p (a b)")
            wo_raw = mixed[0][:].rearrange("p a b -> p (a b)")
            sp.dma_start(wqkv_raw, A["wqkv"]).then_inc(weights_in, 16)
            sp.dma_start(wo_raw, A["wo"]).then_inc(weights_in, 16)
            sp.wait_ge(pool_setup, POOL_SETUP)
            for i in range(2):
                for g2 in range(2):
                    copy_rows(sp, k_stack[i][AUX + 2 * g2:AUX + 2 * g2 + 2, :, g2, :], ones).then_inc(ones_in, 16)
            sp.wait_ge(ones_in, 64)

            def stack(m, half):
                if half == 0:
                    wait_alone(sp, pool_setup, q_lo_done, R * (m.index + 1))
                    wait_alone(sp, pool_setup, k_lo_done, 2 * (m.index + 1))
                wait_alone(sp, pool_setup, probs_scored, PROB_UNITS * (m.index - 2) + PROB_UNITS // 2 * (half + 1))
                qs, ks = q_stack[m.parity], k_stack[m.parity]
                for gp in range(GP // 2 * half, GP // 2 * (half + 1)):
                    src = slice(PAIR * gp, PAIR * (gp + 1))
                    for part, (q, k) in enumerate([(q_hi, k_hi), (q_hi, k_lo), (q_lo, k_hi)]):
                        dst = slice(PAIR * part, PAIR * (part + 1))
                        copy_rows(sp, qs[dst, gp, :, :], q[src, :, :]).then_inc(stack_in[half], 16)
                        copy_rows(sp, ks[dst, gp, :, :], k[src, :, :]).then_inc(stack_in[half], 16)
                copy_rows(sp, qs[AUX:AUX + 4, GP // 2 * half:GP // 2 * (half + 1), :, :], zeros).then_inc(stack_in[half], 16)

            def iteration(n, prep, front, score, soft, tail):
                m, after, t = n.ahead(2), n.ahead(3), n.ahead(-1)
                if prep:
                    wait_alone(sp, pool_setup, ln1_step, NORM_STEPS * after.index)
                    sp.dma_start(xt[:], rows(A["x"], after)).then_inc(x_in, 16)
                    wait_alone(sp, pool_setup, ctx_split, 2 * after.index)
                    sp.dma_start(cT_raw[:], A["ctxT"][:, bass.ds(S * after.index, S)].rearrange(
                        "(k p) s -> p k s", p=P)).then_inc(ctx_in, 16)
                if front:
                    stack(m, 0)
                if tail:
                    wait_alone(sp, pool_setup, tail_step, 12 * (t.index + 1))
                    sp.dma_start(rows(x2_buf, t), x2[:]).then_inc(x2_out, 16)
                if score and not front:
                    sp.wait_ge(front_done, 6 * B)
                    sp.wait_ge(k_lo_done, 2 * B)
                    sp.wait_ge(v_ready, B)
                    sp.dma_start(common.w_raw[:, 0:WW], A["experts"][0]).then_inc(common.raw_in, 16)
                if soft:
                    wait_alone(sp, pool_setup, tail_step, 12 * n.index)
                    sp.dma_start(x_res[:], rows(A["x"], n)).then_inc(res_in, 16)
                if tail:
                    wait_alone(sp, pool_setup, ln2_step, NORM_STEPS * (t.index + 1))
                    sp.dma_start(rows(xn_buf, t), xn2[:]).then_inc(xn2_out, 16)
                if front:
                    stack(m, 1)

            pipeline(iteration, sp)

        @block.gpsimd
        def _(pool):
            pool.dma_start(bq[:], A["bq"]).then_inc(consts_in, 16)
            pool.dma_start(bk[:], A["bk"]).then_inc(consts_in, 16)
            pool.dma_start(bv[:], A["bv"]).then_inc(consts_in, 16)
            pool.dma_start(parity[:], A["parity"]).then_inc(consts_in, 16)
            pool.dma_start(tanh_gate[:], A["g_xattn"].partition_broadcast(P)).then_inc(consts_in, 16)
            pool.dma_start(common.tanh_ffn[:], A["g_ffn"].partition_broadcast(P)).then_inc(consts_in, 16)
            pool.dma_start(bo_gated[:], A["bo"].partition_broadcast(P)).then_inc(consts_in, 16)
            pool.dma_start(causal_raw[:, 0], A["causal"].rearrange("(c p) k -> p c k", p=P)).then_inc(consts_in, 16)
            pool.dma_start(causal_raw[:, 1], A["causalT"].rearrange("(c p) q -> p c q", p=P)).then_inc(consts_in, 16)
            pool.dma_start(pad_raw[:], A["pad"].partition_broadcast(P)).then_inc(consts_in, 16)
            pool.dma_start(padT_raw[:], A["padT"].rearrange("(c p) b -> p c b", p=P)).then_inc(consts_in, 16)
            pool.memset(identf[:], 0.0).then_inc(pool_setup, 1)
            pool.memset(identb[:], 0.0).then_inc(pool_setup, 1)
            pool.wait_ge(pool_setup, 2)
            for ident in (identf, identb):
                pool.affine_select(out=ident[:], in_=ident[:], compare_op=ALU.not_equal, fill=1.0, base=0,
                                   pattern=[[-1, P]], channel_multiplier=1).then_inc(pool_setup, 1)
            pool.memset(ones.bitcast(F32), 1.0).then_inc(pool_setup, 1)
            for i in range(2):
                pool.memset(k_stack[i][:].bitcast(F32), 0.0).then_inc(pool_setup, 1)
                pool.memset(v_ones[i][:], 0.0).then_inc(pool_setup, 1)
            pool.wait_ge(pool_setup, 9)
            for i in range(2):
                pool.memset(v_ones[i][:, :, :, HD:HD + 1], 1.0).then_inc(pool_setup, 1)
            pool.wait_ge(consts_in, 16 * 11)
            pool.tensor_scalar(causal_neg[:], causal_raw[:, 0], NEG, None, ALU.mult).then_inc(pool_setup, 1)
            pool.tensor_scalar(causalT_neg[:], causal_raw[:, 1], NEG, None, ALU.mult).then_inc(pool_setup, 1)
            pool.tensor_scalar(padT_neg[:], padT_raw[:], NEG, None, ALU.mult).then_inc(mask_setup, 1)
            pool.tensor_scalar(pad_neg[:], pad_raw[:], NEG, None, ALU.mult).then_inc(mask_setup, 1)
            pool.wait_ge(mask_setup, 2)
            pool.wait_ge(pool_setup, POOL_SETUP)

            def iteration(n, prep, front, score, soft, tail):
                m, after = n.ahead(2), n.ahead(3)
                if prep:
                    at_least(pool, ctx_in, 16 * (after.index + 1))
                    wait_alone(pool, mask_setup, front_done, 6 * (after.index - 1) + 5)
                    pool.tensor_copy(cT_hi[:], cT_raw[:]).then_inc(ctx_split, 1)
                    at_least(pool, ctx_split, 2 * after.index + 1)
                    pool.tensor_tensor(cT_lo[:], cT_raw[:], cT_hi[:].bitcast(F32), ALU.subtract).then_inc(ctx_split, 1)
                if front:
                    at_least(pool, maxima_done, SCORE_UNITS * (m.index - 1))
                    pool.tensor_tensor(mask[m.parity][:], causal_neg[:],
                                       pad_neg[:, bass.ds(m.index, 1), :].to_broadcast([P, QC, S]),
                                       ALU.add).then_inc(mask_done, 1)
                if soft:
                    at_least(pool, res_in, 16 * (n.index + 1))
                    at_least(pool, act_setup, 2)
                    pool.tensor_tensor(x_res[:], x_res[:], bo_gated[:].unsqueeze(1).to_broadcast([P, QC, D]),
                                       ALU.add).then_inc(res_done, 1)
                if front:
                    at_least(pool, probs_scored, PROB_UNITS * (m.index - 1))
                    pool.tensor_tensor(maskT[m.parity][:], causalT_neg[:],
                                       padT_neg[:, :, bass.ds(m.index, 1)].to_broadcast([P, QC, S]),
                                       ALU.add).then_inc(maskT_done, 1)
                    at_least(pool, v_staged, m.index + 1)
                    wait_alone(pool, mask_setup, pv_done, 8 * (m.index - 1))
                    pool.tensor_copy(v_ones[m.parity][:, :, :, 0:HD], v_stage[:]).then_inc(v_ready, 1)

                if soft and not score:
                    common.split_lo_up_down(pool, 0, 1)

            pipeline(iteration, pool)

        @block.tensor
        def _(pe):
            pe.wait_ge(pool_setup, POOL_SETUP)
            pe.wait_ge(ones_in, 64)
            pe.wait_ge(dve_setup, 4)

            def products(out_, left, right):
                n = len(left)
                for c in range(n):
                    for j, (a, b) in enumerate([(0, 0), (1, 0), (0, 1)]):
                        last = pe.matmul(out_, left[c][a], right[c][b], start=c == 0 and j == 0,
                                         stop=c == n - 1 and j == 2)
                return last

            def front_transposes(m, f):
                at_least(pe, ln1_step, NORM_STEPS * (m.index + 1))
                at_least(pe, (kv_copied, v_staged)[f], (4, 1)[f] * m.index)
                for k in range(2):
                    for c in range(QC):
                        last = pe.transpose(front_bank[f][:, k * S + c * P:k * S + (c + 1) * P],
                                            xn[:, c, (2 * f + k) * P:(2 * f + k + 1) * P], identf[:])
                last.then_inc(front_done, 1)

            def front_queries(m, f):
                if f == 0:
                    at_least(pe, xT_lo_done, 2 * (m.index + 1))
                for r in (2 * f, 2 * f + 1):
                    last = products(front_bank[f][:, (r % 2) * S:(r % 2 + 1) * S],
                                    [(wqkv_hi[:, c, r * P:(r + 1) * P], wqkv_lo[:, c, r * P:(r + 1) * P]) for c in range(KC)],
                                    [(xT_hi[:, c, :], xT_lo[:, c, :]) for c in range(KC)])
                last.then_inc(front_done, 1)

            def front_keys_values(m):
                at_least(pe, ctx_split, 2 * (m.index + 1))
                at_least(pe, q_lo_done, R * m.index + 2)
                for j in range(2):
                    cols = slice(D + j * P, D + (j + 1) * P)
                    last = products(front_bank[0][:, j * S:(j + 1) * S],
                                    [(wqkv_hi[:, c, cols], wqkv_lo[:, c, cols]) for c in range(KC)],
                                    [(cT_hi[:, c, :], cT_lo[:, c, :]) for c in range(KC)])
                last.then_inc(front_done, 1)

            def front_values(m):
                at_least(pe, kv_copied, 4 * m.index + 1)
                at_least(pe, q_lo_done, R * (m.index + 1))
                for c in range(QC):
                    last = pe.transpose(front_bank[1][:, c * P:(c + 1) * P], vT[:, c * P:(c + 1) * P], identf[:])
                last.then_inc(front_done, 1)

            def score_unit(m, u):
                gp, r, c = u // (R * QC), u // QC % R, u % QC
                if u % (SCORE_UNITS // 2) == 0:
                    at_least(pe, stack_in[2 * u // SCORE_UNITS], 16 * STACK_DMAS * (m.index + 1))
                bank = score_bank[(m.parity + u) % 2]
                if u == 0:
                    at_least(pe, maxima_done, SCORE_UNITS * m.index)
                elif u == 1:
                    at_least(pe, maxT_copied, m.index)
                else:
                    at_least(pe, maxima_done, SCORE_UNITS * m.index + u - 1)
                pe.matmul(bank[:].rearrange("p a b -> p (a b)"), q_stack[m.parity][:, gp, r, c * P:(c + 1) * P],
                          k_stack[m.parity][:, gp].rearrange("p a b -> p (a b)"),
                          start=True, stop=True).then_inc(scores_done, 1)

            def transpose_maxima(m):
                wait_alone(pe, dve_setup, max_split, 2 * (m.index + 1))
                bank = score_bank[(m.parity + SCORE_UNITS) % 2][:].rearrange("p a b -> p (a b)")
                for c in range(QC):
                    last = pe.transpose(bank[0:2 * H, c * P:(c + 1) * P],
                                        neg_max[:, c].rearrange("p a b h -> p (a b h)").bitcast(F32), identf[:])
                last.then_inc(maxT_done, 1)

            def prob_unit(n, v):
                gg, rp, kc, j = v // 16, v // 8 % 2, v // 4 % 2, v % 4
                gp, g2 = 2 * gg + j // 2, j % 2
                if v == 0:
                    at_least(pe, max_in, 16 * (n.index + 1))
                    at_least(pe, maskT_done, n.index + 1)
                at_least(pe, exp_done, PROB_UNITS * n.index + v - 1)
                bank = prob_bank[v % 2][:].rearrange("p a b -> p (a b)")
                pe.matmul(bank, k_stack[n.parity][:, gp, g2, kc * P:(kc + 1) * P],
                          q_stack[n.parity][:, gp, 2 * rp:2 * rp + 2, :].rearrange("p a b -> p (a b)"),
                          start=True, stop=False)
                pe.matmul(prob_bank[v % 2][:], identb[:],
                          maskT[n.parity][:, kc, :].unsqueeze(1).to_broadcast([P, 2, S]),
                          start=False, stop=True).then_inc(probs_scored, 1)

            def value_group(n, k):
                gg, w, kc = k // 4, k // 2, k % 2
                if k == 0:
                    at_least(pe, v_ready, n.index + 1)
                at_least(pe, exp_done, PROB_UNITS * n.index + 4 * k + 4)
                if kc == 0:
                    at_least(pe, mixed_done, 4 * n.index + w)
                for j in range(4):
                    last = pe.matmul(pv_bank[32 * j:32 * (j + 1), :], v_ones[n.parity][:, kc, 4 * gg + j, :],
                                     probs[:, (4 * k + j) % 8, :], start=kc == 0, stop=kc == 1)
                last.then_inc(pv_done, 1)

            def tail_unmix(t, c, gg):
                at_least(pe, mixed_done, 4 * (t.index + 1))
                at_least(pe, tail_step, 12 * t.index + 6 * c + 2 * gg)
                for r in range(R):
                    last = pe.transpose(tail_bank[:, r * P:(r + 1) * P],
                                        mixed[t.parity][:, 2 * gg + r // 2, (r % 2) * S + c * P:(r % 2) * S + (c + 1) * P],
                                        identf[:])
                last.then_inc(tail_done, 1)

            def tail_transposes(t, c):
                at_least(pe, tail_step, 12 * t.index + 6 * c + 4)
                for k in range(KC):
                    last = pe.transpose(tail_bank[:, k * P:(k + 1) * P], attn[:, c, k * P:(k + 1) * P], identf[:])
                last.then_inc(tail_done, 1)

            def tail_project(t, c):
                at_least(pe, tail_step, 12 * t.index + 6 * c + 5)
                products(tail_bank[:], [(aT_hi[:, k, :], aT_lo[:, k, :]) for k in range(KC)],
                         [(wo_hi[:, k, :], wo_lo[:, k, :]) for k in range(KC)]).then_inc(tail_done, 1)

            def iteration(n, prep, front, score, soft, tail):
                m, s, t = n.ahead(2), n.ahead(1), n.ahead(-1)
                for slot in range(SLOTS):
                    if score and slot < SCORE_UNITS:
                        score_unit(s, slot)
                    if soft and 0 <= slot - PROB_LAG < PROB_UNITS:
                        prob_unit(n, slot - PROB_LAG)
                    if soft and 0 <= slot - PV_LAG <= 28 and (slot - PV_LAG) % 4 == 0:
                        value_group(n, (slot - PV_LAG) // 4)
                    if front:
                        if slot in (0, 1):
                            front_transposes(m, slot)
                        if slot in (9, 11):
                            front_queries(m, (slot - 9) // 2)
                        if slot == 13:
                            front_keys_values(m)
                        if slot == 15:
                            front_values(m)
                    if tail:
                        for c in range(QC):
                            if slot == 17 * c:
                                tail_unmix(t, c, 0)
                            if slot == 17 * c + 2:
                                tail_unmix(t, c, 1)
                            if slot == 17 * c + 4:
                                tail_transposes(t, c)
                            if slot == 17 * c + 7:
                                tail_project(t, c)
                    if score and slot == 34:
                        transpose_maxima(s)

            pipeline(iteration, pe)

        @block.scalar
        def _(act):
            act.wait_ge(consts_in, 16 * 11)
            act.activation(tanh_gate[:], tanh_gate[:], ACT.Tanh).then_inc(act_setup, 1)
            act.wait_ge(act_setup, 1)
            act.activation(bo_gated[:], bo_gated[:], ACT.Copy, scale=tanh_gate[:, 0:1]).then_inc(act_setup, 1)
            act.wait_ge(weights_in, 32)
            act.activation(wqkv_hi[:].rearrange("p a b -> p (a b)"), probs[:, 0:6, :].rearrange("p a b -> p (a b)"),
                           ACT.Copy).then_inc(act_setup, 1)
            act.activation(wo_hi[:].rearrange("p a b -> p (a b)"), mixed[0][:].rearrange("p a b -> p (a b)"),
                           ACT.Copy).then_inc(act_setup, 1)
            act.activation(common.tanh_ffn[:], common.tanh_ffn[:], ACT.Tanh).then_inc(act_setup, 1)
            act.wait_ge(dve_setup, 4)

            def front_x_hi(m, f):
                at_least(act, front_done, 6 * m.index + f + 1)
                at_least(act, front_done, 6 * (m.index - 1) + 4)
                act.activation(xT_hi[:, 2 * f:2 * f + 2, :].rearrange("p a b -> p (a b)"), front_bank[f][:],
                               ACT.Copy).then_inc(xT_hi_done, 1)

            def front_q_hi(m, r):
                at_least(act, front_done, 6 * m.index + 3 + r // 2)
                if r == 0:
                    for half in range(2):
                        at_least(act, stack_in[half], 16 * STACK_DMAS * m.index)
                act.activation(q_hi[:, r, :], front_bank[r // 2][:, (r % 2) * S:(r % 2 + 1) * S], ACT.Identity,
                               bias=bq[:, r:r + 1]).then_inc(q_hi_done, 1)

            def front_kv(m):
                at_least(act, front_done, 6 * m.index + 5)
                act.activation(vT[:], front_bank[0][:, S:2 * S], ACT.Identity, bias=bv[:, 0:1]).then_inc(kv_copied, 1)
                for half in range(2):
                    at_least(act, stack_in[half], 16 * STACK_DMAS * m.index)
                act.activation(k_raw[:], front_bank[0][:, 0:S], ACT.Identity, bias=bk[:, 0:1]).then_inc(kv_copied, 1)
                at_least(act, kv_copied, 4 * m.index + 2)
                for g2 in range(2):
                    act.activation(k_hi[:, g2, :], k_raw[:], ACT.Copy, scale=parity[:, g2:g2 + 1]).then_inc(kv_copied, 1)

            def front_v(m):
                at_least(act, front_done, 6 * m.index + 6)
                at_least(act, v_ready, m.index)
                act.activation(v_stage[:].rearrange("p c g d -> p (c g d)"), front_bank[1][:, 0:QC * P],
                               ACT.Copy).then_inc(v_staged, 1)

            def exp_unit(n, v):
                at_least(act, probs_scored, PROB_UNITS * n.index + v + 1)
                if v % 4 == 0:
                    at_least(act, pv_done, 8 * n.index + v // 4 - 1)
                act.activation(probs[:, v % 8, :], prob_bank[v % 2][:].rearrange("p a b -> p (a b)"), ACT.Exp,
                               scale=HD ** -0.5).then_inc(exp_done, 1)

            def copy_mixed(n, w):
                at_least(act, pv_done, 8 * n.index + 2 * w + 2)
                if w == 0:
                    at_least(act, tail_done, 8 * (n.index - 1))
                act.activation(mixed[n.parity][:, w, :], pv_bank[:], ACT.Copy).then_inc(mixed_done, 1)

            def stack_maxima(m):
                at_least(act, maxT_done, m.index + 1)
                at_least(act, max_in, 16 * m.index)
                at_least(act, stack_in[0], 16 * STACK_DMAS * (m.index + 1))
                at_least(act, stack_in[1], 16 * STACK_DMAS * (m.index + 1))
                act.activation(neg_maxT[:], score_bank[(m.parity + SCORE_UNITS) % 2][0:2 * H].rearrange(
                    "p a b -> p (a b)")[:, 0:S], ACT.Copy).then_inc(maxT_copied, 1)
                at_least(act, maxT_copied, m.index + 1)
                copy_rows(act, q_stack[m.parity][AUX:AUX + 4].rearrange("o g r s -> o (g r s)"), neg_maxT[:]).then_inc(max_in, 16)

            def tail_hi(t, c):
                at_least(act, tail_done, 8 * t.index + 4 * c + 3)
                at_least(act, tail_done, 8 * t.index + 4 * c)
                act.activation(aT_hi[:].rearrange("p k q -> p (k q)"), tail_bank[:], ACT.Copy).then_inc(aT_hi_done, 1)

            def iteration(n, prep, front, score, soft, tail):
                m, s, t = n.ahead(2), n.ahead(1), n.ahead(-1)
                for slot in range(SLOTS):
                    if soft and 0 <= slot - PROB_LAG < PROB_UNITS:
                        exp_unit(n, slot - PROB_LAG)
                    if soft and slot in (13, 21, 29, 37):
                        copy_mixed(n, (slot - 13) // 8)
                    if tail and slot in (5, 22):
                        tail_hi(t, slot // 22)
                    if front:
                        if slot in (1, 2):
                            front_x_hi(m, slot - 1)
                        if slot in (10, 12):
                            front_q_hi(m, slot - 10)
                            front_q_hi(m, slot - 9)
                        if slot == 14:
                            front_kv(m)
                        if slot == 16:
                            front_v(m)
                    if score and slot == 35:
                        stack_maxima(s)
                    if soft and not score and slot in (3, 11, 19):
                        act.wait_ge(common.raw_in, 16)
                        act.wait_ge(xT_lo_done, 2 * B)
                        common.split_hi(act, 0, slot // 8)

            pipeline(iteration, act)

        @block.vector
        def _(dve):
            dve.memset(q_stack[0][:].bitcast(F32), 0.0).then_inc(dve_setup, 1)
            dve.memset(q_stack[1][:].bitcast(F32), 0.0).then_inc(dve_setup, 1)
            dve.wait_ge(act_setup, 5)
            dve.tensor_tensor(wqkv_lo[:].rearrange("p a b -> p (a b)"), probs[:, 0:6, :].rearrange("p a b -> p (a b)"),
                              wqkv_hi[:].rearrange("p a b -> p (a b)").bitcast(F32), ALU.subtract).then_inc(dve_setup, 1)
            dve.tensor_tensor(wo_lo[:].rearrange("p a b -> p (a b)"), mixed[0][:].rearrange("p a b -> p (a b)"),
                              wo_hi[:].rearrange("p a b -> p (a b)").bitcast(F32), ALU.subtract).then_inc(dve_setup, 1)

            def norm_step(k, which, x, out_, step, index):
                stats, mv, var = ln_stats[:, which], ln_mv[:, which], ln_var[:, which]
                y, t = ln_y[:, which], ln_t[:, which]
                wait_alone(dve, dve_setup, step, NORM_STEPS * index + k)
                if k < 2:
                    ins = dve.bn_stats(stats[:, k, :], x[:, k, :])
                elif k < 4:
                    ins = dve.bn_aggr(mv[:, k - 2, :], stats[:, k - 2, :])
                elif k == 4:
                    ins = dve.tensor_scalar(var, mv[:, :, 1], EPS, None, ALU.add)
                elif k == 5:
                    ins = dve.tensor_scalar(t.bitcast(I32), var.bitcast(I32), 1, None, ALU.logical_shift_right)
                elif k == 6:
                    ins = dve.tensor_scalar(y.bitcast(I32), t.bitcast(I32), -1.0, RSQRT_MAGIC, ALU.mult, ALU.add)
                elif k < 16:
                    if k % 3 == 1:
                        ins = dve.scalar_tensor_tensor(t, y, -0.5, y, ALU.mult, ALU.mult)
                    elif k % 3 == 2:
                        ins = dve.tensor_tensor(t, t, var, ALU.mult)
                    else:
                        ins = dve.scalar_tensor_tensor(y, t, 1.5, y, ALU.add, ALU.mult)
                else:
                    c = k - 16
                    ins = dve.tensor_scalar(out_[:, c, :], x[:, c, :], mv[:, c, 0:1], y[:, c:c + 1], ALU.subtract, ALU.mult)
                ins.then_inc(step, 1)

            def prep_norm(m, k):
                if k == 0:
                    at_least(dve, x_in, 16 * (m.index + 1))
                if k == 16:
                    at_least(dve, front_done, 6 * (m.index - 1) + 2)
                norm_step(k, 0, xt, xn, ln1_step, m.index)

            def front_x_lo(m, f):
                at_least(dve, xT_hi_done, 2 * m.index + f + 1)
                dve.tensor_tensor(xT_lo[:, 2 * f:2 * f + 2, :].rearrange("p a b -> p (a b)"), front_bank[f][:],
                                  xT_hi[:, 2 * f:2 * f + 2, :].rearrange("p a b -> p (a b)").bitcast(F32),
                                  ALU.subtract).then_inc(xT_lo_done, 1)

            def front_q_lo(m, r):
                at_least(dve, q_hi_done, R * m.index + 2 * (r // 2) + 2)
                dve.scalar_tensor_tensor(q_lo[:, r, :], front_bank[r // 2][:, (r % 2) * S:(r % 2 + 1) * S],
                                         bq[:, r:r + 1], q_hi[:, r, :].bitcast(F32), ALU.add,
                                         ALU.subtract).then_inc(q_lo_done, 1)

            def front_k_lo(m):
                at_least(dve, kv_copied, 4 * (m.index + 1))
                for g2 in range(2):
                    dve.scalar_tensor_tensor(k_lo[:, g2, :], k_raw[:], parity[:, g2:g2 + 1], k_hi[:, g2, :].bitcast(F32),
                                             ALU.mult, ALU.subtract).then_inc(k_lo_done, 1)

            def maxima_unit(m, u):
                gp, r, c = u // (R * QC), u // QC % R, u % QC
                if u == 0:
                    at_least(dve, mask_done, m.index + 1)
                    at_least(dve, max_split, 2 * m.index)
                wait_alone(dve, dve_setup, scores_done, SCORE_UNITS * m.index + u + 1)
                bank = score_bank[(m.parity + u) % 2]
                for g2 in range(2):
                    head = g2 * H // 2 + gp * R + r
                    last = dve.tensor_tensor_reduce(out=bank[:, g2, :], in0=bank[:, g2, :], in1=mask[m.parity][:, c, :],
                                                    scale=1.0, scalar=-3e38, op0=ALU.add, op1=ALU.max,
                                                    accum_out=row_max[:, c, head:head + 1])
                last.then_inc(maxima_done, 1)

            def split_maxima(m):
                at_least(dve, maxima_done, SCORE_UNITS * (m.index + 1))
                at_least(dve, maxT_done, m.index)
                maxima = row_max[:].rearrange("p c (a h) -> p c a h", a=2)
                dve.tensor_scalar(neg_max[:, :, :, 0, :], maxima, -1.0, None, ALU.mult).then_inc(max_split, 1)
                at_least(dve, max_split, 2 * m.index + 1)
                dve.scalar_tensor_tensor(neg_max[:, :, :, 1, :], maxima, -1.0, neg_max[:, :, :, 0, :].bitcast(F32),
                                         ALU.mult, ALU.subtract).then_inc(max_split, 1)

            def tail_normalize(t, c, gg):
                done = 12 * t.index + 6 * c + 2 * gg
                at_least(dve, tail_done, 8 * t.index + 4 * c + gg + 1)
                at_least(dve, tail_step, done)
                heads = tail_bank[:].rearrange("p (h w) -> p h w", w=2 * HD)
                sums = inv_sum[:].rearrange("p r j -> p (r j)")
                dve.reciprocal(sums, heads[:, :, HD]).then_inc(tail_step, 1)
                at_least(dve, tail_step, done + 1)
                dve.tensor_tensor(attn[:, c, gg * S:(gg + 1) * S].rearrange("p (h w) -> p h w", w=HD),
                                  heads[:, :, 0:HD], sums.unsqueeze(2).to_broadcast([P, H // 2, HD]),
                                  ALU.mult).then_inc(tail_step, 1)

            def tail_lo(t, c):
                at_least(dve, aT_hi_done, 2 * t.index + c + 1)
                dve.tensor_tensor(aT_lo[:].rearrange("p k q -> p (k q)"), tail_bank[:],
                                  aT_hi[:].rearrange("p k q -> p (k q)").bitcast(F32),
                                  ALU.subtract).then_inc(tail_step, 1)

            def tail_residual(t, c):
                at_least(dve, tail_done, 8 * t.index + 4 * c + 4)
                if c == 0:
                    at_least(dve, res_done, t.index + 1)
                    at_least(dve, x2_out, 16 * t.index)
                    at_least(dve, ln2_step, NORM_STEPS * t.index)
                dve.scalar_tensor_tensor(x2[:, c, :], tail_bank[:], tanh_gate[:, 0:1], x_res[:, c, :], ALU.mult,
                                         ALU.add).then_inc(tail_step, 1)

            def tail_norm(t, k):
                if k == 0:
                    at_least(dve, tail_step, 12 * (t.index + 1))
                if k == 16:
                    at_least(dve, xn2_out, 16 * t.index)
                norm_step(k, 1, x2, xn2, ln2_step, t.index)

            NORM_SLOTS = [(0, 1), (2, 3, 4), (5, 6, 7), (8, 9, 10), (11, 12, 13), (14, 15), (16,), (17,)]

            def iteration(n, prep, front, score, soft, tail):
                after, m, s, t = n.ahead(3), n.ahead(2), n.ahead(1), n.ahead(-1)
                for slot in range(SLOTS):
                    if score and slot < SCORE_UNITS:
                        maxima_unit(s, slot)
                    if front:
                        if slot in (2, 3):
                            front_x_lo(m, slot - 2)
                        if slot in (10, 12):
                            front_q_lo(m, slot - 10)
                            front_q_lo(m, slot - 9)
                        if slot == 15:
                            front_k_lo(m)
                    if tail:
                        for c in range(QC):
                            if slot == 17 * c + 1:
                                tail_normalize(t, c, 0)
                            if slot == 17 * c + 3:
                                tail_normalize(t, c, 1)
                            if slot == 17 * c + 5:
                                tail_lo(t, c)
                            if slot == 17 * c + 8:
                                tail_residual(t, c)
                        if 26 <= slot < 34:
                            for k in NORM_SLOTS[slot - 26]:
                                tail_norm(t, k)
                    if prep and 16 <= slot < 24:
                        for k in NORM_SLOTS[slot - 16]:
                            prep_norm(after, k)
                    if score and slot == 32:
                        split_maxima(s)
                    if soft and not score and slot == 24:
                        common.split_lo_gate(dve, 0, 1)

            pipeline(iteration, dve)


CHOSEN_STEP = 19
ROUTE_STEPS = 65


class Step:

    def __init__(self, pair, parity):
        self.pair, self.parity = pair, parity
        self.index = 2 * pair + parity

    def ahead(self, k):
        return Step(self.pair + (self.parity + k) // 2, (self.parity + k) % 2)


def at_step(number):
    return Step(number // 2, number % 2)


BASE_FIRST = 4
RING = 4


class RingStep(Step):

    def __init__(self, turn, place):
        super().__init__(turn * (RING // 2) + place // 2, place % 2)
        self.turn, self.place = turn, place

    def ahead(self, k):
        return RingStep(self.turn + (self.place + k) // RING, (self.place + k) % RING)


def at_ring(number):
    return RingStep(number // RING, number % RING)


def expert_phase(nc, A, x2_buf, xn_buf, out, common):
    with ExitStack() as ctx:
        def sb(name, shape, dt=F32):
            return ctx.enter_context(nc.sbuf_tensor(name, shape, dt))

        def ps(name, shape):
            return ctx.enter_context(nc.psum_tensor(name, shape, F32))

        sem = common.sem

        row_table = nc.dram_tensor("row_table", (SLOT_ROWS, 2), I32, kind="Internal").ap()

        ident, w_raw, w_hi, w_lo = common.ident, common.w_raw, common.w_hi, common.w_lo
        raw_in, tile_in, x2_out, xn2_out = common.raw_in, common.tile_in, common.x2_out, common.xn2_out
        x_tile = [sb(f"x_tile{i}", [P, D]) for i in range(2)]
        w_hi_done, w_lo_dve, w_lo_pool = common.w_hi_done, common.w_lo_dve, common.w_lo_pool
        ones_mat = sb("ones_mat", [P, P])
        consts = sb("consts", [P, CONSTS])
        tanh_ffn = common.tanh_ffn
        zero_rows = sb("zero_rows", [P, D])
        base = sb("base", [P, NT, D])
        xt_hi = [sb(f"xt_hi{i}", [P, KC, P], F32R) for i in range(2)]
        xt_lo = [sb(f"xt_lo{i}", [P, KC, P], F32R) for i in range(2)]
        silu = [sb(f"silu{i}", [P, FE]) for i in range(2)]
        h = sb("h", [P, FC * P])
        h_hi = sb("h_hi", [P, FC, P], F32R)
        h_lo = sb("h_lo", [P, FC, P], F32R)
        y = [sb(f"y{i}", [P, D]) for i in range(2)]
        logits = sb("logits", [P, NT, NE])
        score = sb("score", [P, NT, NE])
        stat = sb("stat", [P, NT])
        inv = sb("inv", [P, NT])
        best = sb("best", [P, NT, PAIRS])
        group_gt = sb("group_gt", [P, NT, PAIRS, PAIRS])
        group_eq = sb("group_eq", [P, NT, PAIRS, PAIRS])
        rank = sb("rank", [P, NT, NE])
        gt = sb("gt", [P, NT, NE, NE])
        eq = sb("eq", [P, NT, NE, NE])
        chosen = sb("chosen", [P, NT, NE])
        weight = sb("weight", [P, NT, NE])
        place = sb("place", [P, NT, NE])
        count = sb("count", [P, NE])
        full = sb("full", [P, NE, NT - 1])
        tiles = sb("tiles", [P, NE])
        before = sb("before", [P, NE, NE])
        start = sb("start", [P, NE])
        end = sb("end", [P, NE])
        slot = sb("slot", [P, TOP, NT])
        row = sb("row", [P, NT, 3, TOP], I32)
        expert_gt = sb("expert_gt", [P, ROUTED_TILES + 2, NE])
        expert = sb("expert", [P, ROUTED_TILES + 2])
        free_f = sb("free_f", [P, ROUTED_TILES + 2])
        parity_f = sb("parity_f", [P, ROUTED_TILES + 2])
        t_load = sb("t_load", [P, ROUTED_TILES + 2], I32)
        t_place = sb("t_place", [P, ROUTED_TILES + 2], I32)
        t_new = sb("t_new", [P, ROUTED_TILES + 2], I32)
        t_free = sb("t_free", [P, ROUTED_TILES + 2], I32)
        row_now = sb("row_now", [P, 4, 3, TOP], I32)
        table = sb("table", [P, ROUTED_TILES, 2], I32)
        x_ring = [sb(f"x_ring{i}", [P, D]) for i in range(RING)]
        gather_idx = [sb(f"gather_idx{i}", [P, 1], I32) for i in range(RING)]
        add_idx = [sb(f"add_idx{i}", [P, 1], I32) for i in range(2)]

        gate_bank = [ps(f"gate_bank{i}", [P, 512]) for i in range(2)]
        up_bank = [ps(f"up_bank{i}", [P, 512]) for i in range(2)]
        xt_bank = ps("xt_bank", [P, 512])
        ht_bank = ps("ht_bank", [P, 512])
        y_bank = [ps(f"y_bank{i}", [P, 512]) for i in range(2)]

        const_in, base_in = sem("const_in"), [sem("base_in_first"), sem("base_in_rest")]
        gathered = [sem(f"gathered_{i}") for i in range(RING)]
        pads_out, shared_out = sem("pads_out"), sem("shared_out")
        table_set, scattered, table_in, added = sem("table_set"), sem("scattered"), sem("table_in"), sem("added")
        b_setup, h_padded = sem("b_setup"), sem("h_padded")
        route_step, exp_scores, counted = sem("route_step"), sem("exp_scores"), sem("counted")
        row_copied, idx_copied = sem("row_copied"), sem("idx_copied")
        gate_done, up_done, xt_done, ht_done, down_done = (
            sem("gate_done"), sem("up_done"), sem("xt_done"), sem("ht_done"), sem("down_done"))
        silu_done, xt_hi_done, h_hi_done, logits_copied = (
            sem("silu_done"), sem("xt_hi_done"), sem("h_hi_done"), sem("logits_copied"))
        xt_lo_done, h_done, h_lo_done, y_done = sem("xt_lo_done"), sem("h_done"), sem("h_lo_done"), sem("y_done")

        block = ctx.enter_context(nc.Block())

        def tile_rows(buf, t):
            return buf[bass.ds(P * t, P), :]

        def step_loop(eng, first, last, body):
            with eng.Fori(0, (last - first + 1) // 2) as pair:
                for k in range(2):
                    body(Step(pair + (first + k) // 2, (first + k) % 2))

        def table_value(eng, tab, s, ahead, hi):
            t = s.index + ahead - FIRST_ROUTED
            return eng.value_load(tab[0:1, bass.ds(t, 1)], min_val=0, max_val=hi)

        @block.sync
        def _(sp):
            def load_weights(j):
                wait_alone(sp, b_setup, raw_in, 16 * j)
                wait_alone(sp, b_setup, w_lo_dve, j - 1)
                wait_alone(sp, b_setup, w_lo_pool, 2 * (j - 1))

            def weights_dma(j, place):
                sp.dma_start(w_raw[:, place * WW:(place + 1) * WW], A["experts"][j]).then_inc(raw_in, 16)

            def load_tile(s, t):
                sp.dma_start(x_tile[s.parity][:], tile_rows(xn_buf, t)).then_inc(tile_in[s.parity], 16)

            sp.wait_ge(xn2_out, 16 * B)
            sp.wait_ge(x2_out, 16 * B)
            for k in range(2):
                load_tile(at_step(k), k)
            for k, (lo, hi) in enumerate([(0, BASE_FIRST), (BASE_FIRST, NT)]):
                sp.dma_start(base[:, lo:hi], x2_buf[lo * P:hi * P, :].rearrange("(t p) d -> p t d", p=P)
                             ).then_inc(base_in[k], 16)
            load_weights(1)
            weights_dma(1, 1)

            def first_half(s):
                wait_alone(sp, b_setup, xt_done, s.index + 1)
                load_tile(s, (s.index + 2) % NT if isinstance(s.index, int) else s.index + 2)

            def store_shared(t):
                sp.dma_start(tile_rows(out, t), base[:, bass.ds(t, 1), :].rearrange("p o d -> p (o d)")).then_inc(shared_out, 16)

            def second_half(s):
                wait_alone(sp, b_setup, xt_done, s.index + 1)
                load_tile(s, s.index + 2 - NT)

            for s in range(2):
                first_half(at_step(s))
            load_weights(2)
            weights_dma(2, 0)
            step_loop(sp, 2, NT - 3, first_half)
            first_half(at_step(NT - 2))
            first_half(at_step(NT - 1))
            load_weights(3)
            weights_dma(3, 1)

            def second_and_store(s):
                second_half(s)
                wait_alone(sp, b_setup, y_done, s.index)
                store_shared(s.index - 1 - NT)

            second_half(at_step(NT))
            second_and_store(at_step(NT + 1))
            step_loop(sp, NT + 2, 2 * NT - 3, second_and_store)
            for t in range(NT - 3, NT):
                sp.wait_ge(y_done, NT + t + 1)
                store_shared(t)
            with sp.Fori(2, SHARED // 2 + NE // 2) as pair:
                for k in range(2):
                    load_weights(2 * pair + k)
                    sp.dma_start(w_raw[:, k * WW:(k + 1) * WW], A["experts"][bass.ds(2 * pair + k, 1)].rearrange(
                        "o p w -> (o p) w")).then_inc(raw_in, 16)
            sp.wait_ge(shared_out, 16 * NT)

        @block.gpsimd
        def _(pool):
            pool.dma_start(consts[:], A["consts"]).then_inc(const_in, 16)
            pool.dma_start(row_table, A["no_rows"]).then_inc(table_set, 16)
            pool.memset(ones_mat[:], 1.0).then_inc(b_setup, 1)
            pool.memset(zero_rows[:], 0.0).then_inc(b_setup, 1)
            pool.wait_ge(b_setup, 2)
            pool.dma_start(xn_buf[T:T + P, :], zero_rows[:]).then_inc(pads_out, 16)
            pool.dma_start(out[T:T + P, :], zero_rows[:]).then_inc(added, 16)

            for j in range(1, 3):
                common.split_lo_up_down(pool, j % 2 * WW, j + 1)

            pool.wait_ge(table_set, 16)
            pool.wait_ge(route_step, ROUTE_STEPS)
            with pool.Fori(0, NT // 4) as four:
                wait_alone(pool, b_setup, scattered, 16 * 8 * four)
                pool.tensor_copy(row_now[:], row[:, bass.ds(4 * four, 4)]).then_inc(row_copied, 1)
                wait_alone(pool, b_setup, row_copied, four + 1)
                for t in range(4):
                    for k in range(TOP):
                        pool.indirect_dma_start(
                            out=row_table, out_offset=bass.IndirectOffsetOnAxis(ap=row_now[:, t, 0, k:k + 1], axis=0),
                            in_=row_now[:, t, k + 1, :], in_offset=None).then_inc(scattered, 16)
            pool.wait_ge(scattered, 16 * TOP * NT)
            pool.dma_start(table[:], row_table.rearrange("(t p) w -> p t w", p=P)).then_inc(table_in, 16)
            pool.wait_ge(table_in, 16)
            pool.wait_ge(pads_out, 16)

            def copy_index(dst, tile_number, turn):
                pool.tensor_copy(dst[:], table[:, bass.ds(tile_number, 1), 0]).then_inc(idx_copied, 1)
                wait_alone(pool, b_setup, idx_copied, turn)

            def gather(s, turn):
                at_least(pool, xt_done, s.index + 1 - RING)
                copy_index(gather_idx[s.place], s.index - FIRST_ROUTED, turn)
                pool.indirect_dma_start(out=x_ring[s.place][:], out_offset=None, in_=xn_buf,
                                        in_offset=bass.IndirectOffsetOnAxis(ap=gather_idx[s.place][:, :1], axis=0)
                                        ).then_inc(gathered[s.place], 16)

            def add_rows(s, turn):
                p = (s.parity + 1) % 2
                t = s.index - 1 - FIRST_ROUTED
                at_least(pool, added, 16 * t + 16)
                copy_index(add_idx[p], t, turn)
                wait_alone(pool, b_setup, y_done, s.index)
                pool.indirect_dma_start(out=out, out_offset=bass.IndirectOffsetOnAxis(ap=add_idx[p][:, :1], axis=0),
                                        in_=y[p][:], in_offset=None, compute_op=ALU.add).then_inc(added, 16)

            def split_new(s):
                new = table_value(pool, t_new, s, 2, 1)
                with pool.If(new > 0):
                    count_ = table_value(pool, t_load, s, 2, NE - 1) + SHARED + 1
                    place = table_value(pool, t_place, s, 2, WW)
                    common.split_lo_up_down(pool, place, count_)

            for k in range(RING):
                gather(at_ring(FIRST_ROUTED + k), k + 1)
            for s in (FIRST_ROUTED - 1, FIRST_ROUTED):
                split_new(at_step(s))
            pool.wait_ge(shared_out, 16 * NT)

            def step(s):
                turn = RING + 2 * (s.index - FIRST_ROUTED) - 1
                gather(s.ahead(RING - 1), turn)
                add_rows(s, turn + 1)
                split_new(s)

            last_turns = STEPS - RING - 2
            with pool.Fori(FIRST_ROUTED // RING, last_turns // RING) as turn:
                for k in range(RING):
                    step(RingStep(turn, 1).ahead(k))
            for k in range(last_turns // RING * RING + 1, STEPS - RING + 1):
                step(at_ring(k))
            gathers = RING + 2 * (STEPS - RING - FIRST_ROUTED) + 1
            for k in range(RING):
                add_rows(at_ring(STEPS - RING + 1 + k), gathers + k)
                if STEPS - RING + 1 + k <= STEPS - 3:
                    split_new(at_ring(STEPS - RING + 1 + k))
            pool.wait_ge(added, 16 * (ROUTED_TILES + 1))

        @block.tensor
        def _(pe):

            def products(out_, left, right):
                n = len(left)
                for c in range(n):
                    for k, (a, b) in enumerate([(0, 0), (1, 0), (0, 1)]):
                        last = pe.matmul(out_, left[c][a], right[c][b], start=c == 0 and k == 0,
                                         stop=c == n - 1 and k == 2)
                return last

            def weight_parts(place, at, n):
                return w_hi[:, bass.ds(place + at, n)], w_lo[:, bass.ds(place + at, n)]

            def gate_up(s, place, gate_w, loads):
                if loads is not None:
                    pe.wait_ge(w_lo_dve, loads)
                pe.wait_ge(xt_lo_done, s.index + 1)
                at_least(pe, h_done, s.index - 1)
                left = [(xt_hi[s.parity][:, c, :], xt_lo[s.parity][:, c, :]) for c in range(KC)]
                products(gate_bank[s.parity][:, 0:gate_w], left,
                         [weight_parts(place, c * GATE_W, gate_w) for c in range(KC)]).then_inc(gate_done, 1)
                if loads is not None:
                    pe.wait_ge(w_lo_pool, 2 * loads - 1)
                products(up_bank[s.parity][:, 0:FE], left,
                         [weight_parts(place, UP_AT + c * FE, FE) for c in range(KC)]).then_inc(up_done, 1)

            def transpose_x(s, gather):
                if gather:
                    at_least(pe, gathered[s.place], 16 * (s.turn - FIRST_ROUTED // RING + 1))
                    x = x_ring[s.place]
                else:
                    at_least(pe, tile_in[s.parity], 16 * (s.pair + 1))
                    x = x_tile[s.parity]
                at_least(pe, xt_lo_done, s.index)
                for c in range(KC):
                    last = pe.transpose(xt_bank[:, c * P:(c + 1) * P], x[:, c * P:(c + 1) * P], ident[:])
                last.then_inc(xt_done, 1)

            def transpose_h(s):
                pe.wait_ge(h_done, s.index + 1)
                at_least(pe, h_lo_done, s.index)
                for c in range(FC):
                    last = pe.transpose(ht_bank[:, c * P:(c + 1) * P], h[:, c * P:(c + 1) * P], ident[:])
                last.then_inc(ht_done, 1)

            def down(s, place):
                pe.wait_ge(h_lo_done, s.index + 1)
                at_least(pe, y_done, s.index - 1)
                products(y_bank[s.parity][:], [(h_hi[:, c, :], h_lo[:, c, :]) for c in range(FC)],
                         [weight_parts(place, DOWN_AT + c * D, D) for c in range(FC)]).then_inc(down_done, 1)

            def step(s, place, place_before, gate_w=FE, loads=None, gather=False, first=False, last=False):
                gate_up(s, place, gate_w, loads)
                if not last:
                    transpose_x(s.ahead(1), gather)
                if not first:
                    if loads is not None:
                        pe.wait_ge(w_lo_pool, 2 * loads)
                    down(s.ahead(-1), place_before)
                transpose_h(s)

            def places(s):
                return table_value(pe, t_load, s, 0, NE - 1) + SHARED + 1, table_value(pe, t_place, s, 0, WW)

            kept = [pe.alloc_register(name) for name in ("place_before", "loads_now", "place_now")]

            def keep(before, loads, place):
                for register, value in zip(kept, (before, loads, place)):
                    pe.reg_mov(register, value)

            def routed(first, n):
                before, loads, place = [pe.snap(r, min_val=0, max_val=m) for r, m in zip(kept, (WW, SHARED + NE, WW))]
                for k in range(n):
                    s = first.ahead(k)
                    after = places(s.ahead(1))
                    step(s, place, before, loads=loads, gather=True)
                    before, (loads, place) = place, after
                keep(before, loads, place)

            transpose_x(at_step(0), False)
            step(at_step(0), 0, 0, GATE_W, 1, first=True)
            for s in (1, 2):
                step(at_step(s), 0, 0, GATE_W, 1)
            step_loop(pe, 3, NT - 2, lambda s: step(s, 0, 0, GATE_W))
            step(at_step(NT - 1), 0, 0, GATE_W)
            step(at_step(NT), WW, 0, loads=2)

            pe.wait_ge(route_step, CHOSEN_STEP)
            pe.wait_ge(b_setup, 2)
            ranks = ht_bank[:, 0:NT * NE]
            flat = chosen[:].rearrange("p t e -> p (t e)")
            pe.matmul(ranks, consts[:, 0:P], flat, start=True, stop=False, skip_group_check=True)
            for t in range(NT - 1):
                n = NT - 1 - t
                pe.matmul(ht_bank[:, (t + 1) * NE:NT * NE].rearrange("p (t e) -> p t e", e=NE), ones_mat[:],
                          chosen[:, t:t + 1, :].to_broadcast([P, n, NE]), start=False, stop=t == NT - 2,
                          skip_group_check=True)
            for t in range(NT):
                last = pe.matmul(ht_bank[:, NT * NE:NT * NE + NE], ones_mat[:], chosen[:, t, :], start=t == 0,
                                 stop=t == NT - 1, skip_group_check=True)
            last.then_inc(counted, 1)

            step_loop(pe, NT + 1, 2 * NT - 2, lambda s: step(s, WW, WW))
            pe.wait_ge(route_step, ROUTE_STEPS)
            step(at_ring(2 * NT - 1), WW, WW, gather=True)
            s = at_ring(FIRST_ROUTED)
            step(s, 0, WW, loads=SHARED + 1, gather=True)
            keep(0, *places(at_ring(FIRST_ROUTED + 1)))
            with pe.Fori(FIRST_ROUTED // RING, (STEPS - 3) // RING) as turn:
                routed(RingStep(turn, 1), RING)
            s = at_ring(STEPS - 2)
            before, loads, place = [pe.snap(r, min_val=0, max_val=m) for r, m in zip(kept, (WW, SHARED + NE, WW))]
            last_loads, last_place = places(s.ahead(1))
            step(s, place, before, loads=loads, gather=True)
            step(s.ahead(1), last_place, place, loads=last_loads, last=True)
            down(s.ahead(1), last_place)

        @block.scalar
        def _(act):
            def split(j):
                act.wait_ge(raw_in, 16 * (j + 1))
                for k in range(3):
                    common.split_hi(act, j % 2 * WW, k)

            def x_hi(s):
                act.wait_ge(xt_done, s.index + 1)
                at_least(act, up_done, s.index - 1)
                act.activation(xt_hi[s.parity][:].rearrange("p c q -> p (c q)"), xt_bank[:], ACT.Copy).then_inc(xt_hi_done, 1)

            def gate(s, with_logits):
                act.wait_ge(gate_done, s.index + 1)
                if with_logits:
                    act.activation(logits[:, bass.ds(s.index, 1), :].rearrange("p o e -> p (o e)"),
                                   gate_bank[s.parity][:, FE:GATE_W], ACT.Copy).then_inc(logits_copied, 1)
                at_least(act, h_done, s.index - 1)
                act.activation(silu[s.parity][:], gate_bank[s.parity][:, 0:FE], ACT.Silu).then_inc(silu_done, 1)

            def hidden_hi(s):
                act.wait_ge(ht_done, s.index + 1)
                at_least(act, down_done, s.index)
                act.activation(h_hi[:].rearrange("p c q -> p (c q)"), ht_bank[:, 0:FC * P], ACT.Copy).then_inc(h_hi_done, 1)

            def split_new(s):
                new = table_value(act, t_new, s, 2, 1)
                with act.If(new > 0):
                    count_ = table_value(act, t_load, s, 2, NE - 1) + SHARED + 1
                    place = table_value(act, t_place, s, 2, WW)
                    free = table_value(act, t_free, s, 2, STEPS)
                    act.wait_ge(down_done, free)
                    act.wait_ge(raw_in, 16 * count_)
                    for k in range(3):
                        common.split_hi(act, place, k)

            def step(s, with_logits=False, new=False, last=False):
                gate(s, with_logits)
                if not last:
                    x_hi(s.ahead(1))
                hidden_hi(s)
                if new:
                    split_new(s)

            x_hi(at_step(0))
            step(at_step(0), with_logits=True)
            step_loop(act, 1, NT - 2, lambda s: step(s, with_logits=True))
            split(1)
            step(at_step(NT - 1), with_logits=True)
            step(at_step(NT))
            act.wait_ge(route_step, 2)
            act.activation(score[:], score[:], ACT.Exp).then_inc(exp_scores, 1)
            act.wait_ge(down_done, NT)
            split(2)
            step_loop(act, NT + 1, 2 * NT - 2, step)
            act.wait_ge(route_step, ROUTE_STEPS)
            step(at_step(2 * NT - 1), new=True)
            step(at_step(2 * NT), new=True)
            step_loop(act, FIRST_ROUTED + 1, STEPS - 3, lambda s: step(s, new=True))
            step(at_step(STEPS - 2))
            step(at_step(STEPS - 1), last=True)

        @block.vector
        def _(dve):
            dve.memset(h[:, FE:FC * P], 0.0).then_inc(h_padded, 1)

            def split_new(s):
                new = table_value(dve, t_new, s, 2, 1)
                with dve.If(new > 0):
                    count_ = table_value(dve, t_load, s, 2, NE - 1) + SHARED + 1
                    place = table_value(dve, t_place, s, 2, WW)
                    common.split_lo_gate(dve, place, count_)

            def x_lo(s):
                dve.wait_ge(xt_hi_done, s.index + 1)
                dve.tensor_tensor(xt_lo[s.parity][:].rearrange("p c q -> p (c q)"), xt_bank[:],
                                  xt_hi[s.parity][:].rearrange("p c q -> p (c q)").bitcast(F32),
                                  ALU.subtract).then_inc(xt_lo_done, 1)

            def hidden(s):
                dve.wait_ge(silu_done, s.index + 1)
                dve.wait_ge(up_done, s.index + 1)
                at_least(dve, ht_done, s.index)
                dve.tensor_tensor(h[:, 0:FE], up_bank[s.parity][:, 0:FE], silu[s.parity][:], ALU.mult).then_inc(h_done, 1)

            def hidden_lo(s):
                dve.wait_ge(h_hi_done, s.index + 1)
                dve.tensor_tensor(h_lo[:].rearrange("p c q -> p (c q)"), ht_bank[:, 0:FC * P],
                                  h_hi[:].rearrange("p c q -> p (c q)").bitcast(F32), ALU.subtract).then_inc(h_lo_done, 1)

            def shared_y(s, t, second):
                dve.wait_ge(down_done, s.index + 1)
                if second:
                    at_least(dve, y_done, s.index + 1 - NT)
                rows = base[:, bass.ds(t, 1), :].rearrange("p o d -> p (o d)")
                dve.scalar_tensor_tensor(rows, y_bank[s.parity][:], tanh_ffn[:, 0:1], rows, ALU.mult, ALU.add).then_inc(y_done, 1)

            def routed_y(s):
                dve.wait_ge(down_done, s.index + 1)
                at_least(dve, added, 16 * (s.index - FIRST_ROUTED))
                t = s.index - FIRST_ROUTED
                dve.tensor_scalar(y[s.parity][:], y_bank[s.parity][:], table[:, bass.ds(t, 1), 1].bitcast(F32), None,
                                  ALU.mult).then_inc(y_done, 1)

            def step(s, finish_before, new=False, last=False):
                hidden(s)
                if not last:
                    x_lo(s.ahead(1))
                if finish_before is not None:
                    finish_before(s.ahead(-1))
                hidden_lo(s)
                if new:
                    split_new(s)

            def route():
                done = 0

                def then(ins):
                    nonlocal done
                    ins.then_inc(route_step, 1)
                    done += 1
                    dve.wait_ge(route_step, done)

                def tri(at, n):
                    return consts[:, at:at + n * n].rearrange("p (i j) -> p i j", i=n).unsqueeze(1).to_broadcast([P, NT, n, n])

                dve.wait_ge(const_in, 16)
                dve.wait_ge(logits_copied, NT)
                then(dve.tensor_reduce(stat[:], logits[:], AX.X, ALU.max))
                then(dve.tensor_tensor(score[:], logits[:], stat[:].unsqueeze(2).to_broadcast([P, NT, NE]), ALU.subtract))
                dve.wait_ge(exp_scores, 1)
                then(dve.tensor_reduce(stat[:], score[:], AX.X, ALU.add))
                then(dve.reciprocal(inv[:], stat[:]))
                then(dve.tensor_tensor(score[:], score[:], inv[:].unsqueeze(2).to_broadcast([P, NT, NE]), ALU.mult))
                pairs = score[:].rearrange("p t (g e) -> p t g e", e=2)
                then(dve.tensor_tensor(best[:], pairs[:, :, :, 0], pairs[:, :, :, 1], ALU.max))
                shape = [P, NT, PAIRS, PAIRS]
                mine, other = best[:].unsqueeze(3).to_broadcast(shape), best[:].unsqueeze(2).to_broadcast(shape)
                then(dve.tensor_tensor(group_gt[:], other, mine, ALU.is_gt))
                then(dve.tensor_tensor(group_eq[:], other, mine, ALU.is_equal))
                then(dve.tensor_tensor(group_eq[:], group_eq[:], tri(C_TRI4, PAIRS), ALU.mult))
                then(dve.tensor_tensor(group_gt[:], group_gt[:], group_eq[:], ALU.add))
                then(dve.tensor_reduce(best[:], group_gt[:], AX.X, ALU.add))
                then(dve.tensor_scalar(best[:], best[:], float(TOP), None, ALU.is_lt))
                then(dve.tensor_tensor(pairs, pairs, best[:].unsqueeze(3).to_broadcast([P, NT, PAIRS, 2]), ALU.mult))
                shape = [P, NT, NE, NE]
                mine, other = score[:].unsqueeze(3).to_broadcast(shape), score[:].unsqueeze(2).to_broadcast(shape)
                then(dve.tensor_tensor(gt[:], other, mine, ALU.is_gt))
                then(dve.tensor_tensor(eq[:], other, mine, ALU.is_equal))
                then(dve.tensor_tensor(eq[:], eq[:], tri(C_TRI, NE), ALU.mult))
                then(dve.tensor_tensor(gt[:], gt[:], eq[:], ALU.add))
                then(dve.tensor_reduce(rank[:], gt[:], AX.X, ALU.add))
                then(dve.tensor_scalar(chosen[:], rank[:], float(TOP), None, ALU.is_lt))
                assert done == CHOSEN_STEP
                then(dve.scalar_tensor_tensor(weight[:], score[:], tanh_ffn[:, 0:1], chosen[:], ALU.mult, ALU.mult))
                dve.wait_ge(counted, 1)
                then(dve.tensor_copy(count[:], ht_bank[:, NT * NE:NT * NE + NE]))
                shape = [P, NE, NT - 1]
                then(dve.tensor_tensor(full[:], count[:].unsqueeze(2).to_broadcast(shape),
                                       consts[:, C_FULL:C_FULL + NT - 1].unsqueeze(1).to_broadcast(shape), ALU.is_gt))
                then(dve.tensor_reduce(tiles[:], full[:], AX.X, ALU.add))
                then(dve.tensor_scalar(tiles[:], tiles[:], 1.0, None, ALU.add))
                then(dve.tensor_tensor(before[:], tiles[:].unsqueeze(1).to_broadcast([P, NE, NE]),
                                       consts[:, C_TRI:C_TRI + NE * NE].rearrange("p (i j) -> p i j", i=NE), ALU.mult))
                then(dve.tensor_reduce(start[:], before[:], AX.X, ALU.add))
                then(dve.tensor_tensor(end[:], start[:], tiles[:], ALU.add))
                then(dve.tensor_scalar(start[:], start[:], float(P), None, ALU.mult))
                then(dve.tensor_tensor(place[:], ht_bank[:, 0:NT * NE].rearrange("p (t e) -> p t e", e=NE),
                                       start[:].unsqueeze(1).to_broadcast([P, NT, NE]), ALU.add))
                then(dve.tensor_tensor(rank[:], place[:], chosen[:], ALU.mult))
                then(dve.tensor_reduce(slot[:, 1], rank[:], AX.X, ALU.max))
                then(dve.scalar_tensor_tensor(rank[:], place[:], -float(SLOT_ROWS), chosen[:], ALU.add, ALU.mult))
                then(dve.tensor_reduce(slot[:, 0], rank[:], AX.X, ALU.min))
                then(dve.tensor_scalar(slot[:, 0], slot[:, 0], float(SLOT_ROWS), None, ALU.add))
                for k in range(TOP):
                    then(dve.tensor_copy(row[:, :, 0, k], slot[:, k]))
                    then(dve.tensor_copy(row[:, :, 1 + k, 0], consts[:, C_TOK:C_TOK + NT]))
                    then(dve.tensor_tensor(rank[:], place[:], slot[:, k].unsqueeze(2).to_broadcast([P, NT, NE]), ALU.is_equal))
                    then(dve.tensor_tensor(rank[:], rank[:], weight[:], ALU.mult))
                    then(dve.tensor_reduce(row[:, :, 1 + k, 1].bitcast(F32), rank[:], AX.X, ALU.add))
                n = ROUTED_TILES + 2
                shape = [P, n, NE]
                tile_number = consts[:, C_TILE:C_TILE + n]
                then(dve.tensor_tensor(expert_gt[:, :, 0:NE - 1], tile_number.unsqueeze(2).to_broadcast([P, n, NE - 1]),
                                       end[:, 0:NE - 1].unsqueeze(1).to_broadcast([P, n, NE - 1]), ALU.is_ge))
                then(dve.tensor_reduce(expert[:], expert_gt[:, :, 0:NE - 1], AX.X, ALU.add))
                then(dve.tensor_copy(t_load[:], expert[:]))
                then(dve.tensor_scalar(parity_f[:], expert_gt[:, :, 0], float(WW), None, ALU.mult))
                for e in range(1, NE - 1):
                    then(dve.scalar_tensor_tensor(parity_f[:], expert_gt[:, :, e], float(WW if e % 2 == 0 else -WW),
                                                  parity_f[:], ALU.mult, ALU.add))
                then(dve.tensor_copy(t_place[:], parity_f[:]))
                then(dve.memset(t_new[:, 0:1], 0))
                then(dve.tensor_tensor(t_new[:, 1:n], expert[:, 1:n], expert[:, 0:n - 1], ALU.is_gt))
                then(dve.tensor_scalar(free_f[:], expert_gt[:, :, 0], float(NT), float(NT), ALU.mult, ALU.add))
                for e in range(1, NE - 1):
                    then(dve.scalar_tensor_tensor(free_f[:], expert_gt[:, :, e], tiles[:, e - 1:e], free_f[:],
                                                  ALU.mult, ALU.add))
                then(dve.tensor_copy(t_free[:], free_f[:]))
                assert done == ROUTE_STEPS, done

            def first_half(s):
                shared_y(s, s.index, False)

            def second_half(s):
                shared_y(s, s.index - NT, True)

            x_lo(at_step(0))
            dve.wait_ge(h_padded, 1)
            step(at_step(0), None)
            dve.wait_ge(base_in[0], 16)
            for s in range(1, BASE_FIRST + 1):
                step(at_step(s), first_half)
            dve.wait_ge(base_in[1], 16)
            step_loop(dve, BASE_FIRST + 1, NT - 2, lambda s: step(s, first_half))
            common.split_lo_gate(dve, WW, 2)
            step(at_step(NT - 1), first_half)
            step(at_step(NT), first_half)
            route()
            common.split_lo_gate(dve, 0, 3)
            step_loop(dve, NT + 1, 2 * NT - 2, lambda s: step(s, second_half))
            step(at_step(2 * NT - 1), second_half, new=True)
            step(at_step(2 * NT), second_half, new=True)
            dve.wait_ge(table_in, 16)
            step_loop(dve, FIRST_ROUTED + 1, STEPS - 3, lambda s: step(s, routed_y, new=True))
            step(at_step(STEPS - 2), routed_y)
            step(at_step(STEPS - 1), routed_y, last=True)
            routed_y(at_step(STEPS - 1))


def layout(i):
    import numpy as np

    def c(a):
        return np.ascontiguousarray(a)

    def wide(w):
        n = -(-w.shape[0] // P) * P
        full = np.zeros((n, w.shape[1]), np.float32)
        full[:w.shape[0]] = w
        return full.reshape(n // P, P, -1).transpose(1, 0, 2)

    def expert(gate, up, down_w, router=None):
        router = np.zeros((NE, D), np.float32) if router is None else router
        return np.concatenate([wide(np.concatenate([gate, router]).T).reshape(P, -1), wide(up.T).reshape(P, -1),
                               wide(down_w.T).reshape(P, -1)], axis=1)

    f = {}
    f["x"] = c(i["x"].reshape(T, D))
    f["ctxT"] = c(i["ctx_2048"].reshape(T, D).T)
    causal, pad = i["mask_SxS2_bc0"], i["mask_BxS2_bk0"]
    f["causal"], f["causalT"], f["pad"], f["padT"] = c(causal), c(causal.T), c(pad), c(pad.T)
    wq = i["L0_xattn_Wq"].reshape(G, R, HD, D).transpose(1, 0, 2, 3).reshape(D, D)
    f["wqkv"] = c(wide(np.concatenate([wq, i["L0_xattn_Wk"], i["L0_xattn_Wv"]]).T).reshape(P, -1))
    wo = i["L0_xattn_Wo"].T.reshape(2, G // 2, R, HD, D).transpose(0, 2, 1, 3, 4).reshape(D, D)
    f["wo"] = c(wide(wo).reshape(P, -1))
    f["bq"] = c(i["L0_xattn_bq"].reshape(G, R, HD).transpose(0, 2, 1).reshape(P, R))
    f["bk"], f["bv"] = c(i["L0_xattn_bk"].reshape(P, 1)), c(i["L0_xattn_bv"].reshape(P, 1))
    f["bo"], f["g_xattn"], f["g_ffn"] = c(i["L0_xattn_bo"]), c(i["g_xattn"]), c(i["g_ffn"])
    odd = np.arange(P) // HD % 2
    f["parity"] = c(np.stack([1 - odd, odd], 1).astype(np.float32))
    sg, su, sd = i["L0_ffn_sh_gate_w"], i["L0_ffn_sh_up_w"], i["L0_ffn_sh_down_w"]
    packed = [expert(sg[k * FE:(k + 1) * FE], su[k * FE:(k + 1) * FE], sd[:, k * FE:(k + 1) * FE],
                     i["L0_ffn_gate_weight"] if k == 0 else None) for k in range(SHARED)]
    packed += [expert(i["L0_ffn_gate_w"][e], i["L0_ffn_up_w"][e], i["L0_ffn_down_w"][e]) for e in range(NE)]
    f["experts"] = c(np.stack(packed))
    row = np.concatenate([np.tri(NE, k=-1).ravel(), np.tri(PAIRS, k=-1).ravel(), P * np.arange(1, NT),
                          np.arange(ROUTED_TILES + 2)])
    f["consts"] = c(np.concatenate([np.tri(P, k=-1).T, np.tile(row, (P, 1)),
                                    np.arange(P)[:, None] + P * np.arange(NT)[None]], axis=1).astype(np.float32))
    spare = T + np.arange(SLOT_ROWS) % P
    f["no_rows"] = c(np.stack([spare, np.zeros(SLOT_ROWS)], 1).astype(np.int32))
    return f


def kernel(**inputs):
    import numpy as np
    import concourse.bacc as bacc
    from concourse.bass_utils import run_bass_kernel_spmd

    nc = bacc.Bacc("TRN2", target_bir_lowering=False, num_devices=1)
    laid = layout({name: np.asarray(a) for name, a in inputs.items()})
    arrays, A = {}, {}
    for name, a in laid.items():
        arrays[f"in_{name}_dram"] = a
        A[name] = nc.dram_tensor(f"in_{name}_dram", a.shape, mybir.dt.from_np(a.dtype), kind="ExternalInput").ap()
    out = nc.dram_tensor("out_0_dram", (T + P, D), F32, kind="ExternalOutput").ap()
    build_kernel(nc, A, out)
    r = run_bass_kernel_spmd(nc, [arrays], core_ids=[0])
    return r.results[0]["out_0_dram"][:T].reshape(B, S, D)
```

```python
from contextlib import ExitStack

import concourse.bass as bass
from concourse import mybir

F32 = mybir.dt.float32
F32R = mybir.dt.float32r
BF16 = mybir.dt.bfloat16
I32 = mybir.dt.int32
U8 = mybir.dt.uint8
ALU = mybir.AluOpType
ACT = mybir.ActivationFunctionType
AX = mybir.AxisListType

P = 128
B, S, D = 8, 256, 512
T = B * S
QC = S // P
KC = D // P
G, R, HD = 8, 4, 16
GP = G // 2
H = G * R
PAIR = 2 * HD
AUX = 3 * PAIR
NEG = -1e30
EPS = 1e-5
RSQRT_MAGIC = float(0x5F3759DF)
STAT_STEPS = 7
PREP_STAT_SLOTS, TAIL_STAT_SLOTS = (16, 17, 18, 19, 20, 21, 22), (30, 32, 33, 34, 35, 35, 36)
NEWTON = 12
NORM_STEPS = NEWTON + QC

SCORE_UNITS = GP * R * QC
PROB_UNITS = G * QC * R // 2
PROB_LAG = 3
PV_LAG = PROB_LAG + 5
SLOTS = PV_LAG + 4 * 7 + 2
POOL_SETUP = 11
STACK_DMAS = 13

NE, TOP, FE = 8, 2, 352
PAIRS = NE // 2
NT = T // P
GATE_W = FE + NE
UP_AT = KC * GATE_W
DOWN_AT = UP_AT + KC * FE
FC = -(-FE // P)
WW = DOWN_AT + FC * D
PARTS = ((0, UP_AT), (UP_AT, DOWN_AT), (DOWN_AT, WW))
SHARED = 2
ROUTED_TILES = T * TOP // P + NE - 1
FIRST_ROUTED = SHARED * NT
STEPS = FIRST_ROUTED + ROUTED_TILES
SLOT_ROWS = ROUTED_TILES * P
C_TRI = P
C_TRI4 = C_TRI + NE * NE
C_FULL = C_TRI4 + PAIRS * PAIRS
C_TILE = C_FULL + NT - 1
C_TOK = C_TILE + ROUTED_TILES + 2
CONSTS = C_TOK + NT


def at_least(eng, sem, value):
    if isinstance(value, int) and value <= 0:
        return
    eng.wait_ge(sem, value)


def wait_alone(eng, over, sem, value):
    if isinstance(value, int):
        at_least(eng, sem, value)
        return
    count = eng.to_reg(value)
    eng.wait_ge(over, 1)
    eng.wait_ge(sem, count)


class Batch:

    def __init__(self, pair, parity):
        self.pair, self.parity = pair, parity
        self.index = 2 * pair + parity

    def ahead(self, k):
        return Batch(self.pair + (self.parity + k) // 2, (self.parity + k) % 2)


class Common:

    def __init__(self, nc, stack):
        def sb(name, shape, dt=F32):
            return stack.enter_context(nc.sbuf_tensor(name, shape, dt))

        self.sem = lambda name: stack.enter_context(nc.semaphore(name))
        self.ident = sb("ident", [P, P])
        self.w_raw = sb("w_raw", [P, 2 * WW])
        self.w_hi = sb("w_hi", [P, 2 * WW], F32R)
        self.w_lo = sb("w_lo", [P, 2 * WW], F32R)
        self.tanh_ffn = sb("tanh_ffn", [P, 1])
        self.x2_out, self.xn2_out = self.sem("x2_out"), self.sem("xn2_out")
        self.raw_in = self.sem("raw_in")
        self.tile_in = [self.sem("tile_in_a"), self.sem("tile_in_b")]
        self.w_hi_done, self.w_lo_dve, self.w_lo_pool = self.sem("w_hi_done"), self.sem("w_lo_dve"), self.sem("w_lo_pool")

    def split_hi(self, act, place, k):
        lo, hi = PARTS[k]
        words = bass.ds(place + lo, hi - lo)
        act.activation(self.w_hi[:, words], self.w_raw[:, words], ACT.Copy).then_inc(self.w_hi_done, 1)

    def split_lo(self, eng, place, k, done):
        lo, hi = PARTS[k]
        words = bass.ds(place + lo, hi - lo)
        eng.tensor_tensor(self.w_lo[:, words], self.w_raw[:, words], self.w_hi[:, words].bitcast(F32),
                          ALU.subtract).then_inc(done, 1)

    def split_lo_gate(self, dve, place, number):
        dve.wait_ge(self.w_hi_done, 3 * number - 2)
        self.split_lo(dve, place, 0, self.w_lo_dve)

    def split_lo_up_down(self, pool, place, number):
        for k in (1, 2):
            pool.wait_ge(self.w_hi_done, 3 * number - 2 + k)
            self.split_lo(pool, place, k, self.w_lo_pool)


def build_kernel(nc, A, out):
    x2_buf = nc.dram_tensor("x2_buf", (T, D), F32, kind="Internal").ap()
    xn_buf = nc.dram_tensor("xn_buf", (T + P, D), F32, kind="Internal").ap()
    with ExitStack() as stack:
        common = Common(nc, stack)
        attention_phase(nc, A, x2_buf, xn_buf, common)
        expert_phase(nc, A, x2_buf, xn_buf, out, common)


def attention_phase(nc, A, x2_buf, xn_buf, common):
    with ExitStack() as ctx:
        def sb(name, shape, dt=F32):
            return ctx.enter_context(nc.sbuf_tensor(name, shape, dt))

        def ps(name, shape):
            return ctx.enter_context(nc.psum_tensor(name, shape, F32))

        sem = common.sem

        def part(buf, at, *shape):
            dims = dict(zip("abcd", shape))
            names = " ".join(dims)
            n = 1
            for size in shape:
                n *= size
            return buf[:, at:at + n].rearrange(f"p ({names}) -> p {names}", **dims)

        identf = common.ident
        identb = part(common.w_raw, WW + 4 * QC * D + QC * H, P // 2).bitcast(BF16)
        tanh_gate = sb("tanh_gate", [P, 1])
        bo_gated = sb("bo_gated", [P, D])
        bq = sb("bq", [P, R])
        bk = sb("bk", [P, 1])
        parity = sb("parity", [P, 2])
        bv = sb("bv", [P, 1])
        wqkv_hi = part(common.w_hi, 0, KC, 768)
        wqkv_lo = part(common.w_lo, 0, KC, 768)
        wo_hi = part(common.w_lo, WW, KC, D)
        wo_lo = part(common.w_lo, WW + KC * D, KC, D)
        causal_raw = part(common.w_raw, WW + 3 * QC * D, 2 * QC * S // 4).bitcast(U8).rearrange(
            "p (a c s) -> p a c s", a=2, c=QC)
        causal_neg = sb("causal_neg", [P, QC, S], BF16)
        causalT_neg = sb("causalT_neg", [P, QC, S], BF16)
        pad_raw = part(common.w_raw, 2 * QC * D + KC * S + 3 * S, B * S // 4).bitcast(U8).rearrange(
            "p (b s) -> p b s", b=B)
        pad_neg = sb("pad_neg", [P, B, S], BF16)
        padT_raw = sb("padT_raw", [P, QC, B], U8)
        padT_neg = sb("padT_neg", [P, QC, B], BF16)
        xt = part(common.w_raw, 0, QC, D)
        ln_stats = sb("ln_stats", [P, 2, QC, 6])
        ln_mv = sb("ln_mv", [P, 2, QC, 2])
        ln_var = sb("ln_var", [P, 2, QC])
        ln_y = sb("ln_y", [P, 2, QC])
        ln_t = sb("ln_t", [P, 2, QC])
        xn = part(common.w_raw, QC * D, QC, D)
        xT_hi = part(common.w_hi, KC * 768, KC, S)
        xT_lo = part(common.w_lo, KC * 768, KC, S)
        cT_raw = part(common.w_raw, 2 * QC * D, KC, S)
        cT_hi = part(common.w_hi, WW, KC, S)
        cT_lo = part(common.w_hi, WW + KC * S, KC, S)
        q_hi = part(common.w_hi, WW + 2 * KC * S, R, S)
        q_lo = part(common.w_hi, WW + 2 * KC * S + R * S, R, S)
        k_raw = part(common.w_raw, 2 * QC * D + KC * S, S)
        k_hi = sb("k_hi", [P, 2, S], F32R)
        k_lo = sb("k_lo", [P, 2, S], F32R)
        vT = part(common.w_raw, 2 * QC * D + KC * S + S, S)
        v_stage = part(common.w_raw, 2 * QC * D + KC * S + 2 * S, QC, G, HD)
        q_stack = [sb(f"q_stack{i}", [P, GP, R, S], F32R) for i in range(2)]
        k_stack = [sb(f"k_stack{i}", [P, GP, 2, S], F32R) for i in range(2)]
        v_ones = [sb(f"v_ones{i}", [P, QC, G, 2 * HD]) for i in range(2)]
        mask = [sb(f"mask{i}", [P, QC, S], BF16) for i in range(2)]
        maskT = [sb(f"maskT{i}", [P, QC, S], BF16) for i in range(2)]
        row_max = part(common.w_raw, WW + 4 * QC * D, QC, H)
        neg_max = part(common.w_hi, WW + 2 * (KC + R) * S, QC, 2, 2, H // 2)
        neg_maxT = part(common.w_lo[0:2 * H], WW + 2 * KC * D, S)
        probs = sb("probs", [P, 8, 512])
        mixed = [sb(f"mixed{i}", [P, 4, 512]) for i in range(2)]
        inv_sum = sb("inv_sum", [P, R, 4])
        attn = part(common.w_raw, WW, QC, D)
        aT_hi = sb("aT_hi", [P, KC, P], F32R)
        aT_lo = sb("aT_lo", [P, KC, P], F32R)
        x_res = part(common.w_raw, WW + QC * D, QC, D)
        x2 = part(common.w_raw, WW + 2 * QC * D, QC, D)
        xn2 = part(common.w_raw, WW + 3 * QC * D, QC, D)

        ones = probs[0:2, 6:8, :].rearrange("p a b -> p (a b)").rearrange(
            "p (g s) -> p g s", g=GP)
        zeros = k_stack[0][AUX + 4:AUX + 8].rearrange("p g h s -> p (g h s)").rearrange(
            "p (g r s) -> p g r s", g=GP // 2, r=R)

        score_bank = [ps(f"score_bank{i}", [P, 2, S]) for i in range(2)]
        prob_bank = [ps(f"prob_bank{i}", [P, 2, S]) for i in range(2)]
        pv_bank = ps("pv_bank", [P, 512])
        front_bank = [ps(f"front_bank{i}", [P, 512]) for i in range(2)]
        tail_bank = ps("tail_bank", [P, 512])

        wqkv_in, wo_in, consts_in, masks_in = sem("wqkv_in"), sem("wo_in"), sem("consts_in"), sem("masks_in")
        ones_in = sem("ones_in")
        x_in, ctx_in, res_in = sem("x_in"), sem("ctx_in"), sem("res_in")
        stack_in = [sem("stack_in_a"), sem("stack_in_b")]
        max_in = sem("max_in")
        x2_out, xn2_out = common.x2_out, common.xn2_out
        pool_setup, mask_setup = sem("pool_setup"), sem("mask_setup")
        dve_setup, act_setup = sem("dve_setup"), sem("act_setup")
        front_done, scores_done, maxT_done = sem("front_done"), sem("scores_done"), sem("maxT_done")
        probs_scored, pv_done, tail_done = sem("probs_scored"), sem("pv_done"), sem("tail_done")
        ln1_stat, xT_lo_done, q_lo_done, k_lo_done = sem("ln1_stat"), sem("xT_lo_done"), sem("q_lo_done"), sem("k_lo_done")
        maxima_done, max_split = sem("maxima_done"), sem("max_split")
        tail_step, ln2_stat = sem("tail_step"), sem("ln2_stat")
        xT_hi_done, q_hi_done, kv_copied, v_staged = sem("xT_hi_done"), sem("q_hi_done"), sem("kv_copied"), sem("v_staged")
        exp_done, mixed_done, maxT_copied, aT_hi_done = sem("exp_done"), sem("mixed_done"), sem("maxT_copied"), sem("aT_hi_done")
        ln1_step, ln2_step = sem("ln1_step"), sem("ln2_step")
        ctx_split, mask_done, maskT_done, res_done, v_ready = (
            sem("ctx_split"), sem("mask_done"), sem("maskT_done"), sem("res_done"), sem("v_ready"))

        block = ctx.enter_context(nc.Block())

        def rows(buf, batch):
            return buf[bass.ds(S * batch.index, S), :].rearrange("(c p) d -> p c d", p=P)

        def copy_rows(eng, dst, src):
            return eng.dma_start(dst.bitcast(F32), src.bitcast(F32))

        def pipeline(iteration, eng):
            def part(n):
                return dict(prep=0 <= n + 3 < B, front=0 <= n + 2 < B, score=0 <= n + 1 < B, soft=0 <= n < B,
                            tail=0 <= n - 1 < B)
            for n in (-3, -2, -1, 0):
                iteration(Batch(n // 2, n % 2), **part(n))
            with eng.Fori(0, B // 2 - 2) as pair:
                for k in (1, 2):
                    iteration(Batch(pair, 0).ahead(k), prep=True, front=True, score=True, soft=True, tail=True)
            for n in (B - 3, B - 2, B - 1, B):
                iteration(Batch(n // 2, n % 2), **part(n))

        @block.sync
        def _(sp):
            wqkv_raw = probs[:, 0:6, :].rearrange("p a b -> p (a b)")
            wo_raw = mixed[0][:].rearrange("p a b -> p (a b)")
            
            def constants():
                sp.dma_start(wqkv_raw, A["wqkv"]).then_inc(wqkv_in, 16)
                sp.dma_start(wo_raw, A["wo"]).then_inc(wo_in, 16)
                sp.wait_ge(pool_setup, POOL_SETUP)
                for i in range(2):
                    for g2 in range(2):
                        copy_rows(sp, k_stack[i][AUX + 2 * g2:AUX + 2 * g2 + 2, :, g2, :], ones).then_inc(ones_in, 16)
                sp.wait_ge(ones_in, 64)

            def stack(m, half):
                if half == 0:
                    wait_alone(sp, pool_setup, q_lo_done, R * (m.index + 1))
                    wait_alone(sp, pool_setup, k_lo_done, 2 * (m.index + 1))
                wait_alone(sp, pool_setup, probs_scored, PROB_UNITS * (m.index - 2) + PROB_UNITS // 2 * (half + 1))
                qs, ks = q_stack[m.parity], k_stack[m.parity]
                for gp in range(GP // 2 * half, GP // 2 * (half + 1)):
                    src = slice(PAIR * gp, PAIR * (gp + 1))
                    for part, (q, k) in enumerate([(q_hi, k_hi), (q_hi, k_lo), (q_lo, k_hi)]):
                        dst = slice(PAIR * part, PAIR * (part + 1))
                        copy_rows(sp, qs[dst, gp, :, :], q[src, :, :]).then_inc(stack_in[half], 16)
                        copy_rows(sp, ks[dst, gp, :, :], k[src, :, :]).then_inc(stack_in[half], 16)
                copy_rows(sp, qs[AUX:AUX + 4, GP // 2 * half:GP // 2 * (half + 1), :, :], zeros).then_inc(stack_in[half], 16)

            def iteration(n, prep, front, score, soft, tail):
                m, after, t = n.ahead(2), n.ahead(3), n.ahead(-1)
                if prep:
                    wait_alone(sp, pool_setup, ln1_step, NORM_STEPS * after.index)
                    sp.dma_start(xt[:], rows(A["x"], after)).then_inc(x_in, 16)
                    wait_alone(sp, pool_setup, ctx_split, 2 * after.index)
                    sp.dma_start(cT_raw[:], A["ctxT"][:, bass.ds(S * after.index, S)].rearrange(
                        "(k p) s -> p k s", p=P)).then_inc(ctx_in, 16)
                if prep and not front:
                    constants()
                if front:
                    stack(m, 0)
                if tail:
                    wait_alone(sp, pool_setup, tail_step, 12 * (t.index + 1))
                    sp.dma_start(rows(x2_buf, t), x2[:]).then_inc(x2_out, 16)
                if score and not front:
                    sp.wait_ge(front_done, 6 * B)
                    sp.wait_ge(k_lo_done, 2 * B)
                    sp.wait_ge(v_ready, B)
                    sp.dma_start(common.w_raw[:, 0:WW], A["experts"][0]).then_inc(common.raw_in, 16)
                if soft:
                    wait_alone(sp, pool_setup, tail_step, 12 * n.index)
                    sp.dma_start(x_res[:], rows(A["x"], n)).then_inc(res_in, 16)
                if front:
                    stack(m, 1)
                if tail:
                    wait_alone(sp, pool_setup, ln2_step, NORM_STEPS * (t.index + 1))
                    sp.dma_start(rows(xn_buf, t), xn2[:]).then_inc(xn2_out, 16)

            pipeline(iteration, sp)

        @block.gpsimd
        def _(pool):
            pool.dma_start(causal_raw[:, 0], A["causal"].rearrange("(c p) k -> p c k", p=P)).then_inc(masks_in, 16)
            pool.dma_start(causal_raw[:, 1], A["causalT"].rearrange("(c p) q -> p c q", p=P)).then_inc(masks_in, 16)
            pool.dma_start(pad_raw[:], A["pad"].partition_broadcast(P)).then_inc(masks_in, 16)
            pool.dma_start(padT_raw[:], A["padT"].rearrange("(c p) b -> p c b", p=P)).then_inc(masks_in, 16)
            pool.memset(identf[:], 0.0).then_inc(pool_setup, 1)
            pool.memset(identb[:], 0.0).then_inc(pool_setup, 1)
            pool.wait_ge(pool_setup, 2)
            for ident in (identf, identb):
                pool.affine_select(out=ident[:], in_=ident[:], compare_op=ALU.not_equal, fill=1.0, base=0,
                                   pattern=[[-1, P]], channel_multiplier=1).then_inc(pool_setup, 1)
            pool.memset(ones, 1.0).then_inc(pool_setup, 1)
            for i in range(2):
                pool.memset(k_stack[i][:].bitcast(F32), 0.0).then_inc(pool_setup, 1)
                pool.memset(v_ones[i][:], 0.0).then_inc(pool_setup, 1)
            pool.wait_ge(pool_setup, 9)
            for i in range(2):
                pool.memset(v_ones[i][:, :, :, HD:HD + 1], 1.0).then_inc(pool_setup, 1)

            def masks():
                pool.wait_ge(masks_in, 16 * 4)
                pool.tensor_scalar(causal_neg[:], causal_raw[:, 0], NEG, None, ALU.mult).then_inc(mask_setup, 1)
                pool.tensor_scalar(pad_neg[:], pad_raw[:], NEG, None, ALU.mult).then_inc(mask_setup, 1)
                pool.tensor_scalar(causalT_neg[:], causal_raw[:, 1], NEG, None, ALU.mult).then_inc(mask_setup, 1)
                pool.tensor_scalar(padT_neg[:], padT_raw[:], NEG, None, ALU.mult).then_inc(mask_setup, 1)
                pool.wait_ge(mask_setup, 4)

            def prepare_context(after):
                at_least(pool, ctx_in, 16 * (after.index + 1))
                wait_alone(pool, pool_setup, front_done, 6 * (after.index - 1) + 5)
                pool.tensor_copy(cT_hi[:], cT_raw[:]).then_inc(ctx_split, 1)
                at_least(pool, ctx_split, 2 * after.index + 1)
                pool.tensor_tensor(cT_lo[:], cT_raw[:], cT_hi[:].bitcast(F32), ALU.subtract).then_inc(ctx_split, 1)

            def norm_step(k, which, x, out_, step, index):
                mv, var, y, t = ln_mv[:, which], ln_var[:, which], ln_y[:, which], ln_t[:, which]
                if k:
                    wait_alone(pool, pool_setup, step, NORM_STEPS * index + k)
                if k < NEWTON:
                    if k % 4 == 0:
                        ins = pool.tensor_tensor(t, y, y, ALU.mult)
                    elif k % 4 == 1:
                        ins = pool.tensor_tensor(t, t, var, ALU.mult)
                    elif k % 4 == 2:
                        ins = pool.tensor_scalar(t, t, -0.5, 1.5, ALU.mult, ALU.add)
                    else:
                        ins = pool.tensor_tensor(y, y, t, ALU.mult)
                else:
                    c = k - NEWTON
                    ins = pool.tensor_scalar(out_[:, c, :], x[:, c, :], mv[:, c, 0:1], y[:, c:c + 1], ALU.subtract, ALU.mult)
                ins.then_inc(step, 1)

            def iteration(n, prep, front, score, soft, tail):
                m, after, t = n.ahead(2), n.ahead(3), n.ahead(-1)
                if front:
                    at_least(pool, maxima_done, SCORE_UNITS * (m.index - 1))
                    pool.tensor_tensor(mask[m.parity][:], causal_neg[:],
                                       pad_neg[:, bass.ds(m.index, 1), :].to_broadcast([P, QC, S]),
                                       ALU.add).then_inc(mask_done, 1)
                if prep and front:
                    prepare_context(after)
                if prep:
                    wait_alone(pool, pool_setup, ln1_stat, STAT_STEPS * (after.index + 1))
                    for k in range(NORM_STEPS):
                        if k == NEWTON:
                            wait_alone(pool, pool_setup, front_done, 6 * (after.index - 1) + 2)
                        norm_step(k, 0, xt, xn, ln1_step, after.index)
                if prep and not front:
                    prepare_context(after)
                    masks()
                if soft:
                    at_least(pool, res_in, 16 * (n.index + 1))
                    at_least(pool, act_setup, 5)
                    pool.tensor_tensor(x_res[:], x_res[:], bo_gated[:].unsqueeze(1).to_broadcast([P, QC, D]),
                                       ALU.add).then_inc(res_done, 1)
                if front:
                    at_least(pool, probs_scored, PROB_UNITS * (m.index - 1))
                    pool.tensor_tensor(maskT[m.parity][:], causalT_neg[:],
                                       padT_neg[:, :, bass.ds(m.index, 1)].to_broadcast([P, QC, S]),
                                       ALU.add).then_inc(maskT_done, 1)
                if front:
                    at_least(pool, v_staged, m.index + 1)
                    wait_alone(pool, pool_setup, pv_done, 8 * (m.index - 1))
                    pool.tensor_copy(v_ones[m.parity][:, :, :, 0:HD], v_stage[:]).then_inc(v_ready, 1)
                if tail:
                    wait_alone(pool, pool_setup, ln2_stat, STAT_STEPS * (t.index + 1))
                    for k in range(NORM_STEPS if soft else NEWTON):
                        if k == NEWTON:
                            wait_alone(pool, pool_setup, xn2_out, 16 * t.index)
                        norm_step(k, 1, x2, xn2, ln2_step, t.index)
                if soft and not score:
                    common.split_lo_up_down(pool, 0, 1)

            pipeline(iteration, pool)

        @block.tensor
        def _(pe):
            pe.wait_ge(pool_setup, POOL_SETUP)
            pe.wait_ge(dve_setup, 3)

            def products(out_, left, right):
                n = len(left)
                for c in range(n):
                    for j, (a, b) in enumerate([(0, 0), (1, 0), (0, 1)]):
                        last = pe.matmul(out_, left[c][a], right[c][b], start=c == 0 and j == 0,
                                         stop=c == n - 1 and j == 2)
                return last

            def front_transposes(m, f):
                at_least(pe, ln1_step, NORM_STEPS * (m.index + 1))
                at_least(pe, (kv_copied, v_staged)[f], (4, 1)[f] * m.index)
                for k in range(2):
                    for c in range(QC):
                        last = pe.transpose(front_bank[f][:, k * S + c * P:k * S + (c + 1) * P],
                                            xn[:, c, (2 * f + k) * P:(2 * f + k + 1) * P], identf[:])
                last.then_inc(front_done, 1)

            def front_queries(m, f):
                if f == 0:
                    at_least(pe, xT_lo_done, 2 * (m.index + 1))
                for r in (2 * f, 2 * f + 1):
                    last = products(front_bank[f][:, (r % 2) * S:(r % 2 + 1) * S],
                                    [(wqkv_hi[:, c, r * P:(r + 1) * P], wqkv_lo[:, c, r * P:(r + 1) * P]) for c in range(KC)],
                                    [(xT_hi[:, c, :], xT_lo[:, c, :]) for c in range(KC)])
                last.then_inc(front_done, 1)

            def front_keys_values(m):
                at_least(pe, ctx_split, 2 * (m.index + 1))
                at_least(pe, q_lo_done, R * m.index + 2)
                for j in range(2):
                    cols = slice(D + j * P, D + (j + 1) * P)
                    last = products(front_bank[0][:, j * S:(j + 1) * S],
                                    [(wqkv_hi[:, c, cols], wqkv_lo[:, c, cols]) for c in range(KC)],
                                    [(cT_hi[:, c, :], cT_lo[:, c, :]) for c in range(KC)])
                last.then_inc(front_done, 1)

            def front_values(m):
                at_least(pe, kv_copied, 4 * m.index + 1)
                at_least(pe, q_lo_done, R * (m.index + 1))
                for c in range(QC):
                    last = pe.transpose(front_bank[1][:, c * P:(c + 1) * P], vT[:, c * P:(c + 1) * P], identf[:])
                last.then_inc(front_done, 1)

            def score_unit(m, u):
                gp, r, c = u // (R * QC), u // QC % R, u % QC
                if u % (SCORE_UNITS // 2) == 0:
                    at_least(pe, stack_in[2 * u // SCORE_UNITS], 16 * STACK_DMAS * (m.index + 1))
                bank = score_bank[(m.parity + u) % 2]
                if u == 0:
                    at_least(pe, maxima_done, SCORE_UNITS * m.index)
                elif u == 1:
                    at_least(pe, maxT_copied, m.index)
                else:
                    at_least(pe, maxima_done, SCORE_UNITS * m.index + u - 1)
                pe.matmul(bank[:].rearrange("p a b -> p (a b)"), q_stack[m.parity][:, gp, r, c * P:(c + 1) * P],
                          k_stack[m.parity][:, gp].rearrange("p a b -> p (a b)"),
                          start=True, stop=True).then_inc(scores_done, 1)

            def transpose_maxima(m):
                wait_alone(pe, dve_setup, max_split, 2 * (m.index + 1))
                bank = score_bank[(m.parity + SCORE_UNITS) % 2][:].rearrange("p a b -> p (a b)")
                for c in range(QC):
                    last = pe.transpose(bank[0:2 * H, c * P:(c + 1) * P],
                                        neg_max[:, c].rearrange("p a b h -> p (a b h)").bitcast(F32), identf[:])
                last.then_inc(maxT_done, 1)

            def prob_unit(n, v):
                gg, rp, kc, j = v // 16, v // 8 % 2, v // 4 % 2, v % 4
                gp, g2 = 2 * gg + j // 2, j % 2
                if v == 0:
                    at_least(pe, max_in, 16 * (n.index + 1))
                    at_least(pe, maskT_done, n.index + 1)
                at_least(pe, exp_done, PROB_UNITS * n.index + v - 1)
                bank = prob_bank[v % 2][:].rearrange("p a b -> p (a b)")
                pe.matmul(bank, k_stack[n.parity][:, gp, g2, kc * P:(kc + 1) * P],
                          q_stack[n.parity][:, gp, 2 * rp:2 * rp + 2, :].rearrange("p a b -> p (a b)"),
                          start=True, stop=False)
                pe.matmul(prob_bank[v % 2][:], identb[:],
                          maskT[n.parity][:, kc, :].unsqueeze(1).to_broadcast([P, 2, S]),
                          start=False, stop=True).then_inc(probs_scored, 1)

            def value_group(n, k):
                gg, w, kc = k // 4, k // 2, k % 2
                if k == 0:
                    at_least(pe, v_ready, n.index + 1)
                at_least(pe, exp_done, PROB_UNITS * n.index + 4 * k + 4)
                if kc == 0:
                    at_least(pe, mixed_done, 4 * n.index + w)
                for j in range(4):
                    last = pe.matmul(pv_bank[32 * j:32 * (j + 1), :], v_ones[n.parity][:, kc, 4 * gg + j, :],
                                     probs[:, (4 * k + j) % 8, :], start=kc == 0, stop=kc == 1)
                last.then_inc(pv_done, 1)

            def tail_unmix(t, c, gg):
                at_least(pe, mixed_done, 4 * (t.index + 1))
                at_least(pe, tail_step, 12 * t.index + 6 * c + 2 * gg)
                for r in range(R):
                    last = pe.transpose(tail_bank[:, r * P:(r + 1) * P],
                                        mixed[t.parity][:, 2 * gg + r // 2, (r % 2) * S + c * P:(r % 2) * S + (c + 1) * P],
                                        identf[:])
                last.then_inc(tail_done, 1)

            def tail_transposes(t, c):
                at_least(pe, tail_step, 12 * t.index + 6 * c + 4)
                for k in range(KC):
                    last = pe.transpose(tail_bank[:, k * P:(k + 1) * P], attn[:, c, k * P:(k + 1) * P], identf[:])
                last.then_inc(tail_done, 1)

            def tail_project(t, c):
                at_least(pe, tail_step, 12 * t.index + 6 * c + 5)
                products(tail_bank[:], [(aT_hi[:, k, :], aT_lo[:, k, :]) for k in range(KC)],
                         [(wo_hi[:, k, :], wo_lo[:, k, :]) for k in range(KC)]).then_inc(tail_done, 1)

            def iteration(n, prep, front, score, soft, tail):
                m, s, t = n.ahead(2), n.ahead(1), n.ahead(-1)
                if score and not soft:
                    pe.wait_ge(ones_in, 64)
                    pe.wait_ge(dve_setup, 4)
                for slot in range(SLOTS):
                    if score and slot < SCORE_UNITS:
                        score_unit(s, slot)
                    if soft and 0 <= slot - PROB_LAG < PROB_UNITS:
                        prob_unit(n, slot - PROB_LAG)
                    if soft and 0 <= slot - PV_LAG <= 28 and (slot - PV_LAG) % 4 == 0:
                        value_group(n, (slot - PV_LAG) // 4)
                    if front:
                        if slot in (0, 1):
                            front_transposes(m, slot)
                        if slot in (9, 11):
                            front_queries(m, (slot - 9) // 2)
                        if slot == 13:
                            front_keys_values(m)
                        if slot == 15:
                            front_values(m)
                    if tail:
                        for c in range(QC):
                            if slot == 17 * c:
                                tail_unmix(t, c, 0)
                            if slot == 17 * c + 3:
                                tail_unmix(t, c, 1)
                            if slot == 17 * c + 6:
                                tail_transposes(t, c)
                            if slot == 17 * c + 10:
                                tail_project(t, c)
                    if score and slot == 34:
                        transpose_maxima(s)

            pipeline(iteration, pe)

        @block.scalar
        def _(act):
            act.dma_start(bq[:], A["bq"]).then_inc(consts_in, 16)
            act.dma_start(bk[:], A["bk"]).then_inc(consts_in, 16)
            act.dma_start(bv[:], A["bv"]).then_inc(consts_in, 16)
            act.dma_start(parity[:], A["parity"]).then_inc(consts_in, 16)
            act.dma_start(tanh_gate[:], A["g_xattn"].partition_broadcast(P)).then_inc(consts_in, 16)
            act.dma_start(common.tanh_ffn[:], A["g_ffn"].partition_broadcast(P)).then_inc(consts_in, 16)
            act.dma_start(bo_gated[:], A["bo"].partition_broadcast(P)).then_inc(consts_in, 16)
            act.wait_ge(wqkv_in, 16)
            act.activation(wqkv_hi[:].rearrange("p a b -> p (a b)"), probs[:, 0:6, :].rearrange("p a b -> p (a b)"),
                           ACT.Copy).then_inc(act_setup, 1)
            act.wait_ge(wo_in, 16)
            act.activation(wo_hi[:].rearrange("p a b -> p (a b)"), mixed[0][:].rearrange("p a b -> p (a b)"),
                           ACT.Copy).then_inc(act_setup, 1)
            act.wait_ge(consts_in, 16 * 7)
            act.activation(tanh_gate[:], tanh_gate[:], ACT.Tanh).then_inc(act_setup, 1)
            act.activation(common.tanh_ffn[:], common.tanh_ffn[:], ACT.Tanh).then_inc(act_setup, 1)
            act.wait_ge(act_setup, 4)
            act.activation(bo_gated[:], bo_gated[:], ACT.Copy, scale=tanh_gate[:, 0:1]).then_inc(act_setup, 1)

            def front_x_hi(m, f):
                at_least(act, front_done, 6 * m.index + f + 1)
                at_least(act, front_done, 6 * (m.index - 1) + 4)
                act.activation(xT_hi[:, 2 * f:2 * f + 2, :].rearrange("p a b -> p (a b)"), front_bank[f][:],
                               ACT.Copy).then_inc(xT_hi_done, 1)

            def front_q_hi(m, r):
                at_least(act, front_done, 6 * m.index + 3 + r // 2)
                if r == 0:
                    for half in range(2):
                        at_least(act, stack_in[half], 16 * STACK_DMAS * m.index)
                act.activation(q_hi[:, r, :], front_bank[r // 2][:, (r % 2) * S:(r % 2 + 1) * S], ACT.Identity,
                               bias=bq[:, r:r + 1]).then_inc(q_hi_done, 1)

            def front_kv(m):
                at_least(act, front_done, 6 * m.index + 5)
                act.activation(vT[:], front_bank[0][:, S:2 * S], ACT.Identity, bias=bv[:, 0:1]).then_inc(kv_copied, 1)
                for half in range(2):
                    at_least(act, stack_in[half], 16 * STACK_DMAS * m.index)
                act.activation(k_raw[:], front_bank[0][:, 0:S], ACT.Identity, bias=bk[:, 0:1]).then_inc(kv_copied, 1)
                at_least(act, kv_copied, 4 * m.index + 2)
                for g2 in range(2):
                    act.activation(k_hi[:, g2, :], k_raw[:], ACT.Copy, scale=parity[:, g2:g2 + 1]).then_inc(kv_copied, 1)

            def front_v(m):
                at_least(act, front_done, 6 * m.index + 6)
                at_least(act, v_ready, m.index)
                act.activation(v_stage[:].rearrange("p c g d -> p (c g d)"), front_bank[1][:, 0:QC * P],
                               ACT.Copy).then_inc(v_staged, 1)

            def exp_unit(n, v):
                at_least(act, probs_scored, PROB_UNITS * n.index + v + 1)
                if v % 4 == 0:
                    at_least(act, pv_done, 8 * n.index + v // 4 - 1)
                act.activation(probs[:, v % 8, :], prob_bank[v % 2][:].rearrange("p a b -> p (a b)"), ACT.Exp,
                               scale=HD ** -0.5).then_inc(exp_done, 1)

            def copy_mixed(n, w):
                at_least(act, pv_done, 8 * n.index + 2 * w + 2)
                if w == 0:
                    at_least(act, tail_done, 8 * (n.index - 1))
                act.activation(mixed[n.parity][:, w, :], pv_bank[:], ACT.Copy).then_inc(mixed_done, 1)

            def stack_maxima(m):
                at_least(act, maxT_done, m.index + 1)
                at_least(act, max_in, 16 * m.index)
                at_least(act, stack_in[0], 16 * STACK_DMAS * (m.index + 1))
                at_least(act, stack_in[1], 16 * STACK_DMAS * (m.index + 1))
                act.activation(neg_maxT[:], score_bank[(m.parity + SCORE_UNITS) % 2][0:2 * H].rearrange(
                    "p a b -> p (a b)")[:, 0:S], ACT.Copy).then_inc(maxT_copied, 1)
                at_least(act, maxT_copied, m.index + 1)
                copy_rows(act, q_stack[m.parity][AUX:AUX + 4].rearrange("o g r s -> o (g r s)"), neg_maxT[:]).then_inc(max_in, 16)

            def tail_hi(t, c):
                at_least(act, tail_done, 8 * t.index + 4 * c + 3)
                at_least(act, tail_done, 8 * t.index + 4 * c)
                act.activation(aT_hi[:].rearrange("p k q -> p (k q)"), tail_bank[:], ACT.Copy).then_inc(aT_hi_done, 1)

            def iteration(n, prep, front, score, soft, tail):
                m, s, t = n.ahead(2), n.ahead(1), n.ahead(-1)
                if score and not soft:
                    act.wait_ge(dve_setup, 4)
                for slot in range(SLOTS):
                    if soft and 0 <= slot - PROB_LAG < PROB_UNITS:
                        exp_unit(n, slot - PROB_LAG)
                    if soft and slot in (13, 21, 29, 37):
                        copy_mixed(n, (slot - 13) // 8)
                    if tail and slot in (7, 24):
                        tail_hi(t, slot // 24)
                    if front:
                        if slot in (1, 2):
                            front_x_hi(m, slot - 1)
                        if slot in (10, 12):
                            front_q_hi(m, slot - 10)
                            front_q_hi(m, slot - 9)
                        if slot == 14:
                            front_kv(m)
                        if slot == 16:
                            front_v(m)
                    if score and slot == 35:
                        stack_maxima(s)
                    if soft and not score and slot in (3, 11, 19):
                        act.wait_ge(common.raw_in, 16)
                        act.wait_ge(xT_lo_done, 2 * B)
                        common.split_hi(act, 0, slot // 8)

            pipeline(iteration, act)

        @block.vector
        def _(dve):
            dve.memset(q_stack[0][:].bitcast(F32), 0.0).then_inc(dve_setup, 1)
            dve.memset(q_stack[1][:].bitcast(F32), 0.0).then_inc(dve_setup, 1)

            def stat_step(k, which, x, step, index):
                stats, mv, var = ln_stats[:, which], ln_mv[:, which], ln_var[:, which]
                y, t = ln_y[:, which], ln_t[:, which]
                wait_alone(dve, dve_setup, step, STAT_STEPS * index + k)
                if k < 2:
                    ins = dve.bn_stats(stats[:, k, :], x[:, k, :])
                elif k < 4:
                    ins = dve.bn_aggr(mv[:, k - 2, :], stats[:, k - 2, :])
                elif k == 4:
                    ins = dve.tensor_scalar(var, mv[:, :, 1], EPS, None, ALU.add)
                elif k == 5:
                    ins = dve.tensor_scalar(t.bitcast(I32), var.bitcast(I32), 1, None, ALU.logical_shift_right)
                else:
                    ins = dve.tensor_scalar(y.bitcast(I32), t.bitcast(I32), -1.0, RSQRT_MAGIC, ALU.mult, ALU.add)
                ins.then_inc(step, 1)

            def prep_stats(m, k):
                if k == 0:
                    at_least(dve, x_in, 16 * (m.index + 1))
                    at_least(dve, ln1_step, NORM_STEPS * m.index)
                stat_step(k, 0, xt, ln1_stat, m.index)

            def front_x_lo(m, f):
                at_least(dve, xT_hi_done, 2 * m.index + f + 1)
                dve.tensor_tensor(xT_lo[:, 2 * f:2 * f + 2, :].rearrange("p a b -> p (a b)"), front_bank[f][:],
                                  xT_hi[:, 2 * f:2 * f + 2, :].rearrange("p a b -> p (a b)").bitcast(F32),
                                  ALU.subtract).then_inc(xT_lo_done, 1)

            def front_q_lo(m, r):
                at_least(dve, q_hi_done, R * m.index + 2 * (r // 2) + 2)
                dve.scalar_tensor_tensor(q_lo[:, r, :], front_bank[r // 2][:, (r % 2) * S:(r % 2 + 1) * S],
                                         bq[:, r:r + 1], q_hi[:, r, :].bitcast(F32), ALU.add,
                                         ALU.subtract).then_inc(q_lo_done, 1)

            def front_k_lo(m):
                at_least(dve, kv_copied, 4 * (m.index + 1))
                for g2 in range(2):
                    dve.scalar_tensor_tensor(k_lo[:, g2, :], k_raw[:], parity[:, g2:g2 + 1], k_hi[:, g2, :].bitcast(F32),
                                             ALU.mult, ALU.subtract).then_inc(k_lo_done, 1)

            def maxima_unit(m, u):
                gp, r, c = u // (R * QC), u // QC % R, u % QC
                if u == 0:
                    at_least(dve, mask_done, m.index + 1)
                    at_least(dve, max_split, 2 * m.index)
                wait_alone(dve, dve_setup, scores_done, SCORE_UNITS * m.index + u + 1)
                bank = score_bank[(m.parity + u) % 2]
                for g2 in range(2):
                    head = g2 * H // 2 + gp * R + r
                    last = dve.tensor_tensor_reduce(out=bank[:, g2, :], in0=bank[:, g2, :], in1=mask[m.parity][:, c, :],
                                                    scale=1.0, scalar=-3e38, op0=ALU.add, op1=ALU.max,
                                                    accum_out=row_max[:, c, head:head + 1])
                last.then_inc(maxima_done, 1)

            def split_maxima(m):
                at_least(dve, maxima_done, SCORE_UNITS * (m.index + 1))
                at_least(dve, maxT_done, m.index)
                maxima = row_max[:].rearrange("p c (a h) -> p c a h", a=2)
                dve.tensor_scalar(neg_max[:, :, :, 0, :], maxima, -1.0, None, ALU.mult).then_inc(max_split, 1)
                at_least(dve, max_split, 2 * m.index + 1)
                dve.scalar_tensor_tensor(neg_max[:, :, :, 1, :], maxima, -1.0, neg_max[:, :, :, 0, :].bitcast(F32),
                                         ALU.mult, ALU.subtract).then_inc(max_split, 1)

            def tail_normalize(t, c, gg):
                done = 12 * t.index + 6 * c + 2 * gg
                at_least(dve, tail_done, 8 * t.index + 4 * c + gg + 1)
                at_least(dve, tail_step, done)
                heads = tail_bank[:].rearrange("p (h w) -> p h w", w=2 * HD)
                sums = inv_sum[:].rearrange("p r j -> p (r j)")
                dve.reciprocal(sums, heads[:, :, HD]).then_inc(tail_step, 1)
                at_least(dve, tail_step, done + 1)
                dve.tensor_tensor(attn[:, c, gg * S:(gg + 1) * S].rearrange("p (h w) -> p h w", w=HD),
                                  heads[:, :, 0:HD], sums.unsqueeze(2).to_broadcast([P, H // 2, HD]),
                                  ALU.mult).then_inc(tail_step, 1)

            def tail_lo(t, c):
                at_least(dve, aT_hi_done, 2 * t.index + c + 1)
                dve.tensor_tensor(aT_lo[:].rearrange("p k q -> p (k q)"), tail_bank[:],
                                  aT_hi[:].rearrange("p k q -> p (k q)").bitcast(F32),
                                  ALU.subtract).then_inc(tail_step, 1)

            def tail_residual(t, c):
                at_least(dve, tail_done, 8 * t.index + 4 * c + 4)
                if c == 0:
                    at_least(dve, res_done, t.index + 1)
                    at_least(dve, x2_out, 16 * t.index)
                    at_least(dve, ln2_step, NORM_STEPS * t.index)
                dve.scalar_tensor_tensor(x2[:, c, :], tail_bank[:], tanh_gate[:, 0:1], x_res[:, c, :], ALU.mult,
                                         ALU.add).then_inc(tail_step, 1)

            def tail_stats(t, k):
                if k == 0:
                    at_least(dve, tail_step, 12 * (t.index + 1))
                    at_least(dve, ln2_step, NORM_STEPS * t.index)
                stat_step(k, 1, x2, ln2_stat, t.index)

            def iteration(n, prep, front, score, soft, tail):
                after, m, s, t = n.ahead(3), n.ahead(2), n.ahead(1), n.ahead(-1)
                for slot in range(SLOTS):
                    if score and slot < SCORE_UNITS:
                        maxima_unit(s, slot)
                    if front:
                        if slot in (2, 3):
                            front_x_lo(m, slot - 2)
                        if slot in (10, 12):
                            front_q_lo(m, slot - 10)
                            front_q_lo(m, slot - 9)
                        if slot == 15:
                            front_k_lo(m)
                    if tail:
                        for c in range(QC):
                            if slot == 17 * c + 1:
                                tail_normalize(t, c, 0)
                            if slot == 17 * c + 4:
                                tail_normalize(t, c, 1)
                            if slot == 17 * c + 8:
                                tail_lo(t, c)
                            if slot == 17 * c + 12:
                                tail_residual(t, c)
                        for k in range(STAT_STEPS):
                            if slot == TAIL_STAT_SLOTS[k]:
                                tail_stats(t, k)
                    for k in range(STAT_STEPS):
                        if prep and slot == PREP_STAT_SLOTS[k]:
                            prep_stats(after, k)
                    if score and slot == 32:
                        split_maxima(s)
                    if soft and not score and slot == 24:
                        common.split_lo_gate(dve, 0, 1)
                if tail and not soft:
                    dve.wait_ge(ln2_step, NORM_STEPS * (B - 1) + NEWTON)
                    dve.wait_ge(xn2_out, 16 * (B - 1))
                    for c in range(QC):
                        dve.tensor_scalar(xn2[:, c, :], x2[:, c, :], ln_mv[:, 1, c, 0:1], ln_y[:, 1, c:c + 1],
                                          ALU.subtract, ALU.mult).then_inc(ln2_step, 1)
                if prep and not front:
                    dve.wait_ge(act_setup, 1)
                    dve.tensor_tensor(wqkv_lo[:].rearrange("p a b -> p (a b)"), probs[:, 0:6, :].rearrange("p a b -> p (a b)"),
                                      wqkv_hi[:].rearrange("p a b -> p (a b)").bitcast(F32), ALU.subtract).then_inc(dve_setup, 1)
                    dve.wait_ge(act_setup, 5)
                    dve.tensor_tensor(wo_lo[:].rearrange("p a b -> p (a b)"), mixed[0][:].rearrange("p a b -> p (a b)"),
                                      wo_hi[:].rearrange("p a b -> p (a b)").bitcast(F32),
                                      ALU.subtract).then_inc(dve_setup, 1)

            pipeline(iteration, dve)


CHOSEN_STEP = 19
ROUTE_STEPS = 65


class Step:

    def __init__(self, pair, parity):
        self.pair, self.parity = pair, parity
        self.index = 2 * pair + parity

    def ahead(self, k):
        return Step(self.pair + (self.parity + k) // 2, (self.parity + k) % 2)


def at_step(number):
    return Step(number // 2, number % 2)


BASE_PART = 4
RING = 4


class RingStep(Step):

    def __init__(self, turn, place):
        super().__init__(turn * (RING // 2) + place // 2, place % 2)
        self.turn, self.place = turn, place

    def ahead(self, k):
        return RingStep(self.turn + (self.place + k) // RING, (self.place + k) % RING)


def at_ring(number):
    return RingStep(number // RING, number % RING)


def expert_phase(nc, A, x2_buf, xn_buf, out, common):
    with ExitStack() as ctx:
        def sb(name, shape, dt=F32):
            return ctx.enter_context(nc.sbuf_tensor(name, shape, dt))

        def ps(name, shape):
            return ctx.enter_context(nc.psum_tensor(name, shape, F32))

        sem = common.sem

        row_table = nc.dram_tensor("row_table", (SLOT_ROWS, 2), I32, kind="Internal").ap()

        ident, w_raw, w_hi, w_lo = common.ident, common.w_raw, common.w_hi, common.w_lo
        raw_in, tile_in, x2_out, xn2_out = common.raw_in, common.tile_in, common.x2_out, common.xn2_out
        x_tile = [sb(f"x_tile{i}", [P, D]) for i in range(2)]
        w_hi_done, w_lo_dve, w_lo_pool = common.w_hi_done, common.w_lo_dve, common.w_lo_pool
        ones_mat = sb("ones_mat", [P, P])
        consts = sb("consts", [P, CONSTS])
        tanh_ffn = common.tanh_ffn
        zero_rows = sb("zero_rows", [P, D])
        base = sb("base", [P, NT, D])
        xt_hi = [sb(f"xt_hi{i}", [P, KC, P], F32R) for i in range(2)]
        xt_lo = [sb(f"xt_lo{i}", [P, KC, P], F32R) for i in range(2)]
        silu = [sb(f"silu{i}", [P, FE]) for i in range(2)]
        h = sb("h", [P, FC * P])
        h_hi = sb("h_hi", [P, FC, P], F32R)
        h_lo = sb("h_lo", [P, FC, P], F32R)
        y = [sb(f"y{i}", [P, D]) for i in range(2)]
        logits = sb("logits", [P, NT, NE])
        score = sb("score", [P, NT, NE])
        stat = sb("stat", [P, NT])
        inv = sb("inv", [P, NT])
        best = sb("best", [P, NT, PAIRS])
        group_gt = sb("group_gt", [P, NT, PAIRS, PAIRS])
        group_eq = sb("group_eq", [P, NT, PAIRS, PAIRS])
        rank = sb("rank", [P, NT, NE])
        gt = sb("gt", [P, NT, NE, NE])
        eq = sb("eq", [P, NT, NE, NE])
        chosen = sb("chosen", [P, NT, NE])
        weight = sb("weight", [P, NT, NE])
        place = sb("place", [P, NT, NE])
        counts = sb("counts", [P, NT * NE + NE])
        full = sb("full", [P, NE, NT - 1])
        tiles = sb("tiles", [P, NE])
        before = sb("before", [P, NE, NE])
        start = sb("start", [P, NE])
        end = sb("end", [P, NE])
        slot = sb("slot", [P, TOP, NT])
        row = sb("row", [P, NT, 3, TOP], I32)
        expert_gt = sb("expert_gt", [P, ROUTED_TILES + 2, NE])
        expert = sb("expert", [P, ROUTED_TILES + 2])
        free_f = sb("free_f", [P, ROUTED_TILES + 2])
        parity_f = sb("parity_f", [P, ROUTED_TILES + 2])
        t_load = sb("t_load", [P, ROUTED_TILES + 2], I32)
        t_place = sb("t_place", [P, ROUTED_TILES + 2], I32)
        t_new = sb("t_new", [P, ROUTED_TILES + 2], I32)
        t_free = sb("t_free", [P, ROUTED_TILES + 2], I32)
        row_now = sb("row_now", [P, 4, 3, TOP], I32)
        table = sb("table", [P, ROUTED_TILES, 2], I32)
        x_ring = [sb(f"x_ring{i}", [P, D]) for i in range(RING)]
        gather_idx = [sb(f"gather_idx{i}", [P, 1], I32) for i in range(RING)]
        add_idx = [sb(f"add_idx{i}", [P, 1], I32) for i in range(2)]

        gate_bank = [ps(f"gate_bank{i}", [P, 512]) for i in range(2)]
        up_bank = [ps(f"up_bank{i}", [P, 512]) for i in range(2)]
        xt_bank = ps("xt_bank", [P, 512])
        ht_bank = ps("ht_bank", [P, 512])
        y_bank = [ps(f"y_bank{i}", [P, 512]) for i in range(2)]

        const_in, base_in = sem("const_in"), [sem("base_in_first"), sem("base_in_rest")]
        gathered = [sem(f"gathered_{i}") for i in range(RING)]
        pads_out, shared_out = sem("pads_out"), sem("shared_out")
        table_set, scattered, table_in, added = sem("table_set"), sem("scattered"), sem("table_in"), sem("added")
        b_setup, h_padded = sem("b_setup"), sem("h_padded")
        route_step, exp_scores, counted = sem("route_step"), sem("exp_scores"), sem("counted")
        row_copied, idx_copied = sem("row_copied"), sem("idx_copied")
        gate_done, up_done, xt_done, ht_done, down_done = (
            sem("gate_done"), sem("up_done"), sem("xt_done"), sem("ht_done"), sem("down_done"))
        silu_done, xt_hi_done, h_hi_done, logits_copied = (
            sem("silu_done"), sem("xt_hi_done"), sem("h_hi_done"), sem("logits_copied"))
        xt_lo_done, h_done, h_lo_done, y_done = sem("xt_lo_done"), sem("h_done"), sem("h_lo_done"), sem("y_done")

        block = ctx.enter_context(nc.Block())

        def tile_rows(buf, t):
            return buf[bass.ds(P * t, P), :]

        def step_loop(eng, first, last, body):
            with eng.Fori(0, (last - first + 1) // 2) as pair:
                for k in range(2):
                    body(Step(pair + (first + k) // 2, (first + k) % 2))

        def table_value(eng, tab, s, ahead, hi):
            t = s.index + ahead - FIRST_ROUTED
            return eng.value_load(tab[0:1, bass.ds(t, 1)], min_val=0, max_val=hi)

        @block.sync
        def _(sp):
            def load_weights(j):
                wait_alone(sp, b_setup, raw_in, 16 * j)
                wait_alone(sp, b_setup, w_lo_dve, j - 1)
                wait_alone(sp, b_setup, w_lo_pool, 2 * (j - 1))

            def weights_dma(j, place):
                sp.dma_start(w_raw[:, place * WW:(place + 1) * WW], A["experts"][j]).then_inc(raw_in, 16)

            def load_tile(s, t):
                sp.dma_start(x_tile[s.parity][:], tile_rows(xn_buf, t)).then_inc(tile_in[s.parity], 16)

            sp.wait_ge(xn2_out, 16 * B)
            sp.wait_ge(x2_out, 16 * B)
            for k in range(2):
                load_tile(at_step(k), k)

            def first_half(s):
                wait_alone(sp, b_setup, xt_done, s.index + 1)
                load_tile(s, (s.index + 2) % NT if isinstance(s.index, int) else s.index + 2)

            def store_shared(t):
                sp.dma_start(tile_rows(out, t), base[:, bass.ds(t, 1), :].rearrange("p o d -> p (o d)")).then_inc(shared_out, 16)

            def second_half(s):
                wait_alone(sp, b_setup, xt_done, s.index + 1)
                load_tile(s, s.index + 2 - NT)

            for k in range(NT // BASE_PART):
                lo, hi = k * BASE_PART, (k + 1) * BASE_PART
                sp.dma_start(base[:, lo:hi], x2_buf[lo * P:hi * P, :].rearrange("(t p) d -> p t d", p=P)
                             ).then_inc(base_in[k > 0], 16)
                first_half(at_step(k))
            load_weights(1)
            weights_dma(1, 1)
            step_loop(sp, NT // BASE_PART, NT - 5, first_half)
            load_weights(2)
            weights_dma(2, 0)
            for k in (NT - 4, NT - 3):
                first_half(at_step(k))
            first_half(at_step(NT - 2))
            first_half(at_step(NT - 1))
            load_weights(3)
            weights_dma(3, 1)

            def second_and_store(s):
                second_half(s)
                wait_alone(sp, b_setup, y_done, s.index)
                store_shared(s.index - 1 - NT)

            second_half(at_step(NT))
            second_and_store(at_step(NT + 1))
            step_loop(sp, NT + 2, 2 * NT - 3, second_and_store)
            for t in range(NT - 3, NT):
                sp.wait_ge(y_done, NT + t + 1)
                store_shared(t)
            with sp.Fori(2, SHARED // 2 + NE // 2) as pair:
                for k in range(2):
                    load_weights(2 * pair + k)
                    sp.dma_start(w_raw[:, k * WW:(k + 1) * WW], A["experts"][bass.ds(2 * pair + k, 1)].rearrange(
                        "o p w -> (o p) w")).then_inc(raw_in, 16)
            sp.wait_ge(shared_out, 16 * NT)

        @block.gpsimd
        def _(pool):
            pool.dma_start(consts[:], A["consts"]).then_inc(const_in, 16)
            pool.dma_start(row_table, A["no_rows"]).then_inc(table_set, 16)
            pool.memset(ones_mat[:], 1.0).then_inc(b_setup, 1)
            pool.memset(zero_rows[:], 0.0).then_inc(b_setup, 1)
            pool.wait_ge(b_setup, 2)
            pool.dma_start(xn_buf[T:T + P, :], zero_rows[:]).then_inc(pads_out, 16)
            pool.dma_start(out[T:T + P, :], zero_rows[:]).then_inc(added, 16)

            for j in range(1, 3):
                common.split_lo_up_down(pool, j % 2 * WW, j + 1)

            pool.wait_ge(table_set, 16)
            pool.wait_ge(route_step, ROUTE_STEPS)
            with pool.Fori(0, NT // 4) as four:
                wait_alone(pool, b_setup, scattered, 16 * 8 * four)
                pool.tensor_copy(row_now[:], row[:, bass.ds(4 * four, 4)]).then_inc(row_copied, 1)
                wait_alone(pool, b_setup, row_copied, four + 1)
                for t in range(4):
                    for k in range(TOP):
                        pool.indirect_dma_start(
                            out=row_table, out_offset=bass.IndirectOffsetOnAxis(ap=row_now[:, t, 0, k:k + 1], axis=0),
                            in_=row_now[:, t, k + 1, :], in_offset=None).then_inc(scattered, 16)
            pool.wait_ge(scattered, 16 * TOP * NT)
            pool.dma_start(table[:], row_table.rearrange("(t p) w -> p t w", p=P)).then_inc(table_in, 16)
            pool.wait_ge(table_in, 16)
            pool.wait_ge(pads_out, 16)

            def copy_index(dst, tile_number, turn):
                pool.tensor_copy(dst[:], table[:, bass.ds(tile_number, 1), 0]).then_inc(idx_copied, 1)
                wait_alone(pool, b_setup, idx_copied, turn)

            def gather(s, turn):
                at_least(pool, xt_done, s.index + 1 - RING)
                copy_index(gather_idx[s.place], s.index - FIRST_ROUTED, turn)
                pool.indirect_dma_start(out=x_ring[s.place][:], out_offset=None, in_=xn_buf,
                                        in_offset=bass.IndirectOffsetOnAxis(ap=gather_idx[s.place][:, :1], axis=0)
                                        ).then_inc(gathered[s.place], 16)

            def add_rows(s, turn):
                p = (s.parity + 1) % 2
                t = s.index - 1 - FIRST_ROUTED
                at_least(pool, added, 16 * t + 16)
                copy_index(add_idx[p], t, turn)
                wait_alone(pool, b_setup, y_done, s.index)
                pool.indirect_dma_start(out=out, out_offset=bass.IndirectOffsetOnAxis(ap=add_idx[p][:, :1], axis=0),
                                        in_=y[p][:], in_offset=None, compute_op=ALU.add).then_inc(added, 16)

            def after_next(s):
                return (table_value(pool, t_new, s, 2, 1), table_value(pool, t_load, s, 2, NE - 1) + SHARED + 1,
                        table_value(pool, t_place, s, 2, WW))

            def split_new(new, count, place):
                with pool.If(new > 0):
                    common.split_lo_up_down(pool, place, count)

            for k in range(RING):
                gather(at_ring(FIRST_ROUTED + k), k + 1)
            for s in (FIRST_ROUTED - 1, FIRST_ROUTED):
                split_new(*after_next(at_step(s)))
            pool.wait_ge(shared_out, 16 * NT)

            def step(s):
                turn = RING + 2 * (s.index - FIRST_ROUTED) - 1
                gather(s.ahead(RING - 1), turn)
                values = after_next(s)
                add_rows(s, turn + 1)
                split_new(*values)

            last_turns = STEPS - RING - 2
            with pool.Fori(FIRST_ROUTED // RING, last_turns // RING) as turn:
                for k in range(RING):
                    step(RingStep(turn, 1).ahead(k))
            for k in range(last_turns // RING * RING + 1, STEPS - RING + 1):
                step(at_ring(k))
            gathers = RING + 2 * (STEPS - RING - FIRST_ROUTED) + 1
            for k in range(RING):
                add_rows(at_ring(STEPS - RING + 1 + k), gathers + k)
                if STEPS - RING + 1 + k <= STEPS - 3:
                    split_new(*after_next(at_ring(STEPS - RING + 1 + k)))
            pool.wait_ge(added, 16 * (ROUTED_TILES + 1))

        @block.tensor
        def _(pe):

            def products(out_, left, right):
                n = len(left)
                for c in range(n):
                    for k, (a, b) in enumerate([(0, 0), (1, 0), (0, 1)]):
                        last = pe.matmul(out_, left[c][a], right[c][b], start=c == 0 and k == 0,
                                         stop=c == n - 1 and k == 2)
                return last

            def weight_parts(place, at, n):
                return w_hi[:, bass.ds(place + at, n)], w_lo[:, bass.ds(place + at, n)]

            def gate_up(s, place, gate_w, loads, fetch):
                if loads is not None:
                    pe.wait_ge(w_lo_dve, loads)
                pe.wait_ge(xt_lo_done, s.index + 1)
                at_least(pe, h_done, s.index - 1)
                left = [(xt_hi[s.parity][:, c, :], xt_lo[s.parity][:, c, :]) for c in range(KC)]
                products(gate_bank[s.parity][:, 0:gate_w], left,
                         [weight_parts(place, c * GATE_W, gate_w) for c in range(KC)]).then_inc(gate_done, 1)
                if loads is not None:
                    pe.wait_ge(w_lo_pool, 2 * loads - 1)
                after = (table_value(pe, t_load, s, 1, NE - 1) + SHARED + 1,) if fetch else ()
                products(up_bank[s.parity][:, 0:FE], left,
                         [weight_parts(place, UP_AT + c * FE, FE) for c in range(KC)]).then_inc(up_done, 1)
                if fetch:
                    after += (table_value(pe, t_place, s, 1, WW),)
                return after

            def transpose_x(s, gather):
                if gather:
                    at_least(pe, gathered[s.place], 16 * (s.turn - FIRST_ROUTED // RING + 1))
                    x = x_ring[s.place]
                else:
                    at_least(pe, tile_in[s.parity], 16 * (s.pair + 1))
                    x = x_tile[s.parity]
                at_least(pe, xt_lo_done, s.index)
                for c in range(KC):
                    last = pe.transpose(xt_bank[:, c * P:(c + 1) * P], x[:, c * P:(c + 1) * P], ident[:])
                last.then_inc(xt_done, 1)

            def transpose_h(s):
                pe.wait_ge(h_done, s.index + 1)
                at_least(pe, h_lo_done, s.index)
                for c in range(FC):
                    last = pe.transpose(ht_bank[:, c * P:(c + 1) * P], h[:, c * P:(c + 1) * P], ident[:])
                last.then_inc(ht_done, 1)

            def down(s, place):
                pe.wait_ge(h_lo_done, s.index + 1)
                at_least(pe, y_done, s.index - 1)
                products(y_bank[s.parity][:], [(h_hi[:, c, :], h_lo[:, c, :]) for c in range(FC)],
                         [weight_parts(place, DOWN_AT + c * D, D) for c in range(FC)]).then_inc(down_done, 1)

            def step(s, place, place_before, gate_w=FE, loads=None, gather=False, first=False, last=False, fetch=False):
                after = gate_up(s, place, gate_w, loads, fetch)
                if not last:
                    transpose_x(s.ahead(1), gather)
                if not first:
                    if loads is not None:
                        pe.wait_ge(w_lo_pool, 2 * loads)
                    down(s.ahead(-1), place_before)
                transpose_h(s)
                return after

            def places(s):
                return table_value(pe, t_load, s, 0, NE - 1) + SHARED + 1, table_value(pe, t_place, s, 0, WW)

            kept = [pe.alloc_register(name) for name in ("place_before", "loads_now", "place_now")]

            def keep(before, loads, place):
                for register, value in zip(kept, (before, loads, place)):
                    pe.reg_mov(register, value)

            def routed(first, n):
                before, loads, place = [pe.snap(r, min_val=0, max_val=m) for r, m in zip(kept, (WW, SHARED + NE, WW))]
                for k in range(n):
                    s = first.ahead(k)
                    after = step(s, place, before, loads=loads, gather=True, fetch=True)
                    before, (loads, place) = place, after
                keep(before, loads, place)

            transpose_x(at_step(0), False)
            step(at_step(0), 0, 0, GATE_W, 1, first=True)
            for s in (1, 2):
                step(at_step(s), 0, 0, GATE_W, 1)
            step_loop(pe, 3, NT - 2, lambda s: step(s, 0, 0, GATE_W))
            step(at_step(NT - 1), 0, 0, GATE_W)
            step(at_step(NT), WW, 0, loads=2)
            for s in (NT + 1, NT + 2):
                step(at_step(s), WW, WW)

            pe.wait_ge(route_step, CHOSEN_STEP)
            pe.wait_ge(h_lo_done, NT + 3)
            pe.wait_ge(b_setup, 2)
            ranks = ht_bank[:, 0:NT * NE]
            flat = chosen[:].rearrange("p t e -> p (t e)")
            pe.matmul(ranks, consts[:, 0:P], flat, start=True, stop=False, skip_group_check=True)
            for t in range(NT - 1):
                n = NT - 1 - t
                pe.matmul(ht_bank[:, (t + 1) * NE:NT * NE].rearrange("p (t e) -> p t e", e=NE), ones_mat[:],
                          chosen[:, t:t + 1, :].to_broadcast([P, n, NE]), start=False, stop=t == NT - 2,
                          skip_group_check=True)
            for t in range(NT):
                last = pe.matmul(ht_bank[:, NT * NE:NT * NE + NE], ones_mat[:], chosen[:, t, :], start=t == 0,
                                 stop=t == NT - 1, skip_group_check=True)
            last.then_inc(counted, 1)

            step_loop(pe, NT + 3, 2 * NT - 2, lambda s: step(s, WW, WW))
            pe.wait_ge(route_step, ROUTE_STEPS)
            step(at_ring(2 * NT - 1), WW, WW, gather=True)
            s = at_ring(FIRST_ROUTED)
            step(s, 0, WW, loads=SHARED + 1, gather=True)
            keep(0, *places(at_ring(FIRST_ROUTED + 1)))
            with pe.Fori(FIRST_ROUTED // RING, (STEPS - 3) // RING) as turn:
                routed(RingStep(turn, 1), RING)
            s = at_ring(STEPS - 2)
            before, loads, place = [pe.snap(r, min_val=0, max_val=m) for r, m in zip(kept, (WW, SHARED + NE, WW))]
            last_loads, last_place = places(s.ahead(1))
            step(s, place, before, loads=loads, gather=True)
            step(s.ahead(1), last_place, place, loads=last_loads, last=True)
            down(s.ahead(1), last_place)

        @block.scalar
        def _(act):
            def split(j):
                act.wait_ge(raw_in, 16 * (j + 1))
                for k in range(3):
                    common.split_hi(act, j % 2 * WW, k)

            def x_hi(s):
                act.wait_ge(xt_done, s.index + 1)
                at_least(act, up_done, s.index - 1)
                act.activation(xt_hi[s.parity][:].rearrange("p c q -> p (c q)"), xt_bank[:], ACT.Copy).then_inc(xt_hi_done, 1)

            def gate(s, with_logits):
                act.wait_ge(gate_done, s.index + 1)
                if with_logits:
                    act.activation(logits[:, bass.ds(s.index, 1), :].rearrange("p o e -> p (o e)"),
                                   gate_bank[s.parity][:, FE:GATE_W], ACT.Copy).then_inc(logits_copied, 1)
                at_least(act, h_done, s.index - 1)
                act.activation(silu[s.parity][:], gate_bank[s.parity][:, 0:FE], ACT.Silu).then_inc(silu_done, 1)

            def hidden_hi(s):
                act.wait_ge(ht_done, s.index + 1)
                at_least(act, down_done, s.index)
                act.activation(h_hi[:].rearrange("p c q -> p (c q)"), ht_bank[:, 0:FC * P], ACT.Copy).then_inc(h_hi_done, 1)

            def after_next(s):
                return (table_value(act, t_new, s, 2, 1), table_value(act, t_load, s, 2, NE - 1) + SHARED + 1,
                        table_value(act, t_place, s, 2, WW), table_value(act, t_free, s, 2, STEPS))

            def split_new(new, count, place, free):
                with act.If(new > 0):
                    act.wait_ge(down_done, free)
                    act.wait_ge(raw_in, 16 * count)
                    for k in range(3):
                        common.split_hi(act, place, k)

            def step(s, with_logits=False, new=False, last=False):
                gate(s, with_logits)
                if not last:
                    x_hi(s.ahead(1))
                values = after_next(s) if new else None
                hidden_hi(s)
                if new:
                    split_new(*values)

            x_hi(at_step(0))
            step(at_step(0), with_logits=True)
            step_loop(act, 1, NT - 2, lambda s: step(s, with_logits=True))
            split(1)
            step(at_step(NT - 1), with_logits=True)
            step(at_step(NT))
            act.wait_ge(route_step, 2)
            act.activation(score[:], score[:], ACT.Exp).then_inc(exp_scores, 1)
            act.wait_ge(down_done, NT)
            split(2)
            step_loop(act, NT + 1, 2 * NT - 2, step)
            act.wait_ge(route_step, ROUTE_STEPS)
            step(at_step(2 * NT - 1), new=True)
            step(at_step(2 * NT), new=True)
            step_loop(act, FIRST_ROUTED + 1, STEPS - 3, lambda s: step(s, new=True))
            step(at_step(STEPS - 2))
            step(at_step(STEPS - 1), last=True)

        @block.vector
        def _(dve):
            dve.memset(h[:, FE:FC * P], 0.0).then_inc(h_padded, 1)

            def after_next(s):
                return (table_value(dve, t_new, s, 2, 1), table_value(dve, t_load, s, 2, NE - 1) + SHARED + 1,
                        table_value(dve, t_place, s, 2, WW))

            def split_new(new, count, place):
                with dve.If(new > 0):
                    common.split_lo_gate(dve, place, count)

            def x_lo(s):
                dve.wait_ge(xt_hi_done, s.index + 1)
                dve.tensor_tensor(xt_lo[s.parity][:].rearrange("p c q -> p (c q)"), xt_bank[:],
                                  xt_hi[s.parity][:].rearrange("p c q -> p (c q)").bitcast(F32),
                                  ALU.subtract).then_inc(xt_lo_done, 1)

            def hidden(s):
                dve.wait_ge(silu_done, s.index + 1)
                dve.wait_ge(up_done, s.index + 1)
                at_least(dve, ht_done, s.index)
                dve.tensor_tensor(h[:, 0:FE], up_bank[s.parity][:, 0:FE], silu[s.parity][:], ALU.mult).then_inc(h_done, 1)

            def hidden_lo(s):
                dve.wait_ge(h_hi_done, s.index + 1)
                dve.tensor_tensor(h_lo[:].rearrange("p c q -> p (c q)"), ht_bank[:, 0:FC * P],
                                  h_hi[:].rearrange("p c q -> p (c q)").bitcast(F32), ALU.subtract).then_inc(h_lo_done, 1)

            def shared_y(s, t, second):
                dve.wait_ge(down_done, s.index + 1)
                if second:
                    at_least(dve, y_done, s.index + 1 - NT)
                rows = base[:, bass.ds(t, 1), :].rearrange("p o d -> p (o d)")
                dve.scalar_tensor_tensor(rows, y_bank[s.parity][:], tanh_ffn[:, 0:1], rows, ALU.mult, ALU.add).then_inc(y_done, 1)

            def routed_y(s):
                dve.wait_ge(down_done, s.index + 1)
                at_least(dve, added, 16 * (s.index - FIRST_ROUTED))
                t = s.index - FIRST_ROUTED
                dve.tensor_scalar(y[s.parity][:], y_bank[s.parity][:], table[:, bass.ds(t, 1), 1].bitcast(F32), None,
                                  ALU.mult).then_inc(y_done, 1)

            def step(s, finish_before, new=False, last=False):
                hidden(s)
                if not last:
                    x_lo(s.ahead(1))
                if finish_before is not None:
                    finish_before(s.ahead(-1))
                values = after_next(s) if new else None
                hidden_lo(s)
                if new:
                    split_new(*values)

            done = 0

            def then(ins):
                nonlocal done
                ins.then_inc(route_step, 1)
                done += 1
                dve.wait_ge(route_step, done)

            def tri(at, n):
                return consts[:, at:at + n * n].rearrange("p (i j) -> p i j", i=n).unsqueeze(1).to_broadcast([P, NT, n, n])

            def route_scores():
                dve.wait_ge(const_in, 16)
                dve.wait_ge(logits_copied, NT)
                then(dve.tensor_reduce(stat[:], logits[:], AX.X, ALU.max))
                then(dve.tensor_tensor(score[:], logits[:], stat[:].unsqueeze(2).to_broadcast([P, NT, NE]), ALU.subtract))
                dve.wait_ge(exp_scores, 1)
                then(dve.tensor_reduce(stat[:], score[:], AX.X, ALU.add))
                then(dve.reciprocal(inv[:], stat[:]))
                then(dve.tensor_tensor(score[:], score[:], inv[:].unsqueeze(2).to_broadcast([P, NT, NE]), ALU.mult))
                pairs = score[:].rearrange("p t (g e) -> p t g e", e=2)
                then(dve.tensor_tensor(best[:], pairs[:, :, :, 0], pairs[:, :, :, 1], ALU.max))
                shape = [P, NT, PAIRS, PAIRS]
                mine, other = best[:].unsqueeze(3).to_broadcast(shape), best[:].unsqueeze(2).to_broadcast(shape)
                then(dve.tensor_tensor(group_gt[:], other, mine, ALU.is_gt))
                then(dve.tensor_tensor(group_eq[:], other, mine, ALU.is_equal))
                then(dve.tensor_tensor(group_eq[:], group_eq[:], tri(C_TRI4, PAIRS), ALU.mult))
                then(dve.tensor_tensor(group_gt[:], group_gt[:], group_eq[:], ALU.add))
                then(dve.tensor_reduce(best[:], group_gt[:], AX.X, ALU.add))
                then(dve.tensor_scalar(best[:], best[:], float(TOP), None, ALU.is_lt))
                then(dve.tensor_tensor(pairs, pairs, best[:].unsqueeze(3).to_broadcast([P, NT, PAIRS, 2]), ALU.mult))

            def route_experts():
                shape = [P, NT, NE, NE]
                mine, other = score[:].unsqueeze(3).to_broadcast(shape), score[:].unsqueeze(2).to_broadcast(shape)
                then(dve.tensor_tensor(gt[:], other, mine, ALU.is_gt))
                then(dve.tensor_tensor(eq[:], other, mine, ALU.is_equal))
                then(dve.tensor_tensor(eq[:], eq[:], tri(C_TRI, NE), ALU.mult))
                then(dve.tensor_tensor(gt[:], gt[:], eq[:], ALU.add))
                then(dve.tensor_reduce(rank[:], gt[:], AX.X, ALU.add))
                then(dve.tensor_scalar(chosen[:], rank[:], float(TOP), None, ALU.is_lt))
                assert done == CHOSEN_STEP
                then(dve.scalar_tensor_tensor(weight[:], score[:], tanh_ffn[:, 0:1], chosen[:], ALU.mult, ALU.mult))

            def route_counts():
                dve.wait_ge(counted, 1)
                then(dve.tensor_copy(counts[:], ht_bank[:, 0:NT * NE + NE]))

            def route_tiles():
                shape = [P, NE, NT - 1]
                then(dve.tensor_tensor(full[:], counts[:, NT * NE:NT * NE + NE].unsqueeze(2).to_broadcast(shape),
                                       consts[:, C_FULL:C_FULL + NT - 1].unsqueeze(1).to_broadcast(shape), ALU.is_gt))
                then(dve.tensor_reduce(tiles[:], full[:], AX.X, ALU.add))
                then(dve.tensor_scalar(tiles[:], tiles[:], 1.0, None, ALU.add))
                then(dve.tensor_tensor(before[:], tiles[:].unsqueeze(1).to_broadcast([P, NE, NE]),
                                       consts[:, C_TRI:C_TRI + NE * NE].rearrange("p (i j) -> p i j", i=NE), ALU.mult))
                then(dve.tensor_reduce(start[:], before[:], AX.X, ALU.add))
                then(dve.tensor_tensor(end[:], start[:], tiles[:], ALU.add))
                then(dve.tensor_scalar(start[:], start[:], float(P), None, ALU.mult))

            def route_rows():
                then(dve.tensor_tensor(place[:], counts[:, 0:NT * NE].rearrange("p (t e) -> p t e", e=NE),
                                       start[:].unsqueeze(1).to_broadcast([P, NT, NE]), ALU.add))
                then(dve.tensor_tensor(rank[:], place[:], chosen[:], ALU.mult))
                then(dve.tensor_reduce(slot[:, 1], rank[:], AX.X, ALU.max))
                then(dve.scalar_tensor_tensor(rank[:], place[:], -float(SLOT_ROWS), chosen[:], ALU.add, ALU.mult))
                then(dve.tensor_reduce(slot[:, 0], rank[:], AX.X, ALU.min))
                then(dve.tensor_scalar(slot[:, 0], slot[:, 0], float(SLOT_ROWS), None, ALU.add))
                for k in range(TOP):
                    then(dve.tensor_copy(row[:, :, 0, k], slot[:, k]))
                    then(dve.tensor_copy(row[:, :, 1 + k, 0], consts[:, C_TOK:C_TOK + NT]))
                    then(dve.tensor_tensor(rank[:], place[:], slot[:, k].unsqueeze(2).to_broadcast([P, NT, NE]), ALU.is_equal))
                    then(dve.tensor_tensor(rank[:], rank[:], weight[:], ALU.mult))
                    then(dve.tensor_reduce(row[:, :, 1 + k, 1].bitcast(F32), rank[:], AX.X, ALU.add))

            def route_tables():
                n = ROUTED_TILES + 2
                shape = [P, n, NE]
                tile_number = consts[:, C_TILE:C_TILE + n]
                then(dve.tensor_tensor(expert_gt[:, :, 0:NE - 1], tile_number.unsqueeze(2).to_broadcast([P, n, NE - 1]),
                                       end[:, 0:NE - 1].unsqueeze(1).to_broadcast([P, n, NE - 1]), ALU.is_ge))
                then(dve.tensor_reduce(expert[:], expert_gt[:, :, 0:NE - 1], AX.X, ALU.add))
                then(dve.tensor_copy(t_load[:], expert[:]))
                then(dve.tensor_scalar(parity_f[:], expert_gt[:, :, 0], float(WW), None, ALU.mult))
                for e in range(1, NE - 1):
                    then(dve.scalar_tensor_tensor(parity_f[:], expert_gt[:, :, e], float(WW if e % 2 == 0 else -WW),
                                                  parity_f[:], ALU.mult, ALU.add))
                then(dve.tensor_copy(t_place[:], parity_f[:]))
                then(dve.memset(t_new[:, 0:1], 0))
                then(dve.tensor_tensor(t_new[:, 1:n], expert[:, 1:n], expert[:, 0:n - 1], ALU.is_gt))
                then(dve.tensor_scalar(free_f[:], expert_gt[:, :, 0], float(NT), float(NT), ALU.mult, ALU.add))
                for e in range(1, NE - 1):
                    then(dve.scalar_tensor_tensor(free_f[:], expert_gt[:, :, e], tiles[:, e - 1:e], free_f[:],
                                                  ALU.mult, ALU.add))
                then(dve.tensor_copy(t_free[:], free_f[:]))
                assert done == ROUTE_STEPS, done

            def first_half(s):
                shared_y(s, s.index, False)

            def second_half(s):
                shared_y(s, s.index - NT, True)

            x_lo(at_step(0))
            dve.wait_ge(h_padded, 1)
            step(at_step(0), None)
            dve.wait_ge(base_in[0], 16)
            for s in range(1, BASE_PART + 1):
                step(at_step(s), first_half)
            dve.wait_ge(base_in[1], 16 * (NT // BASE_PART - 1))
            step_loop(dve, BASE_PART + 1, NT - 2, lambda s: step(s, first_half))
            common.split_lo_gate(dve, WW, 2)
            step(at_step(NT - 1), first_half)
            step(at_step(NT), first_half)
            route_scores()
            step(at_step(NT + 1), second_half)
            route_experts()
            step(at_step(NT + 2), second_half)
            route_counts()
            step(at_step(NT + 3), second_half)
            route_tiles()
            route_rows()
            step(at_step(NT + 4), second_half)
            route_tables()
            step(at_step(NT + 5), second_half)
            common.split_lo_gate(dve, 0, 3)
            step(at_step(NT + 6), second_half)
            step_loop(dve, NT + 7, 2 * NT - 2, lambda s: step(s, second_half))
            step(at_step(2 * NT - 1), second_half, new=True)
            step(at_step(2 * NT), second_half, new=True)
            dve.wait_ge(table_in, 16)
            step_loop(dve, FIRST_ROUTED + 1, STEPS - 3, lambda s: step(s, routed_y, new=True))
            step(at_step(STEPS - 2), routed_y)
            step(at_step(STEPS - 1), routed_y, last=True)
            routed_y(at_step(STEPS - 1))


def layout(i):
    import numpy as np

    def c(a):
        return np.ascontiguousarray(a)

    def wide(w):
        n = -(-w.shape[0] // P) * P
        full = np.zeros((n, w.shape[1]), np.float32)
        full[:w.shape[0]] = w
        return full.reshape(n // P, P, -1).transpose(1, 0, 2)

    def expert(gate, up, down_w, router=None):
        router = np.zeros((NE, D), np.float32) if router is None else router
        return np.concatenate([wide(np.concatenate([gate, router]).T).reshape(P, -1), wide(up.T).reshape(P, -1),
                               wide(down_w.T).reshape(P, -1)], axis=1)

    f = {}
    f["x"] = c(i["x"].reshape(T, D))
    f["ctxT"] = c(i["ctx_2048"].reshape(T, D).T)
    causal, pad = i["mask_SxS2_bc0"], i["mask_BxS2_bk0"]
    f["causal"], f["causalT"], f["pad"], f["padT"] = c(causal), c(causal.T), c(pad), c(pad.T)
    wq = i["L0_xattn_Wq"].reshape(G, R, HD, D).transpose(1, 0, 2, 3).reshape(D, D)
    f["wqkv"] = c(wide(np.concatenate([wq, i["L0_xattn_Wk"], i["L0_xattn_Wv"]]).T).reshape(P, -1))
    wo = i["L0_xattn_Wo"].T.reshape(2, G // 2, R, HD, D).transpose(0, 2, 1, 3, 4).reshape(D, D)
    f["wo"] = c(wide(wo).reshape(P, -1))
    f["bq"] = c(i["L0_xattn_bq"].reshape(G, R, HD).transpose(0, 2, 1).reshape(P, R))
    f["bk"], f["bv"] = c(i["L0_xattn_bk"].reshape(P, 1)), c(i["L0_xattn_bv"].reshape(P, 1))
    f["bo"], f["g_xattn"], f["g_ffn"] = c(i["L0_xattn_bo"]), c(i["g_xattn"]), c(i["g_ffn"])
    odd = np.arange(P) // HD % 2
    f["parity"] = c(np.stack([1 - odd, odd], 1).astype(np.float32))
    sg, su, sd = i["L0_ffn_sh_gate_w"], i["L0_ffn_sh_up_w"], i["L0_ffn_sh_down_w"]
    packed = [expert(sg[k * FE:(k + 1) * FE], su[k * FE:(k + 1) * FE], sd[:, k * FE:(k + 1) * FE],
                     i["L0_ffn_gate_weight"] if k == 0 else None) for k in range(SHARED)]
    packed += [expert(i["L0_ffn_gate_w"][e], i["L0_ffn_up_w"][e], i["L0_ffn_down_w"][e]) for e in range(NE)]
    f["experts"] = c(np.stack(packed))
    row = np.concatenate([np.tri(NE, k=-1).ravel(), np.tri(PAIRS, k=-1).ravel(), P * np.arange(1, NT),
                          np.arange(ROUTED_TILES + 2)])
    f["consts"] = c(np.concatenate([np.tri(P, k=-1).T, np.tile(row, (P, 1)),
                                    np.arange(P)[:, None] + P * np.arange(NT)[None]], axis=1).astype(np.float32))
    spare = T + np.arange(SLOT_ROWS) % P
    f["no_rows"] = c(np.stack([spare, np.zeros(SLOT_ROWS)], 1).astype(np.int32))
    return f


def kernel(**inputs):
    import numpy as np
    import concourse.bacc as bacc
    from concourse.bass_utils import run_bass_kernel_spmd

    nc = bacc.Bacc("TRN2", target_bir_lowering=False, num_devices=1)
    laid = layout({name: np.asarray(a) for name, a in inputs.items()})
    arrays, A = {}, {}
    for name, a in laid.items():
        arrays[f"in_{name}_dram"] = a
        A[name] = nc.dram_tensor(f"in_{name}_dram", a.shape, mybir.dt.from_np(a.dtype), kind="ExternalInput").ap()
    out = nc.dram_tensor("out_0_dram", (T + P, D), F32, kind="ExternalOutput").ap()
    build_kernel(nc, A, out)
    r = run_bass_kernel_spmd(nc, [arrays], core_ids=[0])
    return r.results[0]["out_0_dram"][:T].reshape(B, S, D)
```
